# Optimizing a Trainium2 kernel written in Bass

```python
import numpy as np
import jax
import jax.numpy as jnp

def _softmax(x, axis=-1):
    return jax.nn.softmax(x, axis=axis)

def _gelu(x):
    return jax.nn.gelu(x, approximate=True)

def _silu(x):
    return jax.nn.silu(x)

def _sigmoid(x):
    return jax.nn.sigmoid(x)

def _layernorm(x, axis=-1, eps=1e-05):
    m = jnp.mean(x, axis=axis, keepdims=True)
    v = jnp.var(x, axis=axis, keepdims=True)
    return (x - m) / jnp.sqrt(v + eps)

def _scatter_add(tgt, idx, src, axis=0):
    return tgt.at[idx].add(src)

def _segment_sum(src, seg, n):
    return jax.ops.segment_sum(src, seg, n)
kernel_name = 'mk_gnn_preln_d2_gnn_r32_9a9099'

def setup_inputs(seed: int=0):
    np.random.seed(seed)
    _w = jnp.asarray

    def _rec_inputs():
        import jax
        import jax.numpy as jnp
        _gk = jax.random.key(seed)
        x = -0.0003713 + 1 * jax.random.normal(jax.random.fold_in(_gk, 1), (50000, 128), jnp.float32)
        _s = jax.random.randint(jax.random.fold_in(_gk, 2), (25000,), 0, 50000, jnp.int32)
        _d = jax.random.randint(jax.random.fold_in(_gk, 3), (25000,), 0, 50000, jnp.int32)
        _loop = jnp.arange(50000, dtype=jnp.int32)
        src = jnp.concatenate([_s, _d, _loop])
        dst = jnp.concatenate([_d, _s, _loop])
        _o = jnp.argsort(dst, stable=True)
        src = src[_o]
        dst = dst[_o]
        edge_attr_64 = -5.16925e-05 + 1.00005 * jax.random.normal(jax.random.fold_in(_gk, 11), (1650000, 64), jnp.float32)
        return (x, src, dst, edge_attr_64)
    x, src, dst, edge_attr_64 = _rec_inputs()

    def _L0_gnn_setup():
        import jax, jax.numpy as jnp
        import numpy as np
        N_NODES = 3125
        N_EDGES = 50000
        IN_CH = 128
        HID_CH = 128
        NEG_SLOPE = 0.01
        key = jax.random.key(seed)
        ks = jax.random.split(key, 8)
        scale_in = 1.0 / np.sqrt(IN_CH)
        scale_h = 1.0 / np.sqrt(HID_CH)
        return {'x': jax.random.normal(ks[0], (N_NODES, IN_CH), dtype=jnp.float32), 'edge_index': jax.random.randint(ks[1], (2, N_EDGES), 0, N_NODES, dtype=jnp.int64), 'Wl1': jax.random.normal(ks[2], (HID_CH, IN_CH), dtype=jnp.float32) * scale_in, 'bl1': jnp.zeros((HID_CH,), dtype=jnp.float32), 'Wr1': jax.random.normal(ks[3], (HID_CH, IN_CH), dtype=jnp.float32) * scale_in, 'Wlh': jax.random.normal(ks[4], (2, HID_CH, HID_CH), dtype=jnp.float32) * scale_h, 'blh': jnp.zeros((2, HID_CH), dtype=jnp.float32), 'Wrh': jax.random.normal(ks[5], (2, HID_CH, HID_CH), dtype=jnp.float32) * scale_h}
    _L0_gnn_all = _L0_gnn_setup()
    _L0_gnn_in = {k: v for k, v in _L0_gnn_all.items() if k in ('Wl1', 'bl1', 'Wr1', 'Wlh', 'blh', 'Wrh')}
    del _L0_gnn_all

    def _L1_gnn_setup():
        import jax, jax.numpy as jnp
        import numpy as np
        NEG_SLOPE = 0.2
        key = jax.random.key(seed)
        ks = jax.random.split(key, 10)
        N, E, D, ED = (3125, 50000, 128, 64)
        x = jax.random.normal(ks[0], (N, D), dtype=jnp.float32)
        edge_index = jax.random.randint(ks[1], (2, E), 0, N, dtype=jnp.int32)
        edge_attr = jax.random.normal(ks[2], (E, ED), dtype=jnp.float32)
        s = 1.0 / np.sqrt(D)
        W = jax.random.normal(ks[3], (D, D), dtype=jnp.float32) * s
        att_src = jax.random.normal(ks[4], (D,), dtype=jnp.float32) * s
        att_dst = jax.random.normal(ks[5], (D,), dtype=jnp.float32) * s
        bias = jnp.zeros((D,), dtype=jnp.float32)
        We = jax.random.normal(ks[6], (ED, D), dtype=jnp.float32) / np.sqrt(ED)
        be = jnp.zeros((D,), dtype=jnp.float32)
        return {'x': x, 'edge_index': edge_index, 'edge_attr': edge_attr, 'W': W, 'att_src': att_src, 'att_dst': att_dst, 'bias': bias, 'We': We, 'be': be}
    _L1_gnn_all = _L1_gnn_setup()
    _L1_gnn_in = {k: v for k, v in _L1_gnn_all.items() if k in ('W', 'att_src', 'att_dst', 'bias', 'We', 'be')}
    del _L1_gnn_all
    return {'x': x, 'src': src, 'dst': dst, 'edge_attr_64': edge_attr_64, 'L0_gnn_Wl1': _L0_gnn_in['Wl1'], 'L0_gnn_bl1': _L0_gnn_in['bl1'], 'L0_gnn_Wr1': _L0_gnn_in['Wr1'], 'L0_gnn_Wlh': _L0_gnn_in['Wlh'], 'L0_gnn_blh': _L0_gnn_in['blh'], 'L0_gnn_Wrh': _L0_gnn_in['Wrh'], 'L1_gnn_W': _L1_gnn_in['W'], 'L1_gnn_att_src': _L1_gnn_in['att_src'], 'L1_gnn_att_dst': _L1_gnn_in['att_dst'], 'L1_gnn_bias': _L1_gnn_in['bias'], 'L1_gnn_We': _L1_gnn_in['We'], 'L1_gnn_be': _L1_gnn_in['be']}

def reference(x, src, dst, edge_attr_64, L0_gnn_Wl1, L0_gnn_bl1, L0_gnn_Wr1, L0_gnn_Wlh, L0_gnn_blh, L0_gnn_Wrh, L1_gnn_W, L1_gnn_att_src, L1_gnn_att_dst, L1_gnn_bias, L1_gnn_We, L1_gnn_be):
    import jax
    import jax.numpy as jnp

    def _L0_gnn_ref(x, edge_index, Wl1, bl1, Wr1, Wlh, blh, Wrh):
        import jax, jax.numpy as jnp
        import numpy as np
        N_NODES = 3125
        N_EDGES = 50000
        IN_CH = 128
        HID_CH = 128
        NEG_SLOPE = 0.01
        N = x.shape[0]
        src = edge_index[0]
        dst = edge_index[1]
        deg = jax.ops.segment_sum(jnp.ones_like(dst, dtype=x.dtype), dst, num_segments=N)
        inv_deg = (1.0 / jnp.maximum(deg, 1.0))[:, None]

        def sage_conv(h, Wl, b, Wr):
            agg = jax.ops.segment_sum(h[src], dst, num_segments=N) * inv_deg
            return agg @ Wl.T + b + h @ Wr.T
        h = jax.nn.leaky_relu(sage_conv(x, Wl1, bl1, Wr1), NEG_SLOPE)
        for i in range(Wlh.shape[0]):
            h = jax.nn.leaky_relu(sage_conv(h, Wlh[i], blh[i], Wrh[i]), NEG_SLOPE)
        return h

    def _L1_gnn_ref(x, edge_index, edge_attr, W, att_src, att_dst, bias, We, be):
        import jax, jax.numpy as jnp
        import numpy as np
        NEG_SLOPE = 0.2
        N = x.shape[0]
        edge_feat = edge_attr @ We + be
        h = x @ W
        loop = jnp.arange(N, dtype=edge_index.dtype)
        src = jnp.concatenate([edge_index[0], loop])
        dst = jnp.concatenate([edge_index[1], loop])
        a_s = h @ att_src
        a_d = h @ att_dst
        e = jax.nn.leaky_relu(a_s[src] + a_d[dst], NEG_SLOPE)
        seg_max = jax.ops.segment_max(e, dst, num_segments=N)
        e = jnp.exp(e - seg_max[dst])
        denom = jax.ops.segment_sum(e, dst, num_segments=N)
        alpha = e / (denom[dst] + 1e-16)
        out = jax.ops.segment_sum(h[src] * alpha[:, None], dst, num_segments=N)
        return out + bias
    edge_index = jnp.stack([src, dst])
    h = jnp.maximum(_layernorm(x, axis=-1), 0.0)
    x = x + _L0_gnn_ref(h, edge_index, L0_gnn_Wl1, L0_gnn_bl1, L0_gnn_Wr1, L0_gnn_Wlh, L0_gnn_blh, L0_gnn_Wrh)
    h = jnp.maximum(_layernorm(x, axis=-1), 0.0)
    x = x + _L1_gnn_ref(h, edge_index, edge_attr_64, L1_gnn_W, L1_gnn_att_src, L1_gnn_att_dst, L1_gnn_bias, L1_gnn_We, L1_gnn_be)
    return x

_drawn_inputs = setup_inputs


def setup_inputs(seed=0):
    import zlib

    import numpy as np

    out = dict(_drawn_inputs(seed))
    spreads = {'L0_gnn_bl1': (0.0, 0.1),
     'L0_gnn_blh': (0.0, 0.1),
     'L1_gnn_bias': (0.0, 0.1),
     'L1_gnn_be': (0.0, 0.1)}
    factors = {'L1_gnn_att_dst': 3.175}
    for name, (base, spread) in spreads.items():
        noise = np.random.default_rng([zlib.crc32(name.encode()), seed]).standard_normal(out[name].shape)
        drawn = base * np.exp(spread * noise) if base else spread * noise
        out[name] = jnp.asarray(drawn.astype(out[name].dtype))
    for name, factor in factors.items():
        out[name] = (out[name] * factor).astype(out[name].dtype)
    return out
```

```python
import concourse.bass as bass
from concourse import mybir
from contextlib import ExitStack

F32 = mybir.dt.float32
BF16 = mybir.dt.bfloat16
I32 = mybir.dt.int32
ALU = mybir.AluOpType
ACT = mybir.ActivationFunctionType
AX = mybir.AxisListType

P = 128
N = 50000
E = 100000
D = 128
TILE = 2 * P
NG = -(-N // TILE)
NPAD = NG * TILE
TAIL = N - (NG - 1) * TILE
BEYOND = 1 << 20
NW = 3
OFF = 56
CH = 5
RUN = CH * P
HALF = NG // 2
RING = 4
NT = -(-N // P)
NE = -(-E // P)
TAIL_T = N - (NT - 1) * P
NAT_P, NAT = 125, 800
CW = 132
FAR = float(1 << 18)
NOWHERE = -1000.0
BIG = 3.0e38
LAYERS = 3
EP = (E // (RUN + 1) + 2) * (RUN + 1)


class Step:

    def __init__(self, i, off):
        self.i, self.off = i, off
        self.t = RING * i + off if not (isinstance(i, int) and i == 0) else off
        self.b = off % 2
        self.r = off % RING
        self.static = isinstance(i, int)

    def at(self, d):
        return Step(self.i, self.off + d)

    def uses(self, ring):
        return (RING // ring) * self.i + self.off // ring if self.off else (RING // ring) * self.i


def steps(eng, body):
    for t in range(RING):
        body(Step(0, t))
    with eng.Fori(1, NG // RING - 1) as i:
        for off in range(RING):
            body(Step(i, off))
    for t in range(NG - RING, NG + 1):
        body(Step(0, t))


class Count:

    def __init__(self, sem):
        self.sem, self.base, self.per, self.i, self.n = sem, 0, 0, 0, 0

    def begin(self, per, i):
        self.per, self.i, self.n = per, i, 0

    def inc(self, instruction, by=1):
        instruction.then_inc(self.sem, by)
        self.n += by

    def now(self):
        return self.at(self.n)

    def at(self, n):
        return self.i * self.per + (self.base + n)

    def end(self, steps):
        assert self.n == self.per, (self.n, self.per)
        self.base += self.per * steps


def build(nc, x, src, dst, wl1, bl1, wr1, wlh, blh, wrh, w_gat, att_s, att_d, bias, out, dbg=None):
    ctx = ExitStack()
    with ctx:
        def sb(name, shape, dt=F32):
            return ctx.enter_context(nc.sbuf_tensor(name, shape, dt))

        def sem(name):
            return ctx.enter_context(nc.semaphore(name))

        tab = [nc.dram_tensor(f"tab{i}", [2 * NPAD, D], F32).ap() for i in range(2)]
        gen_h = nc.dram_tensor("gen_h", [NT * P, CW], F32).ap()
        gen_s = nc.dram_tensor("gen_s", [NT * P, CW], F32).ap()
        edges = [nc.dram_tensor(f"edges{i}", [EP], I32).ap() for i in range(2)]
        tab_c = nc.dram_tensor("tab_c", [NPAD, CW], F32).ap()
        x1_d = nc.dram_tensor("x1_d", [NPAD, D], F32).ap()

        ident = sb("ident", [P, P])
        ones = sb("ones", [P, P])
        iota_i = sb("iota_i", [P, RUN], I32)
        iota = sb("iota", [P, RUN])
        iota_c = sb("iota_c", [P, NW * P], BF16)
        part_i = sb("part_i", [P, 2], I32)
        part = sb("part", [P, 2])
        thr = sb("thr", [P, 2])
        eps = sb("eps", [P, 1])

        w_raw = sb("w_raw", [P, 7, P])
        wcat = sb("wcat", [P, LAYERS, 2 * D])
        w_t = sb("w_t", [P, P])
        wg = sb("wg", [P, D + 2])
        att = sb("att", [P, 2])
        b_bc = sb("b_bc", [P, LAYERS + 1, D])

        d_nat = sb("d_nat", [NAT_P, NAT], I32)
        d_nxt = sb("d_nxt", [NAT_P, NAT], I32)
        s_nat = sb("s_nat", [NAT_P, NAT], I32)
        cmp_n = sb("cmp_n", [NAT_P, NAT])
        cmp_m = sb("cmp_m", [NAT_P, NAT])
        first = sb("first", [NAT_P, P])
        pad = sb("pad", [2, (EP - E) // 2], I32)
        row_d = sb("row_d", [HALF, 2, NAT], I32)
        row_i = sb("row_i", [HALF, 2], I32)
        row_c = sb("row_c", [HALF, 2])
        in_row = sb("in_row", [HALF, 2])
        e_first = sb("e_first", [HALF, 2])
        start_i = sb("start_i", [HALF, 2], I32)
        run_s = sb("run_s", [HALF, 2, RUN + 1], I32)
        run_d = sb("run_d", [HALF, 2, RUN + 1], I32)
        w_a = sb("w_a", [HALF, RUN])
        w_b = sb("w_b", [HALF, RUN])
        w_valid = sb("w_valid", [HALF, RUN])
        w_int = sb("w_int", [HALF, 2, RUN], I32)
        qty = sb("qty", [HALF, 4, RUN])
        stat = sb("stat", [P, 8])
        stat_sb = sb("stat_sb", [1, 8])
        flag_f = sb("flag_f", [1, 8])
        flag = sb("flag", [1, 1], I32)
        place = sb("place", [P, NG, CH])
        vals = sb("vals", [P, NG, CH, 4], BF16)
        cmask = sb("cmask", [P, 2, CH, NW * P], BF16)
        placed = sb("placed", [P, NG, NW, 4])
        idx = sb("idx", [P, NG, NW], I32)
        dcol = sb("dcol", [P, NG, NW])
        empty = sb("empty", [P, NG * NW])

        ibuf = sb("ibuf", [P, RING, NW], I32)
        dbuf = sb("dbuf", [P, RING, NW])
        rows = sb("rows", [P, RING, NW, CW])
        own = sb("own", [P, 2, 2, 2 * D])
        xin = sb("xin", [P, 2, 2, D])
        mask = sb("mask", [P, 2, 4 * P])
        h = sb("h", [P, 2, 2 * D])
        h_t = sb("h_t", [P, 2, 2 * P])
        gu = sb("gu", [P, 2, 2, 2 * D])
        tsum = sb("tsum", [P, 2, D])
        zed = sb("zed", [P, 2, D])
        x1 = sb("x1", [P, 2, 2, D])
        x1b = sb("x1b", [P, 2, 2, D])
        cnt = sb("cnt", [P, 2])
        inv = sb("inv", [P, 2])
        bst = sb("bst", [P, 2, 6])
        mv = sb("mv", [P, 2, 2, 2])
        std = sb("std", [P, 2, 2])
        rstd = sb("rstd", [P, 2, 2])
        nmr = sb("nmr", [P, 2, 2])
        own_c = sb("own_c", [P, 2, 2, CW])
        zb = sb("zb", [P, 2, 2, TILE])
        lr = sb("lr", [P, 2, TILE])
        pen = sb("pen", [P, 2, TILE])
        lm = sb("lm", [P, 2, 2, TILE])
        mx = sb("mx", [P, 2])
        zs = sb("zs", [P, 2])
        ls = sb("ls", [P, 2])
        mm = sb("mm", [P, 2])
        nm = sb("nm", [P, 2, 2])
        dself = sb("dself", [P, 2, 2])
        pself = sb("pself", [P, 2, 2])
        den = sb("den", [P, 2, 2])
        ptwo = sb("ptwo", [P, 2])
        dsum = sb("dsum", [P, 2])
        rden = sb("rden", [P, 2])
        prob = sb("prob", [P, 2, 2, TILE])
        prob_t = sb("prob_t", [P, 2, 2, TILE])
        acc = sb("acc", [P, 2, D])
        res = sb("res", [P, 2, 2, D])

        low = sb("low", [P, P])
        se = sb("se", [P, 2], I32)
        g_row = sb("g_row", [P, CW])
        g_dst = sb("g_dst", [P, CW])
        g_sum = sb("g_sum", [P, CW])
        g_new = sb("g_new", [P, CW])
        g_node = sb("g_node", [P, CW])
        g_init = sb("g_init", [P, 2, CW])
        df = sb("df", [P, 1])
        wide = sb("wide", [P, P])
        same = sb("same", [P, P])
        tmp = sb("tmp", [P, P])
        g1 = sb("g1", [P, 8])
        w_idx = sb("w_idx", [P, 1], I32)
        g_x = sb("g_x", [P, D])
        g_x1 = sb("g_x1", [P, D])
        g_x1b = sb("g_x1b", [P, D])
        g_h = sb("g_h", [P, D])
        g_t = sb("g_t", [P, 2 * P])
        g_st = sb("g_st", [P, 6])
        g_mv = sb("g_mv", [P, 2])
        g_out = sb("g_out", [P, D])

        bank = [ctx.enter_context(nc.psum_tensor(f"bank{i}", [P, 512], F32)) for i in range(8)]
        ps_agg = [bank[0], bank[1]]
        ps_t = [bank[2], bank[3]]
        ps_g = [bank[4], bank[5]]
        ps_u = [bank[6], bank[7]]
        ps_place = [bank[6], bank[7]]
        ps_as = [bank[0], bank[1]]
        ps_ds = [bank[2], bank[3]]
        ps_pt = [bank[4], bank[5]]
        ps_o = [bank[6], bank[7]]

        def pair(bk, w=D, stride=D):
            return bk[:, 0:2 * stride].rearrange("p (j w) -> p j w", j=2)[:, :, 0:w]

        names = ("const_g const_v prep_v prep_p prep_ld nat_ld nxt_ld snat_ld wt_ld att_ld bb_ld row_ld run_ld "
                 "wt_ps wt_cp first_ps idx_g cm_done cm_used pl_ps pl_cp prep_end "
                 "x_ld0 x_ld1 own_ld0 own_ld1 ibuf_cp dbuf_cp mask_done agg_done cnt_v tsum_v inv_v z_v h_v "
                 "ln_v ln_a rs_v nmr_v h_a tr_done ht_cp dense_done g_cp u_cp st0 st1 x1_v x1b_v stx0 stx1 "
                 "turn ownc0 ownc1 x1l0 x1l1 bc_done z_a lr_v pen_v lm_v self_v nm_v ex_a ps_a pt_done pt_cp pv_done "
                 "den_v acc_v res_v out0 out1 zrow flag_v flag_ps wg_cp flag_rdy ge_ld0 ge_rows0 ge_st0 ge_ld1 ge_rows1 ge_st1 ge_ld2 ge_rows2 ge_st2 ge_ld3 ge_rows3 ge_st3 gn_ld0 gn_st0 gn_ld1 gn_st1 gn_ld2 gn_st2 gn_ld3 gn_st3 gn_ld4 gn_st4 ge_v ge_a ge_m gn_v gn_a gn_m low_g edge_st prep_seq turn_v turn_s cs_v cd_v").split()
        S = {n: sem(n) for n in names}
        row_ld = [[sem(f"row_ld{r}_{w}") for w in range(NW)] for r in range(RING)]

        block = ctx.enter_context(nc.Block())

        def tab_rows(t, p):
            return tab[p][bass.ds(t * (2 * TILE), 2 * TILE), :].rearrange("(j p r) d -> p j (r d)", j=2, r=2)

        def node_rows(a, t):
            return a[bass.ds(t * TILE, TILE), :].rearrange("(j p) d -> p j d", j=2)

        def sync_program(eng):
            wt = S["wt_ld"]
            eng.dma_start(w_raw[:, 0, :], wl1).then_inc(wt, 16)
            eng.dma_start(w_raw[:, 1, :], wr1).then_inc(wt, 16)
            for l in range(2):
                eng.dma_start(w_raw[:, 2 + 2 * l, :], wlh[l, :, :]).then_inc(wt, 16)
                eng.dma_start(w_raw[:, 3 + 2 * l, :], wrh[l, :, :]).then_inc(wt, 16)
            eng.dma_start(w_raw[:, 6, :], w_gat).then_inc(wt, 16)
            eng.dma_start(att[:, 0:1], att_s.rearrange("(p a) -> p a", a=1)).then_inc(wt, 16)
            eng.dma_start(att[:, 1:2], att_d.rearrange("(p a) -> p a", a=1)).then_inc(wt, 16)
            for n, b in enumerate([bl1, blh[0, :], blh[1, :], bias]):
                eng.dma_start(b_bc[:, n, :], b.partition_broadcast(P)).then_inc(wt, 16)
            eng.dma_start(d_nat[:, :], dst.rearrange("(p a) -> p a", a=NAT)).then_inc(S["nat_ld"], 16)
            eng.dma_start(s_nat[:, :], src.rearrange("(p a) -> p a", a=NAT)).then_inc(S["nat_ld"], 16)
            for a, to in zip((src, dst), edges):
                eng.dma_start(to[0:E].rearrange("(p a) -> p a", a=NAT), a.rearrange("(p a) -> p a", a=NAT)
                              ).then_inc(S["edge_st"], 16)
            eng.wait_ge(S["const_v"], 1)
            for to in edges:
                eng.dma_start(to[E:EP].rearrange("(p a) -> p a", p=2), pad[:, :]).then_inc(S["edge_st"], 16)
            eng.dma_start(d_nxt[0:NAT_P - 1, :],
                          dst[1:1 + (NAT_P - 1) * NAT].rearrange("(p a) -> p a", a=NAT)).then_inc(S["nxt_ld"], 16)
            eng.dma_start(d_nxt[NAT_P - 1:NAT_P, 0:NAT - 1],
                          dst[1 + (NAT_P - 1) * NAT:E].rearrange("(p a) -> p a", p=1)).then_inc(S["nxt_ld"], 16)

            def load_x(s, n):
                ld = S[f"x_ld{s.b}"]
                if s.static and s.t == NG - 1:
                    eng.dma_start(xin[0:TAIL, s.b, 0, :], x[N - TAIL:N, :]).then_inc(ld, 16)
                else:
                    eng.dma_start(xin[:, s.b, :, :], node_rows(x, s.t)).then_inc(ld, 16)

            def phase0(s):
                if s.static and s.t == 0:
                    load_x(s, 0)
                if not (s.static and s.t >= NG - 1):
                    n = s.at(1)
                    if not (s.static and s.t < 1):
                        eng.wait_ge(S["h_a"], n.t - 1)
                    load_x(n, 0)
                if not (s.static and s.t < 1):
                    o = s.at(-1) if s.off else Step(s.i - 1, RING - 1)
                    eng.wait_ge(S["g_cp"], s.t)
                    eng.wait_ge(S["u_cp"], s.t)
                    eng.dma_start(tab_rows(o.t, 0), gu[:, o.b, :, :]).then_inc(S[f"st{o.b}"], 16)
            eng.wait_ge(S["flag_rdy"], 1)
            ok = eng.value_load(flag[0:1, 0:1], min_val=0, max_val=1)
            with eng.If(ok):
                fast_sync(eng, load_x, phase0)
            with eng.Else():
                general_sync(eng)

        def fast_sync(eng, load_x, phase0):
            eng.wait_ge(S["const_g"], 5)
            steps(eng, phase0)

            for ph in range(1, LAYERS + 1):
                kb = ph * NG
                ka = (ph - 1) * NG
                for b in range(2):
                    eng.wait_ge(S[f"st{b}"], 16 * (kb // 2))

                def load(s):
                    eng.dma_start(own[:, s.b, :, :], tab_rows(s.t, (ph - 1) % 2)).then_inc(S[f"own_ld{s.b}"], 16)
                    if ph == LAYERS:
                        load_x(s, 0)

                def phase(s):
                    if s.static and s.t == 0:
                        load(s)
                    if not (s.static and s.t >= NG - 1):
                        if not (s.static and s.t < 1):
                            eng.wait_ge(S["h_v"], ka + s.t)
                            if ph == LAYERS:
                                eng.wait_ge(S["x1_v"], s.t)
                        load(s.at(1))
                    if not (s.static and s.t < 1):
                        o = s.at(-1) if s.off else Step(s.i - 1, RING - 1)
                        eng.wait_ge(S["g_cp"], kb + s.t)
                        eng.wait_ge(S["u_cp"], kb + s.t)
                        if ph < LAYERS:
                            eng.dma_start(tab_rows(o.t, ph % 2), gu[:, o.b, :, :]).then_inc(S[f"st{o.b}"], 16)
                        else:
                            eng.dma_start(node_rows(tab_c, o.t), gu[:, o.b, :, 0:CW]).then_inc(S[f"st{o.b}"], 16)
                            eng.dma_start(node_rows(x1_d, o.t), x1b[:, o.b, :, :]).then_inc(S[f"stx{o.b}"], 16)
                steps(eng, phase)

            for b in range(2):
                eng.wait_ge(S[f"st{b}"], 16 * ((LAYERS + 1) * NG // 2))
                eng.wait_ge(S[f"stx{b}"], 16 * (NG // 2))

            def load_c(s):
                eng.dma_start(own_c[:, s.b, :, :], node_rows(tab_c, s.t)).then_inc(S[f"ownc{s.b}"], 16)
                eng.dma_start(x1b[:, s.b, :, :], node_rows(x1_d, s.t)).then_inc(S[f"x1l{s.b}"], 16)

            def phase_c(s):
                if not (s.static and s.t >= NG):
                    if not (s.static and s.t < 2):
                        eng.wait_ge(S["res_v"], s.t - 1)
                    load_c(s)
                if not (s.static and s.t < 2):
                    o = s.at(-2) if s.off >= 2 else Step(s.i - 1, RING + s.off - 2)
                    store_c(o, s.t - 1)

            def store_c(o, n):
                eng.wait_ge(S["res_v"], n)
                eng.dma_start(node_rows(out, o.t), res[:, o.b, :, :]).then_inc(S[f"out{o.b}"], 16)
            steps(eng, phase_c)
            eng.wait_ge(S["res_v"], NG)
            eng.dma_start(out[N - TAIL:N, :], res[0:TAIL, (NG - 1) % 2, 0, :]).then_inc(S[f"out{(NG - 1) % 2}"], 16)
            for b in range(2):
                eng.wait_ge(S[f"out{b}"], 16 * NG // 2)

        def gpsimd_program(eng):
            g = S["const_g"]
            eng.memset(ident[:, :], 0.0).then_inc(g, 1)
            eng.iota(iota_i[:, :], pattern=[[1, RUN]], base=0, channel_multiplier=0).then_inc(g, 1)
            eng.iota(part_i[:, :], pattern=[[P, 2]], base=0, channel_multiplier=1).then_inc(g, 1)
            eng.memset(xin[:, :, :, :], 0.0).then_inc(g, 1)
            eng.wait_ge(g, 1)
            eng.affine_select(out=ident[:, :], in_=ident[:, :], compare_op=ALU.not_equal, fill=1.0,
                              base=0, pattern=[[-1, P]], channel_multiplier=1).then_inc(g, 1)
            eng.memset(rows[:, :, :, :], 0.0).then_inc(S["zrow"], 1)
            eng.memset(low[:, :], 0.0).then_inc(S["low_g"], 1)
            eng.memset(g_row[:, :], 0.0).then_inc(S["low_g"], 1)
            eng.memset(g_dst[:, :], 0.0).then_inc(S["low_g"], 1)
            eng.memset(g_sum[:, :], 0.0).then_inc(S["low_g"], 1)
            eng.memset(g_new[:, :], 0.0).then_inc(S["low_g"], 1)
            eng.memset(g_node[:, :], 0.0).then_inc(S["low_g"], 1)
            eng.memset(g_x[:, :], 0.0).then_inc(S["low_g"], 1)
            eng.memset(g_init[:, :, :], 0.0).then_inc(S["low_g"], 1)
            eng.wait_ge(S["low_g"], 8)
            eng.affine_select(out=low[:, :], in_=low[:, :], compare_op=ALU.is_ge, fill=1.0,
                              base=0, pattern=[[1, P]], channel_multiplier=-1).then_inc(S["low_g"], 1)
            eng.memset(g_init[:, 1, D + 1:D + 2], -BIG).then_inc(S["low_g"], 1)
            eng.memset(g_node[:, D:D + 1], 1.0).then_inc(S["low_g"], 1)

            eng.wait_ge(S["prep_v"], 1)
            for q in range(2):
                eng.indirect_dma_start(out=row_d[:, q, :], out_offset=None,
                                       in_=dst.rearrange("(p a) -> p a", a=NAT),
                                       in_offset=bass.IndirectOffsetOnAxis(ap=row_i[:, q:q + 1], axis=0)
                                       ).then_inc(S["row_ld"], 16)
            eng.wait_ge(S["prep_v"], 2)
            eng.wait_ge(S["edge_st"], 64)
            view = [a.rearrange("(p a) -> p a", a=RUN + 1) for a in edges]
            for q in range(2):
                for a, to in zip(view, (run_s, run_d)):
                    eng.indirect_dma_start(out=to[:, q, :], out_offset=None, in_=a,
                                           in_offset=bass.IndirectOffsetOnAxis(ap=start_i[:, q:q + 1], axis=1)
                                           ).then_inc(S["run_ld"], 16)

            eng.wait_ge(S["flag_rdy"], 1)
            ok = eng.value_load(flag[0:1, 0:1], min_val=0, max_val=1)
            with eng.If(ok):
                fast_gpsimd(eng)
            with eng.Else():
                general_gpsimd(eng)

        def fast_gpsimd(eng):
            eng.wait_ge(S["zrow"], 2)
            for ph in range(1, LAYERS + 2):
                ka = (ph - 1) * NG
                for b in range(2):
                    eng.wait_ge(S[f"st{b}"], 16 * (ph * NG // 2))
                table = tab[(ph - 1) % 2] if ph <= LAYERS else tab_c
                width = D if ph <= LAYERS else CW
                last = 2 * NPAD - 1 if ph <= LAYERS else NPAD - 1

                def gathers(s):
                    if s.static and s.t >= NG:
                        return
                    eng.wait_ge(S["ibuf_cp"], ka + s.t + 1)
                    if not (ph == 1 and s.static and s.t < RING):
                        done = "agg_done" if ph <= LAYERS else "pv_done"
                        if ph <= LAYERS:
                            eng.wait_ge(S["agg_done"], ka + s.t - RING + 1)
                        elif not (s.static and s.t < RING):
                            eng.wait_ge(S["pv_done"], s.t - RING + 1)
                    if not s.static:
                        eng.sem_inc(S["turn"], 1)
                    for w in range(NW):
                        eng.indirect_dma_start(out=rows[:, s.r, w, 0:width], out_offset=None, in_=table,
                                               in_offset=bass.IndirectOffsetOnAxis(ap=ibuf[:, s.r, w:w + 1], axis=0),
                                               bounds_check=last, oob_is_err=False
                                               ).then_inc(row_ld[s.r][w], 16)
                if ph == LAYERS + 1:
                    eng.wait_ge(S["agg_done"], LAYERS * NG)
                steps(eng, gathers)

        def scalar_program(eng):
            for n in range(7):
                eng.wait_ge(S["wt_ps"], n + 1)
                to = wcat[:, n // 2, (n % 2) * D:(n % 2 + 1) * D] if n < 6 else w_t[:, :]
                eng.activation(to, bank[n][:, 0:P], ACT.Copy).then_inc(S["wt_cp"], 1)
            eng.activation(wg[:, 0:D], w_raw[:, 6, :], ACT.Copy).then_inc(S["wt_cp"], 1)
            eng.wait_ge(S["wt_ps"], 8)
            eng.activation(wg[:, D:D + 2], bank[0][:, 0:2], ACT.Copy).then_inc(S["wg_cp"], 1)

            for q in range(2):
                for k in range(4):
                    n = 4 * q + k
                    eng.wait_ge(S["prep_p"], n + 1)
                    view = bank[n % 4 + 2][:, 0:CH * HALF].rearrange("p (c t) -> p t c", c=CH)
                    to = place[:, q * HALF:(q + 1) * HALF, :] if k == 0 else \
                        vals[:, q * HALF:(q + 1) * HALF, :, k - 1]
                    eng.activation(to, view, ACT.Copy).then_inc(S["pl_cp"], 1)

            eng.wait_ge(S["flag_rdy"], 1)
            ok = eng.value_load(flag[0:1, 0:1], min_val=0, max_val=1)
            with eng.If(ok):
                fast_scalar(eng)
            with eng.Else():
                general_scalar(eng)

        def fast_scalar(eng):
            def placed_out(s):
                if s.static and s.t >= NG:
                    return
                eng.wait_ge(S["pl_ps"], s.t + 1)
                eng.activation(placed[:, bass.ds(s.t, 1), :, :].rearrange("p t w v -> p (t w v)"),
                               ps_place[s.b][:, 0:NW * 4], ACT.Copy).then_inc(S["prep_end"], 1)
            steps(eng, placed_out)

            def norm(s, k, src_tile):
                eng.wait_ge(S["ln_v"], k + 1)
                eng.activation(std[:, s.b, :], mv[:, s.b, :, 1], ACT.Sqrt, bias=eps[:, 0:1]).then_inc(S["ln_a"], 1)
                eng.wait_ge(S["nmr_v"], k + 1)
                for j in range(2):
                    a = eng.activation(h[:, s.b, j * D:(j + 1) * D], src_tile[:, s.b, j, :], ACT.Relu,
                                       bias=nmr[:, s.b, j:j + 1], scale=rstd[:, s.b, j:j + 1])
                a.then_inc(S["h_a"], 1)

            def ht_copy(b, k):
                eng.wait_ge(S["tr_done"], k + 1)
                eng.activation(h_t[:, b, :], ps_t[b][:, 0:2 * P], ACT.Copy).then_inc(S["ht_cp"], 1)

            def g_copy(b, k, used, width=D):
                eng.wait_ge(S["dense_done"], k + 1)
                if used is not None:
                    eng.wait_ge(S[f"st{b}"], used)
                eng.activation(gu[:, b, :, 0:width], pair(ps_g[b], width, TILE), ACT.Copy).then_inc(S["g_cp"], 1)

            def prev(s):
                return s.at(-1) if s.off else Step(s.i - 1, RING - 1)

            def phase0(s):
                if not (s.static and s.t >= NG):
                    if not (s.static and s.t < 2):
                        eng.wait_ge(S["tr_done"], s.t - 1)
                    norm(s, s.t, xin)
                    ht_copy(s.b, s.t)
                if not (s.static and s.t < 1):
                    o = prev(s)
                    g_copy(o.b, s.t - 1, None if s.static and s.t < 3 else 16 * o.uses(2))
            steps(eng, phase0)

            def idx_copy(s, ph):
                ka = (ph - 1) * NG
                if not (ph == 1 and s.static and s.t < RING):
                    for w in range(NW):
                        eng.wait_ge(row_ld[s.r][w], 16 * (ka // RING + s.uses(RING)))
                frm = idx[:, bass.ds(s.t, 1), :].rearrange("p t w -> p (t w)")
                eng.activation(ibuf[:, s.r, :], frm, ACT.Copy,
                               scale=1.0 if ph <= LAYERS else 0.5).then_inc(S["ibuf_cp"], 1)

            for ph in range(1, LAYERS + 1):
                kb = ph * NG
                if ph == 1:
                    eng.wait_ge(S["idx_g"], 1)

                def phase(s):
                    if s.static and s.t == 0:
                        idx_copy(s, ph)
                    if not (s.static and s.t >= NG - 1):
                        idx_copy(s.at(1), ph)
                    if not (s.static and s.t < 1):
                        o = prev(s)
                        ht_copy(o.b, kb + s.t - 1)
                        g_copy(o.b, kb + s.t - 1, 16 * (kb // 2 + o.uses(2)), D if ph < LAYERS else D + 2)
                    if ph == LAYERS and not (s.static and s.t >= NG):
                        norm(s, NG + s.t, x1)
                steps(eng, phase)

            def phase_c(s):
                if s.static and s.t == 0:
                    idx_copy(s, LAYERS + 1)
                if not (s.static and s.t >= NG - 1):
                    idx_copy(s.at(1), LAYERS + 1)
                if not (s.static and s.t >= NG):
                    eng.wait_ge(S[f"ownc{s.b}"], 16 * (s.uses(2) + 1))
                    eng.wait_ge(S["bc_done"], s.t + 1)
                    if not (s.static and s.t < 2):
                        eng.wait_ge(S["lr_v"], s.t - 1)
                    for j in range(2):
                        a = eng.activation(zb[:, s.b, j, :], ps_as[s.b][:, j * P:j * P + TILE], ACT.Identity,
                                           bias=own_c[:, s.b, j, D + 1:D + 2])
                    a.then_inc(S["z_a"], 1)
                if not (s.static and s.t < 1):
                    o = prev(s)
                    eng.wait_ge(S["pt_done"], s.t)
                    if not (s.static and s.t < 3):
                        eng.wait_ge(S["pv_done"], s.t - 2)
                    eng.activation(prob_t[:, o.b, :, :].rearrange("p j e -> p (j e)"), ps_pt[o.b][:, :],
                                   ACT.Copy).then_inc(S["pt_cp"], 1)
                if not (s.static and s.t >= NG):
                    eng.wait_ge(S["nm_v"], s.t + 1)
                    if not (s.static and s.t < 2):
                        eng.wait_ge(S["pt_done"], s.t - 1)
                        eng.wait_ge(S["res_v"], s.t - 1)
                    for j in range(2):
                        eng.activation(prob[:, s.b, j, :], lm[:, s.b, j, :], ACT.Exp, bias=nm[:, s.b, j:j + 1],
                                       accum_out=den[:, s.b, j:j + 1])
                    eng.activation(pself[:, s.b, :], dself[:, s.b, :], ACT.Exp).then_inc(S["ex_a"], 1)
            steps(eng, phase_c)

        def tensor_program(eng):
            eng.wait_ge(S["const_g"], 5)
            eng.wait_ge(S["wt_ld"], 16 * 13)
            for n in range(7):
                eng.transpose(bank[n][:, 0:P], w_raw[:, n, :], ident[:, :]).then_inc(S["wt_ps"], 1)
            eng.wait_ge(S["wt_cp"], 7)
            eng.matmul(bank[0][:, 0:2], w_t[:, :], att[:, :], start=True, stop=True).then_inc(S["wt_ps"], 1)
            eng.wait_ge(S["prep_ld"], 1)
            eng.transpose(bank[7][:, 0:NAT_P], first[:, :], ident[0:NAT_P, 0:NAT_P]).then_inc(S["first_ps"], 1)
            eng.wait_ge(S["wt_cp"], 8)
            for q in range(2):
                for k in range(4):
                    n = 4 * q + k
                    eng.wait_ge(S["prep_v"], 3 + q)
                    if n >= 4:
                        eng.wait_ge(S["pl_cp"], n - 3)
                    for c in range(CH):
                        m = eng.transpose(bank[n % 4 + 2][:, c * HALF:(c + 1) * HALF],
                                          qty[:, k, c * P:(c + 1) * P], ident[0:HALF, 0:HALF])
                    m.then_inc(S["prep_p"], 1)
            eng.wait_ge(S["flag_v"], 1)
            eng.matmul(bank[1][0:1, 0:8], ones[:, 0:1], stat[:, :], start=True, stop=True).then_inc(S["flag_ps"], 1)

            eng.wait_ge(S["flag_rdy"], 1)
            ok = eng.value_load(flag[0:1, 0:1], min_val=0, max_val=1)
            with eng.If(ok):
                fast_tensor(eng)
            with eng.Else():
                general_tensor(eng)

        def fast_tensor(eng):
            eng.wait_ge(S["pl_cp"], 8)

            def placing(s):
                if s.static and s.t >= NG:
                    return
                eng.wait_ge(S["cm_done"], s.t + 1)
                if not (s.static and s.t < 2):
                    eng.wait_ge(S["prep_end"], s.t - 1)
                for w in range(NW):
                    for c in range(CH):
                        m = eng.matmul(ps_place[s.b][:, 4 * w:4 * w + 3], cmask[:, s.b, c, w * P:(w + 1) * P],
                                       vals[:, bass.ds(s.t, 1), c, 0:3].rearrange("p t v -> p (t v)"),
                                       start=(c == 0), stop=(c == CH - 1))
                m.then_inc(S["pl_ps"], 1)
            steps(eng, placing)

            def turn_h(b, k, ready, n, free):
                eng.wait_ge(ready, n)
                if free is not None:
                    eng.wait_ge(S["ht_cp"], free)
                for j in range(2):
                    m = eng.transpose(ps_t[b][:, j * P:(j + 1) * P], h[:, b, j * D:(j + 1) * D], ident[:, :])
                m.then_inc(S["tr_done"], 1)

            def dense(b, k, w_g, w_u, width, free):
                eng.wait_ge(S["ht_cp"], k + 1)
                if free is not None:
                    eng.wait_ge(S["g_cp"], free)
                    eng.wait_ge(S["u_cp"], free)
                for j in range(2):
                    m = eng.matmul(ps_g[b][:, j * TILE:j * TILE + width], h_t[:, b, j * P:(j + 1) * P], w_g,
                                   start=True, stop=True)
                    if w_u is not None:
                        m = eng.matmul(ps_u[b][:, j * TILE:j * TILE + D], h_t[:, b, j * P:(j + 1) * P], w_u,
                                       start=True, stop=True)
                m.then_inc(S["dense_done"], 1)

            def prev(s):
                return s.at(-1) if s.off else Step(s.i - 1, RING - 1)

            def phase0(s):
                if not (s.static and s.t >= NG):
                    turn_h(s.b, s.t, S["h_a"], s.t + 1, None if s.static and s.t < 2 else s.t - 1)
                if not (s.static and s.t < 1):
                    o = prev(s)
                    dense(o.b, s.t - 1, wcat[:, 0, 0:D], wcat[:, 0, D:2 * D], D, None if s.static and s.t < 3 else s.t - 2)
            steps(eng, phase0)

            for ph in range(1, LAYERS + 1):
                kb = ph * NG
                ka = (ph - 1) * NG

                def phase(s):
                    if not (s.static and s.t < 1):
                        o = prev(s)
                        if ph < LAYERS:
                            turn_h(o.b, 0, S["h_v"], ka + s.t, kb + s.t - 2)
                        else:
                            turn_h(o.b, 0, S["h_a"], NG + s.t, kb + s.t - 2)
                    if not (s.static and s.t >= NG):
                        eng.wait_ge(S["mask_done"], ka + s.t + 1)
                        if not (ph == 1 and s.static and s.t < 2):
                            eng.wait_ge(S["tsum_v"], ka + s.t - 1)
                        for w, j, m0 in ((0, 0, 0), (1, 0, 1), (1, 1, 2), (2, 1, 3)):
                            if m0 != 2:
                                eng.wait_ge(row_ld[s.r][w], 16 * (ka // RING + s.uses(RING) + 1))
                            m = eng.matmul(ps_agg[s.b][:, j * TILE:j * TILE + D + 1],
                                           mask[:, s.b, m0 * P:(m0 + 1) * P], rows[:, s.r, w, 0:D + 1],
                                           start=(m0 % 2 == 0), stop=(m0 % 2 == 1))
                        m.then_inc(S["agg_done"], 1)
                    if not (s.static and s.t < 1):
                        if ph < LAYERS:
                            dense(o.b, kb + s.t - 1, wcat[:, ph, 0:D], wcat[:, ph, D:2 * D], D, kb + s.t - 2)
                        else:
                            dense(o.b, kb + s.t - 1, wg[:, :], None, D + 2, kb + s.t - 2)
                steps(eng, phase)

            eng.wait_ge(S["g_cp"], (LAYERS + 1) * NG)
            eng.wait_ge(S["tsum_v"], LAYERS * NG)

            def phase_c(s):
                if not (s.static and s.t >= NG):
                    for w in range(NW):
                        eng.wait_ge(row_ld[s.r][w], 16 * (LAYERS * NG // RING + s.uses(RING) + 1))
                    eng.wait_ge(S["dbuf_cp"], s.t + 1)
                    if not (s.static and s.t < 2):
                        eng.wait_ge(S["z_a"], s.t - 1)
                        eng.wait_ge(S["pen_v"], s.t - 1)
                    for w in range(NW):
                        eng.transpose(ps_as[s.b][:, w * P:(w + 1) * P],
                                      rows[:, s.r, w, D:D + 1].to_broadcast([P, P]), ident[:, :])
                    for w in range(NW):
                        m = eng.transpose(ps_ds[s.b][:, w * P:(w + 1) * P],
                                          dbuf[:, s.r, w:w + 1].to_broadcast([P, P]), ident[:, :])
                    m.then_inc(S["bc_done"], 1)
                if not (s.static and s.t < 1):
                    o = prev(s)
                    eng.wait_ge(S["ex_a"], s.t)
                    if not (s.static and s.t < 3):
                        eng.wait_ge(S["pt_cp"], s.t - 2)
                    for j in range(2):
                        for w in range(2):
                            m = eng.transpose(ps_pt[o.b][:, (2 * j + w) * P:(2 * j + w + 1) * P],
                                              prob[:, o.b, j, w * P:(w + 1) * P], ident[:, :])
                    m.then_inc(S["pt_done"], 1)
                    eng.wait_ge(S["pt_cp"], s.t)
                    if not (s.static and s.t < 3):
                        eng.wait_ge(S["acc_v"], s.t - 2)
                    for j in range(2):
                        for w in range(2):
                            m = eng.matmul(ps_o[o.b][:, j * D:(j + 1) * D], prob_t[:, o.b, j, w * P:(w + 1) * P],
                                           rows[:, o.r, j + w, 0:D], start=(w == 0), stop=(w == 1))
                    m.then_inc(S["pv_done"], 1)
            steps(eng, phase_c)

        def vector_program(eng):
            eng.memset(pad[:, :], BEYOND)
            eng.memset(d_nxt[:, :], N).then_inc(S["const_v"], 1)
            eng.memset(ones[:, :], 1.0).then_inc(S["const_v"], 1)
            eng.memset(eps[:, :], 1e-5).then_inc(S["const_v"], 1)
            eng.memset(stat[:, :], 0.0).then_inc(S["const_v"], 1)
            eng.wait_ge(S["const_g"], 5)
            seq = [0]

            def op(ins):
                seq[0] += 1
                ins.then_inc(S["prep_seq"], 1)
                eng.wait_ge(S["prep_seq"], seq[0])
            op(eng.tensor_copy(iota[:, :], iota_i[:, :]))
            op(eng.tensor_copy(part[:, :], part_i[:, :]))
            op(eng.tensor_scalar(iota_c[:, :], iota[:, 0:NW * P], -128.0, None, ALU.add))
            op(eng.tensor_scalar(thr[:, 0:1], part[:, 0:1], float(TILE), None, ALU.mult))
            op(eng.tensor_scalar(thr[:, 1:2], part[:, 0:1], float(HALF), float(TILE), ALU.add, ALU.mult))
            eng.wait_ge(S["zrow"], 1)
            eng.memset(rows[:, :, :, D:D + 1], 1.0).then_inc(S["zrow"], 1)

            eng.wait_ge(S["nat_ld"], 32)
            op(eng.tensor_scalar(first[:, :], ones[0:NAT_P, :], d_nat[:, 0:1], None, ALU.mult))
            eng.sem_inc(S["prep_ld"], 1)
            eng.wait_ge(S["nxt_ld"], 32)
            op(eng.tensor_tensor(cmp_n[:, :], d_nat[:, :], d_nxt[:, :], ALU.is_gt))
            op(eng.tensor_reduce(stat[0:NAT_P, 0:1], cmp_n[:, :], AX.X, ALU.add))
            op(eng.tensor_tensor(cmp_n[:, :], d_nat[:, :], d_nxt[:, :], ALU.not_equal))
            op(eng.tensor_reduce(stat[0:NAT_P, 1:2], cmp_n[:, :], AX.X, ALU.add))
            op(eng.tensor_tensor(cmp_m[:, :], s_nat[:, :], d_nat[:, :], ALU.not_equal))
            op(eng.tensor_tensor(cmp_m[:, :], cmp_m[:, :], cmp_n[:, :], ALU.mult))
            op(eng.tensor_reduce(stat[0:NAT_P, 2:3], cmp_m[:, :], AX.X, ALU.add))

            eng.wait_ge(S["first_ps"], 1)
            for q in range(2):
                op(eng.tensor_scalar(cmp_n[0:HALF, 0:NAT_P], bank[7][0:HALF, 0:NAT_P], thr[0:HALF, q:q + 1], None,
                                     ALU.is_lt))
                op(eng.tensor_reduce(row_c[:, q:q + 1], cmp_n[0:HALF, 0:NAT_P], AX.X, ALU.add))
            op(eng.tensor_scalar(row_c[:, :], row_c[:, :], -1.0, 0.0, ALU.add, ALU.max))
            op(eng.tensor_copy(row_i[:, :], row_c[:, :]))
            eng.sem_inc(S["prep_v"], 1)
            eng.wait_ge(S["row_ld"], 32)
            for q in range(2):
                op(eng.tensor_scalar(cmp_n[0:HALF, :], row_d[:, q, :], thr[0:HALF, q:q + 1], None, ALU.is_lt))
                op(eng.tensor_reduce(in_row[:, q:q + 1], cmp_n[0:HALF, :], AX.X, ALU.add))
            op(eng.scalar_tensor_tensor(e_first[:, :], row_c[:, :], float(NAT), in_row[:, :], ALU.mult, ALU.add))
            op(eng.tensor_copy(start_i[:, :], e_first[:, :]))
            eng.sem_inc(S["prep_v"], 1)
            eng.wait_ge(S["run_ld"], 64)
            for q in range(2):
                if q == 1:
                    eng.wait_ge(S["prep_p"], 4)
                drel = qty[:, 3, :]
                op(eng.tensor_tensor(w_valid[:, :], run_d[:, q, 0:RUN], run_d[:, q, 1:RUN + 1], ALU.is_equal))
                op(eng.tensor_scalar(drel, run_d[:, q, 0:RUN], thr[0:HALF, q:q + 1], None, ALU.subtract))
                op(eng.scalar_tensor_tensor(w_valid[:, :], drel, 0.0, w_valid[:, :], ALU.is_ge, ALU.mult))
                op(eng.scalar_tensor_tensor(w_valid[:, :], drel, float(TILE), w_valid[:, :], ALU.is_lt, ALU.mult))
                op(eng.tensor_reduce(stat[0:HALF, 3 + q:4 + q], w_valid[:, :], AX.X, ALU.add))
                op(eng.scalar_tensor_tensor(w_a[:, :], iota[0:HALF, :], float(OFF), drel, ALU.add, ALU.subtract))
                op(eng.tensor_scalar(w_b[:, :], drel, float(P), float(P), ALU.is_ge, ALU.mult))
                op(eng.tensor_tensor(w_b[:, :], w_a[:, :], w_b[:, :], ALU.subtract))
                op(eng.scalar_tensor_tensor(qty[:, 1, :], w_b[:, :], 0.0, w_valid[:, :], ALU.is_lt, ALU.mult))
                op(eng.scalar_tensor_tensor(qty[:, 2, :], w_b[:, :], float(TILE), w_valid[:, :], ALU.is_ge, ALU.mult))
                op(eng.tensor_tensor(qty[:, 1, :], qty[:, 1, :], qty[:, 2, :], ALU.add))
                op(eng.tensor_reduce(stat[0:HALF, 5 + q:6 + q], qty[:, 1, :], AX.X, ALU.add))
                op(eng.scalar_tensor_tensor(w_a[:, :], w_a[:, :], -128.0 - NOWHERE, w_valid[:, :], ALU.add, ALU.mult))
                op(eng.tensor_scalar(qty[:, 0, :], w_a[:, :], NOWHERE, None, ALU.add))
                op(eng.tensor_scalar(drel, drel, 1.0, None, ALU.add))
                op(eng.tensor_scalar(w_int[:, 0, :], run_s[:, q, 0:RUN], 8, None, ALU.logical_shift_right))
                op(eng.tensor_scalar(w_int[:, 1, :], run_s[:, q, 0:RUN], 255, None, ALU.bitwise_and))
                op(eng.tensor_copy(qty[:, 1:3, :], w_int[:, :, :]))
                eng.sem_inc(S["prep_v"], 1)
            eng.sem_inc(S["flag_v"], 1)

            eng.wait_ge(S["flag_ps"], 1)
            op(eng.tensor_copy(stat_sb[:, :], bank[1][0:1, 0:8]))
            op(eng.tensor_tensor(flag_f[:, 0:1], stat_sb[:, 0:1], stat_sb[:, 2:3], ALU.add))
            op(eng.tensor_tensor(flag_f[:, 1:2], stat_sb[:, 5:6], stat_sb[:, 6:7], ALU.add))
            op(eng.tensor_tensor(flag_f[:, 0:1], flag_f[:, 0:1], flag_f[:, 1:2], ALU.add))
            op(eng.tensor_scalar(flag_f[:, 0:1], flag_f[:, 0:1], 0.0, None, ALU.is_equal))
            op(eng.tensor_scalar(flag_f[:, 1:2], stat_sb[:, 1:2], float(N), None, ALU.is_equal))
            op(eng.tensor_tensor(flag_f[:, 2:3], stat_sb[:, 3:4], stat_sb[:, 4:5], ALU.add))
            op(eng.tensor_scalar(flag_f[:, 2:3], flag_f[:, 2:3], float(E - N), None, ALU.is_equal))
            op(eng.tensor_tensor(flag_f[:, 0:1], flag_f[:, 0:1], flag_f[:, 1:2], ALU.mult))
            op(eng.tensor_tensor(flag[:, :], flag_f[:, 0:1], flag_f[:, 2:3], ALU.mult))
            eng.sem_inc(S["flag_rdy"], 1)
            ok = eng.value_load(flag[0:1, 0:1], min_val=0, max_val=1)
            eng.wait_ge(S["wt_ld"], 16 * 13)
            with eng.If(ok):
                fast_vector(eng, op)
            with eng.Else():
                general_vector(eng)

        def fast_vector(eng, op):
            eng.wait_ge(S["pl_cp"], 8)

            def place_mask(s):
                if s.static and s.t >= NG:
                    return
                if not (s.static and s.t < 2):
                    eng.wait_ge(S["pl_ps"], s.t - 1)
                for c in range(CH):
                    m = eng.tensor_scalar(cmask[:, s.b, c, :], iota_c[:, :],
                                          place[:, bass.ds(s.t, 1), c:c + 1].rearrange("p t c -> p (t c)"),
                                          None, ALU.is_equal)
                m.then_inc(S["cm_done"], 1)
            steps(eng, place_mask)
            eng.wait_ge(S["prep_end"], NG)
            pv = placed[:, :, :, :].rearrange("p t w v -> p (t w) v")
            idx_f = idx[:, :, :].rearrange("p t w -> p (t w)")
            dc_f = dcol[:, :, :].rearrange("p t w -> p (t w)")
            op(eng.tensor_scalar(dc_f, pv[:, :, 2], -1.0, None, ALU.add))
            op(eng.tensor_scalar(empty[:, :], dc_f, 0.0, FAR, ALU.is_lt, ALU.mult))
            op(eng.scalar_tensor_tensor(empty[:, :], pv[:, :, 1], 2.0, empty[:, :], ALU.mult, ALU.add))
            op(eng.scalar_tensor_tensor(idx_f, pv[:, :, 0], 512.0, empty[:, :], ALU.mult, ALU.add))
            eng.sem_inc(S["idx_g"], 1)

            def stats(s, k, tile, used):
                for j in range(2):
                    m = eng.bn_stats(bst[:, j, :], tile[:, s.b, j, :])
                m.then_inc(S["self_v"], 1)
                eng.wait_ge(S["self_v"], k + 1)
                if used is not None:
                    eng.wait_ge(S["h_a"], used)
                if not s.static:
                    eng.sem_inc(S["turn_v"], 1)
                for j in range(2):
                    m = eng.bn_aggr(mv[:, s.b, j, :], bst[:, j, :])
                m.then_inc(S["ln_v"], 1)
                eng.wait_ge(S["ln_a"], k + 1)
                eng.reciprocal(rstd[:, s.b, :], std[:, s.b, :]).then_inc(S["rs_v"], 1)
                eng.wait_ge(S["rs_v"], k + 1)
                eng.scalar_tensor_tensor(nmr[:, s.b, :], mv[:, s.b, :, 0], -1.0, rstd[:, s.b, :], ALU.mult,
                                         ALU.mult).then_inc(S["nmr_v"], 1)

            def u_copy(b, k, layer, used):
                eng.wait_ge(S["dense_done"], k + 1)
                if used is not None:
                    eng.wait_ge(S[f"st{b}"], used)
                eng.tensor_tensor(gu[:, b, :, D:2 * D], pair(ps_u[b], D, TILE),
                                  b_bc[:, layer, :].unsqueeze(1).to_broadcast([P, 2, D]), ALU.add
                                  ).then_inc(S["u_cp"], 1)

            def prev(s):
                return s.at(-1) if s.off else Step(s.i - 1, RING - 1)

            eng.wait_ge(S["wt_ld"], 16 * 13)

            def phase0(s):
                if not (s.static and s.t >= NG):
                    eng.wait_ge(S[f"x_ld{s.b}"], 16 * (s.uses(2) + 1))
                    stats(s, s.t, xin, None if s.static and s.t < 2 else s.t - 1)
                if not (s.static and s.t < 1):
                    o = prev(s)
                    u_copy(o.b, s.t - 1, 0, None if s.static and s.t < 3 else 16 * o.uses(2))
            steps(eng, phase0)

            def masks(s, ka):
                if not (ka == 0 and s.static and s.t < 2):
                    eng.wait_ge(S["agg_done"], ka + s.t - 1)
                for w, a, b, to in ((0, 0, P, 0), (1, 0, TILE, P), (2, P, TILE, 3 * P)):
                    m = eng.tensor_scalar(mask[:, s.b, to:to + b - a], iota[:, a:b],
                                          dcol[:, bass.ds(s.t, 1), w:w + 1].rearrange("p t w -> p (t w)"),
                                          None, ALU.is_equal)
                m.then_inc(S["mask_done"], 1)

            for ph in range(1, LAYERS + 1):
                ka = (ph - 1) * NG
                kb = ph * NG

                def phase(s):
                    if s.static and s.t == 0:
                        masks(s, ka)
                    if not (s.static and s.t >= NG - 1):
                        masks(s.at(1), ka)
                    if not (s.static and s.t >= NG):
                        k = ka + s.t
                        eng.wait_ge(S["agg_done"], k + 1)
                        acc_ps = pair(ps_agg[s.b], D + 1, TILE)
                        eng.tensor_scalar(cnt[:, :], acc_ps[:, :, D], 1.0, None, ALU.add).then_inc(S["cnt_v"], 1)
                        eng.wait_ge(S[f"own_ld{s.b}"], 16 * (ka // 2 + s.uses(2) + 1))
                        eng.tensor_tensor(tsum[:, :, :], acc_ps[:, :, 0:D], own[:, s.b, :, 0:D], ALU.add
                                          ).then_inc(S["tsum_v"], 1)
                        eng.wait_ge(S["cnt_v"], k + 1)
                        eng.reciprocal(inv[:, :], cnt[:, :]).then_inc(S["inv_v"], 1)
                        eng.wait_ge(S["tsum_v"], k + 1)
                        eng.wait_ge(S["inv_v"], k + 1)
                        for j in range(2):
                            m = eng.scalar_tensor_tensor(zed[:, j, :], tsum[:, j, :], inv[:, j:j + 1],
                                                         own[:, s.b, j, D:2 * D], ALU.mult, ALU.add)
                        m.then_inc(S["z_v"], 1)
                        eng.wait_ge(S["z_v"], k + 1)
                        if ph < LAYERS:
                            to = h[:, s.b, :].rearrange("p (j d) -> p j d", j=2)
                            eng.wait_ge(S["tr_done"], kb + s.t - 1)
                        else:
                            to = tsum[:, :, :]
                        eng.scalar_tensor_tensor(to, zed[:, :, :], 0.01, zed[:, :, :], ALU.mult, ALU.max
                                                 ).then_inc(S["h_v"], 1)
                        if ph == LAYERS:
                            eng.wait_ge(S["h_v"], k + 1)
                            eng.wait_ge(S[f"x_ld{s.b}"], 16 * (NG // 2 + s.uses(2) + 1))
                            if not (s.static and s.t < 2):
                                eng.wait_ge(S["h_a"], NG + s.t - 1)
                            eng.tensor_tensor(x1[:, s.b, :, :], tsum[:, :, :], xin[:, s.b, :, :], ALU.add
                                              ).then_inc(S["x1_v"], 1)
                            eng.wait_ge(S["x1_v"], s.t + 1)
                            if not (s.static and s.t < 2):
                                eng.wait_ge(S[f"stx{s.b}"], 16 * s.uses(2))
                            eng.tensor_tensor(x1b[:, s.b, :, :], x1[:, s.b, :, :],
                                              b_bc[:, LAYERS, :].unsqueeze(1).to_broadcast([P, 2, D]), ALU.add
                                              ).then_inc(S["x1b_v"], 1)
                            stats(s, NG + s.t, x1, None)
                    if not (s.static and s.t < 1):
                        o = prev(s)
                        if ph < LAYERS:
                            u_copy(o.b, kb + s.t - 1, ph, 16 * (kb // 2 + o.uses(2)))
                        else:
                            eng.wait_ge(S["x1b_v"], s.t)
                            eng.sem_inc(S["u_cp"], 1)
                steps(eng, phase)

            def dst_copy(s):
                if not (s.static and s.t < RING):
                    eng.wait_ge(S["bc_done"], s.t - RING + 1)
                eng.tensor_copy(dbuf[:, s.r, :], dcol[:, bass.ds(s.t, 1), :].rearrange("p t w -> p (t w)")
                                ).then_inc(S["dbuf_cp"], 1)

            def phase_c(s):
                if s.static and s.t == 0:
                    dst_copy(s)
                if not (s.static and s.t >= NG - 1):
                    dst_copy(s.at(1))
                if not (s.static and s.t >= NG):
                    k = s.t
                    oc = own_c[:, s.b, :, :]
                    eng.wait_ge(S[f"ownc{s.b}"], 16 * (s.uses(2) + 1))
                    eng.tensor_tensor(zs[:, :], oc[:, :, D], oc[:, :, D + 1], ALU.add).then_inc(S["cs_v"], 1)
                    eng.wait_ge(S["bc_done"], k + 1)
                    for j in range(2):
                        m = eng.tensor_scalar(pen[:, j, :], ps_ds[s.b][:, j * P:j * P + TILE], part[:, j:j + 1],
                                              -BIG, ALU.not_equal, ALU.mult)
                    m.then_inc(S["pen_v"], 1)
                    eng.wait_ge(S["cs_v"], 5 * k + 1)
                    eng.scalar_tensor_tensor(ls[:, :], zs[:, :], 0.2, zs[:, :], ALU.mult, ALU.max
                                             ).then_inc(S["cs_v"], 1)
                    eng.wait_ge(S["z_a"], k + 1)
                    eng.scalar_tensor_tensor(lr[:, :, :], zb[:, s.b, :, :], 0.2, zb[:, s.b, :, :], ALU.mult, ALU.max
                                             ).then_inc(S["lr_v"], 1)
                    eng.wait_ge(S["pen_v"], k + 1)
                    eng.wait_ge(S["lr_v"], k + 1)
                    if not (s.static and s.t < 2):
                        eng.wait_ge(S["ex_a"], k - 1)
                    eng.tensor_tensor(lm[:, s.b, :, :], lr[:, :, :], pen[:, :, :], ALU.add).then_inc(S["lm_v"], 1)
                    eng.wait_ge(S["lm_v"], k + 1)
                    eng.tensor_reduce(mx[:, :], lm[:, s.b, :, :], AX.X, ALU.max).then_inc(S["cs_v"], 1)
                    eng.wait_ge(S["cs_v"], 5 * k + 3)
                    eng.tensor_tensor(mm[:, :], mx[:, :], ls[:, :], ALU.max).then_inc(S["cs_v"], 1)
                    eng.wait_ge(S["cs_v"], 5 * k + 4)
                    eng.tensor_scalar(nm[:, s.b, :], mm[:, :], -1.0, None, ALU.mult).then_inc(S["cs_v"], 1)
                    eng.tensor_tensor(dself[:, s.b, :], ls[:, :], mm[:, :], ALU.subtract).then_inc(S["nm_v"], 1)
                if not (s.static and s.t < 1):
                    o = prev(s)
                    k = s.t - 1
                    eng.wait_ge(S["ex_a"], k + 1)
                    eng.tensor_scalar(ptwo[:, :], pself[:, o.b, :], 2.0, None, ALU.mult).then_inc(S["cd_v"], 1)
                    eng.wait_ge(S["cd_v"], 3 * k + 1)
                    eng.scalar_tensor_tensor(dsum[:, :], den[:, o.b, :], 1e-16, ptwo[:, :], ALU.add, ALU.add
                                             ).then_inc(S["cd_v"], 1)
                    eng.wait_ge(S["cd_v"], 3 * k + 2)
                    eng.reciprocal(rden[:, :], dsum[:, :]).then_inc(S["cd_v"], 1)
                    eng.wait_ge(S["pv_done"], k + 1)
                    for j in range(2):
                        m = eng.scalar_tensor_tensor(acc[:, j, :], own_c[:, o.b, j, 0:D], ptwo[:, j:j + 1],
                                                     ps_o[o.b][:, j * D:(j + 1) * D], ALU.mult, ALU.add)
                    m.then_inc(S["acc_v"], 1)
                    eng.wait_ge(S["cd_v"], 3 * k + 3)
                    eng.wait_ge(S["acc_v"], k + 1)
                    eng.wait_ge(S[f"x1l{o.b}"], 16 * (o.uses(2) + 1))
                    if not (s.static and s.t < 3):
                        eng.wait_ge(S[f"out{o.b}"], 16 * o.uses(2))
                    for j in range(2):
                        m = eng.scalar_tensor_tensor(res[:, o.b, j, :], acc[:, j, :], rden[:, j:j + 1],
                                                     x1b[:, o.b, j, :], ALU.mult, ALU.add)
                    m.then_inc(S["res_v"], 1)
            steps(eng, phase_c)

        def tile_of(a, t, w=None):
            rows_ = a[bass.ds(t * P, P), :] if not isinstance(t, int) else a[t * P:(t + 1) * P, :]
            return rows_ if w is None else rows_[:, 0:w]

        def node_loop(eng, body):
            with eng.Fori(0, NT - 1) as t:
                body(t, P)
            body(NT - 1, TAIL_T)

        def general_sync(eng):
            vec = {0: 4, 1: 5, 2: 5, 3: 12, 4: 12}
            v_base = 0
            eng.wait_ge(S["low_g"], 11)
            for ph in range(LAYERS + 2):
                ld, st = Count(S[f"gn_ld{ph}"]), Count(S[f"gn_st{ph}"])
                if ph:
                    eng.wait_ge(S[f"ge_st{ph - 1}"], 16 * NE)
                loads = {0: 1, 3: 3, 4: 3}.get(ph, 2)
                stores = {0: 2, 3: 3, 4: 1}.get(ph, 2)

                def body(t, n):
                    ld.begin(16 * loads, t)
                    st.begin(16 * stores, t)
                    if ph in (0, 3):
                        ld.inc(eng.dma_start(g_x[0:n, :], x[bass.ds(t * P, n), :]), 16)
                    if ph:
                        ld.inc(eng.dma_start(g_sum[:, :], tile_of(gen_s, t)), 16)
                        ld.inc(eng.dma_start(g_row[:, :], tile_of(gen_h if ph <= 3 else tab_c, t)), 16)
                    if ph == 4:
                        ld.inc(eng.dma_start(g_x1b[:, :], tile_of(x1_d, t)), 16)
                    if ph == 0:
                        eng.wait_ge(S["gn_a"], 2 * t + 2)
                    else:
                        eng.wait_ge(S["gn_v"], t * vec[ph] + (v_base + vec[ph]))
                    if ph <= 2:
                        st.inc(eng.dma_start(tile_of(gen_h, t), g_node[:, :]), 16)
                    if ph == 3:
                        st.inc(eng.dma_start(tile_of(tab_c, t), g_node[:, :]), 16)
                        st.inc(eng.dma_start(tile_of(x1_d, t), g_x1b[:, :]), 16)
                    if ph <= 3:
                        st.inc(eng.dma_start(tile_of(gen_s, t), g_init[:, int(ph == 3), :]), 16)
                    else:
                        st.inc(eng.dma_start(out[bass.ds(t * P, n), :], g_out[0:n, :]), 16)
                    eng.wait_ge(S[f"gn_st{ph}"], st.now())
                    eng.sem_inc(S["turn_s"], 1)
                node_loop(eng, body)
                ld.end(NT)
                st.end(NT)
                v_base += vec[ph] * NT

        def general_gpsimd(eng):
            stored = {0: 32, 1: 32, 2: 32, 3: 48}
            v_base = 0
            for ph in range(LAYERS + 1):
                ld, rw, st = Count(S[f"ge_ld{ph}"]), Count(S[f"ge_rows{ph}"]), Count(S[f"ge_st{ph}"])
                eng.wait_ge(S[f"gn_st{ph}"], stored[ph] * NT)
                table = gen_h if ph < LAYERS else tab_c[0:NT * P, :]
                k = 3 if ph == LAYERS else 2
                v_n = 7 + 1 if ph < LAYERS else 18
                with eng.Fori(0, NE) as i:
                    ld.begin(32, i)
                    rw.begin(16 * k, i)
                    st.begin(16, i)
                    for c in range(2):
                        ld.inc(eng.dma_start(se[:, c:c + 1],
                                             edges[c][bass.ds(i * P, P)].rearrange("(p a) -> p a", a=1)), 16)
                    eng.wait_ge(S[f"ge_ld{ph}"], ld.now())
                    eng.sem_inc(S["turn"], 1)
                    for to, frm, c in ((g_row, table, 0), (g_sum, gen_s, 1), (g_dst, table, 1))[:k]:
                        rw.inc(eng.indirect_dma_start(out=to[:, :], out_offset=None, in_=frm,
                                                      in_offset=bass.IndirectOffsetOnAxis(ap=se[:, c:c + 1], axis=0),
                                                      bounds_check=N - 1, oob_is_err=False), 16)
                    eng.wait_ge(S["ge_v"], i * v_n + (v_base + v_n))
                    eng.sem_inc(S["turn"], 1)
                    st.inc(eng.indirect_dma_start(out=gen_s, out_offset=bass.IndirectOffsetOnAxis(ap=w_idx[:, :], axis=0),
                                                  in_=g_new[:, :], in_offset=None,
                                                  bounds_check=N - 1, oob_is_err=False), 16)
                    eng.wait_ge(S[f"ge_st{ph}"], st.now())
                    eng.sem_inc(S["turn"], 1)
                for c in (ld, rw, st):
                    c.end(NE)
                v_base += v_n * NE

        def general_scalar(eng):
            nd, v, m = Count(S["gn_a"]), Count(S["gn_v"]), Count(S["gn_m"])

            def after(sem, n):
                eng.wait_ge(sem, n)

            v_base, m_base, a_base = 0, 0, 0
            ge_v_base = ge_m_base = 0
            for ph in range(LAYERS + 2):
                vn = {0: 4, 1: 5, 2: 5, 3: 12, 4: 12}[ph]
                mn = {0: 0, 1: 2, 2: 2, 3: 4, 4: 0}[ph]
                an = {0: 2, 1: 1, 2: 1, 3: 4, 4: 1}[ph]
                if ph == LAYERS + 1:
                    with eng.Fori(0, NE) as i:
                        eng.wait_ge(S["ge_v"], i * 18 + (8 * NE * LAYERS + 16))
                        eng.activation(g1[:, 6:7], g1[:, 5:6], ACT.Exp).then_inc(S["ge_a"], 1)
                        eng.activation(same[:, :], tmp[:, :], ACT.Exp, bias=g1[:, 4:5], accum_out=g1[:, 7:8]
                                       ).then_inc(S["ge_a"], 1)
                        eng.wait_ge(S["ge_m"], i * 4 + (2 * NE * LAYERS + 3))
                        eng.activation(wide[:, :], bank[2][:, 0:P], ACT.Copy).then_inc(S["ge_a"], 1)

                def body(t, n):
                    def a(ins):
                        ins.then_inc(S["gn_a"], 1)

                    def v_at(n):
                        eng.wait_ge(S["gn_v"], t * vn + (v_base + n))

                    def m_at(n):
                        eng.wait_ge(S["gn_m"], t * mn + (m_base + n))
                    if ph == 0:
                        v_at(2)
                        a(eng.activation(g1[:, 0:1], g_mv[:, 1:2], ACT.Sqrt, bias=eps[:, 0:1]))
                        v_at(4)
                        a(eng.activation(g_node[:, 0:D], g_x[:, :], ACT.Relu, bias=g1[:, 2:3], scale=g1[:, 1:2]))
                    elif ph <= LAYERS:
                        m_at(1)
                        a(eng.activation(g_t[:, :], bank[0][:, 0:2 * P], ACT.Copy))
                        if ph == LAYERS:
                            v_at(9)
                            a(eng.activation(g1[:, 0:1], g_mv[:, 1:2], ACT.Sqrt, bias=eps[:, 0:1]))
                            v_at(11)
                            a(eng.activation(g_h[:, :], g_x1[:, :], ACT.Relu, bias=g1[:, 2:3], scale=g1[:, 1:2]))
                            m_at(3)
                            a(eng.activation(g_t[:, 0:P], bank[0][:, 0:P], ACT.Copy))
                    else:
                        v_at(5)
                        a(eng.activation(g1[:, 4:6], g1[:, 2:4], ACT.Exp))
                node_loop(eng, body)
                v_base += vn * NT
                m_base += mn * NT

        def general_tensor(eng):
            v_base = a_base = 0
            for ph in range(LAYERS + 2):
                vn = {0: 4, 1: 5, 2: 5, 3: 12, 4: 12}[ph]
                an = {0: 2, 1: 1, 2: 1, 3: 4, 4: 1}[ph]
                if 1 <= ph <= LAYERS:
                    kb = NE * (ph - 1)
                    with eng.Fori(0, NE) as i:
                        eng.wait_ge(S["ge_v"], i * 8 + (8 * kb + 2))
                        eng.transpose(bank[0][:, 0:P], wide[:, :], ident[:, :]).then_inc(S["ge_m"], 1)
                        eng.wait_ge(S["ge_v"], i * 8 + (8 * kb + 3))
                        eng.wait_ge(S[f"ge_rows{ph - 1}"], i * 32 + 32)
                        eng.matmul(bank[1][:, 0:D + 1], same[:, :], g_row[:, 0:D + 1], start=True, stop=True
                                   ).then_inc(S["ge_m"], 1)
                if ph == LAYERS + 1:
                    vb, ab, mb = 8 * NE * LAYERS, 0, 0
                    with eng.Fori(0, NE) as i:
                        eng.wait_ge(S["ge_v"], i * 18 + (vb + 2))
                        eng.transpose(bank[0][:, 0:P], wide[:, :], ident[:, :]).then_inc(S["ge_m"], 1)
                        eng.wait_ge(S["ge_v"], i * 18 + (vb + 10))
                        eng.transpose(bank[1][:, 0:P], tmp[:, :], ident[:, :]).then_inc(S["ge_m"], 1)
                        eng.wait_ge(S["ge_a"], i * 3 + 2)
                        eng.transpose(bank[2][:, 0:P], same[:, :], ident[:, :]).then_inc(S["ge_m"], 1)
                        eng.wait_ge(S["ge_a"], i * 3 + 3)
                        eng.matmul(bank[3][:, 0:D], wide[:, :], g_row[:, 0:D], start=True, stop=True
                                   ).then_inc(S["ge_m"], 1)

                def body(t, n):
                    if ph in (1, 2, 3):
                        eng.wait_ge(S["gn_v"], t * vn + (v_base + 3))
                        eng.transpose(bank[0][:, 0:P], g_h[:, :], ident[:, :])
                        eng.transpose(bank[0][:, P:2 * P], g_row[:, 0:D], ident[:, :]).then_inc(S["gn_m"], 1)
                        eng.wait_ge(S["gn_a"], t * an + (a_base + 1))
                        eng.matmul(bank[1][:, 0:D], g_t[:, 0:P], wcat[:, ph - 1, 0:D], start=True, stop=False)
                        eng.matmul(bank[1][:, 0:D], g_t[:, P:2 * P], wcat[:, ph - 1, D:2 * D], start=False, stop=True
                                   ).then_inc(S["gn_m"], 1)
                    if ph == 3:
                        eng.wait_ge(S["gn_a"], t * an + (a_base + 3))
                        eng.transpose(bank[0][:, 0:P], g_h[:, :], ident[:, :]).then_inc(S["gn_m"], 1)
                        eng.wait_ge(S["gn_a"], t * an + (a_base + 4))
                        eng.matmul(bank[2][:, 0:D + 2], g_t[:, 0:P], wg[:, :], start=True, stop=True
                                   ).then_inc(S["gn_m"], 1)
                if ph in (1, 2, 3):
                    node_loop(eng, body)
                v_base += vn * NT
                a_base += an * NT

        def general_vector(eng):
            ev, nv = Count(S["ge_v"]), Count(S["gn_v"])
            m_base = a_base = 0
            eng.wait_ge(S["low_g"], 11)

            def edge_ids(o, i, kb):
                eng.wait_ge(S[f"ge_ld{kb // NE}"], i * 32 + 32)
                o(eng.tensor_copy(df[:, :], se[:, 1:2]))
                o(eng.tensor_scalar(wide[:, :], ones[:, :], df[:, 0:1], None, ALU.mult))

            def first_of(o):
                o(eng.tensor_tensor(tmp[:, :], same[:, :], low[:, :], ALU.mult))
                o(eng.tensor_reduce(g1[:, 0:1], tmp[:, :], AX.X, ALU.max))
                o(eng.tensor_scalar(g1[:, 1:2], g1[:, 0:1], FAR, None, ALU.mult))
                o(eng.tensor_tensor(w_idx[:, :], g1[:, 1:2], df[:, :], ALU.add))

            def sums(ph):
                kb = NE * (ph - 1)
                with eng.Fori(0, NE) as i:
                    ev.begin(8, i)

                    def o(ins):
                        ev.inc(ins)
                        eng.wait_ge(S["ge_v"], ev.now())
                    edge_ids(o, i, kb)
                    eng.wait_ge(S["ge_m"], i * 2 + (2 * kb + 1))
                    o(eng.tensor_scalar(same[:, :], bank[0][:, 0:P], df[:, 0:1], None, ALU.is_equal))
                    first_of(o)
                    eng.wait_ge(S["ge_m"], i * 2 + (2 * kb + 2))
                    eng.wait_ge(S[f"ge_rows{ph - 1}"], i * 32 + 32)
                    o(eng.tensor_tensor(g_new[:, 0:D + 1], g_sum[:, 0:D + 1], bank[1][:, 0:D + 1], ALU.add))
                ev.end(NE)

            def attention_sums():
                kb = NE * LAYERS
                with eng.Fori(0, NE) as i:
                    ev.begin(18, i)

                    def o(ins):
                        ev.inc(ins)
                        eng.wait_ge(S["ge_v"], ev.now())
                    edge_ids(o, i, kb)
                    eng.wait_ge(S["ge_m"], i * 4 + (2 * kb + 1))
                    o(eng.tensor_scalar(same[:, :], bank[0][:, 0:P], df[:, 0:1], None, ALU.is_equal))
                    first_of(o)
                    eng.wait_ge(S[f"ge_rows{LAYERS}"], i * 48 + 48)
                    o(eng.tensor_tensor(g1[:, 0:1], g_row[:, D:D + 1], g_dst[:, D + 1:D + 2], ALU.add))
                    o(eng.scalar_tensor_tensor(g1[:, 1:2], g1[:, 0:1], 0.2, g1[:, 0:1], ALU.mult, ALU.max))
                    o(eng.tensor_scalar(tmp[:, :], ones[:, :], g1[:, 1:2], None, ALU.mult))
                    eng.wait_ge(S["ge_m"], i * 4 + (2 * kb + 2))
                    o(eng.tensor_scalar(wide[:, :], same[:, :], -1.0, BIG, ALU.add, ALU.mult))
                    o(eng.tensor_tensor(tmp[:, :], bank[1][:, 0:P], wide[:, :], ALU.add))
                    o(eng.tensor_reduce(g1[:, 2:3], tmp[:, :], AX.X, ALU.max))
                    o(eng.tensor_tensor(g_new[:, D + 1:D + 2], g1[:, 2:3], g_sum[:, D + 1:D + 2], ALU.max))
                    o(eng.tensor_scalar(g1[:, 4:5], g_new[:, D + 1:D + 2], -1.0, None, ALU.mult))
                    o(eng.tensor_tensor(g1[:, 5:6], g_sum[:, D + 1:D + 2], g_new[:, D + 1:D + 2], ALU.subtract))
                    eng.wait_ge(S["ge_a"], i * 3 + 2)
                    o(eng.scalar_tensor_tensor(g_new[:, D:D + 1], g_sum[:, D:D + 1], g1[:, 6:7], g1[:, 7:8],
                                               ALU.mult, ALU.add))
                    eng.wait_ge(S["ge_m"], i * 4 + (2 * kb + 4))
                    o(eng.scalar_tensor_tensor(g_new[:, 0:D], g_sum[:, 0:D], g1[:, 6:7], bank[3][:, 0:D],
                                               ALU.mult, ALU.add))
                ev.end(NE)

            for ph in range(LAYERS + 2):
                if 1 <= ph <= LAYERS:
                    sums(ph)
                if ph == LAYERS + 1:
                    attention_sums()
                vn = {0: 4, 1: 5, 2: 5, 3: 12, 4: 12}[ph]
                mn = {0: 0, 1: 2, 2: 2, 3: 4, 4: 0}[ph]
                an = {0: 2, 1: 1, 2: 1, 3: 4, 4: 1}[ph]
                ln = 16 * {0: 1, 3: 3, 4: 3}.get(ph, 2)

                def body(t, n):
                    nv.begin(vn, t)

                    def o(ins):
                        nv.inc(ins)
                        eng.wait_ge(S["gn_v"], nv.now())

                    def stats_of(tile):
                        o(eng.bn_stats(g_st[:, :], tile))
                        if n == P:
                            eng.sem_inc(S["turn_v"], 1)
                        o(eng.bn_aggr(g_mv[:, :], g_st[:, :]))

                    def scale_of(a_at):
                        eng.wait_ge(S["gn_a"], t * an + (a_base + a_at))
                        o(eng.reciprocal(g1[:, 1:2], g1[:, 0:1]))
                        o(eng.scalar_tensor_tensor(g1[:, 2:3], g_mv[:, 0:1], -1.0, g1[:, 1:2], ALU.mult, ALU.mult))
                    eng.wait_ge(S[f"gn_ld{ph}"], t * ln + ln)
                    if ph == 0:
                        stats_of(g_x[:, :])
                        scale_of(1)
                    elif ph <= LAYERS:
                        o(eng.tensor_scalar(g1[:, 0:1], g_sum[:, D:D + 1], 1.0, None, ALU.max))
                        o(eng.reciprocal(g1[:, 1:2], g1[:, 0:1]))
                        o(eng.tensor_scalar(g_h[:, :], g_sum[:, 0:D], g1[:, 1:2], None, ALU.mult))
                        eng.wait_ge(S["gn_m"], t * mn + (m_base + 2))
                        o(eng.tensor_tensor(tmp[:, :], bank[1][:, 0:D], b_bc[:, ph - 1, :], ALU.add))
                        to = g_node[:, 0:D] if ph < LAYERS else wide[:, :]
                        o(eng.scalar_tensor_tensor(to, tmp[:, :], 0.01, tmp[:, :], ALU.mult, ALU.max))
                        if ph == LAYERS:
                            o(eng.tensor_tensor(g_x1[:, :], wide[:, :], g_x[:, :], ALU.add))
                            o(eng.tensor_tensor(g_x1b[:, :], g_x1[:, :], b_bc[:, LAYERS, :], ALU.add))
                            stats_of(g_x1[:, :])
                            scale_of(2)
                            eng.wait_ge(S["gn_m"], t * mn + (m_base + 4))
                            o(eng.tensor_copy(g_node[:, 0:D + 2], bank[2][:, 0:D + 2]))
                    else:
                        o(eng.tensor_tensor(g1[:, 0:1], g_row[:, D:D + 1], g_row[:, D + 1:D + 2], ALU.add))
                        o(eng.scalar_tensor_tensor(g1[:, 1:2], g1[:, 0:1], 0.2, g1[:, 0:1], ALU.mult, ALU.max))
                        o(eng.tensor_tensor(g1[:, 0:1], g1[:, 1:2], g_sum[:, D + 1:D + 2], ALU.max))
                        o(eng.tensor_tensor(g1[:, 2:3], g_sum[:, D + 1:D + 2], g1[:, 0:1], ALU.subtract))
                        o(eng.tensor_tensor(g1[:, 3:4], g1[:, 1:2], g1[:, 0:1], ALU.subtract))
                        eng.wait_ge(S["gn_a"], t * an + (a_base + 1))
                        o(eng.tensor_scalar(g1[:, 6:7], g1[:, 5:6], 1e-16, None, ALU.add))
                        o(eng.scalar_tensor_tensor(g1[:, 7:8], g_sum[:, D:D + 1], g1[:, 4:5], g1[:, 6:7],
                                                   ALU.mult, ALU.add))
                        o(eng.reciprocal(g1[:, 0:1], g1[:, 7:8]))
                        o(eng.tensor_scalar(tmp[:, :], g_sum[:, 0:D], g1[:, 4:5], None, ALU.mult))
                        o(eng.scalar_tensor_tensor(wide[:, :], g_row[:, 0:D], g1[:, 5:6], tmp[:, :], ALU.mult, ALU.add))
                        o(eng.tensor_scalar(tmp[:, :], wide[:, :], g1[:, 0:1], None, ALU.mult))
                        o(eng.tensor_tensor(g_out[:, :], tmp[:, :], g_x1b[:, :], ALU.add))
                node_loop(eng, body)
                nv.end(NT)
                m_base += mn * NT
                a_base += an * NT

        block.sync(sync_program)
        block.gpsimd(gpsimd_program)
        block.scalar(scalar_program)
        block.tensor(tensor_program)
        block.vector(vector_program)

_INS = ['x', 'src', 'dst', 'L0_gnn_Wl1', 'L0_gnn_bl1', 'L0_gnn_Wr1', 'L0_gnn_Wlh', 'L0_gnn_blh', 'L0_gnn_Wrh',
        'L1_gnn_W', 'L1_gnn_att_src', 'L1_gnn_att_dst', 'L1_gnn_bias']


def kernel(**inputs):
    import numpy as _np
    import concourse.bacc as _bacc
    from concourse import mybir as _mybir
    from concourse.bass_utils import run_bass_kernel_spmd as _run

    nc = _bacc.Bacc("TRN2", target_bir_lowering=False, num_devices=1)
    arrays, args = {}, []
    for name in _INS:
        a = _np.ascontiguousarray(inputs[name])
        arrays[f"in_{name}"] = a
        args.append(nc.dram_tensor(f"in_{name}", a.shape, _mybir.dt.from_np(a.dtype), kind="ExternalInput").ap())
    args.append(nc.dram_tensor("out_0", (N, D), _mybir.dt.float32, kind="ExternalOutput").ap())
    build(nc, *args)
    return _run(nc, [arrays], core_ids=[0]).results[0]["out_0"]
```

```python
import concourse.bass as bass
from concourse import mybir
from contextlib import ExitStack

F32 = mybir.dt.float32
BF16 = mybir.dt.bfloat16
I32 = mybir.dt.int32
ALU = mybir.AluOpType
ACT = mybir.ActivationFunctionType
AX = mybir.AxisListType

P = 128
N = 50000
E = 100000
D = 128
TILE = 2 * P
NG = -(-N // TILE)
NPAD = NG * TILE
TAIL = N - (NG - 1) * TILE
BEYOND = 1 << 20
NW = 3
OFF = 56
CH = 5
RUN = CH * P
BAND = [0, 0, 1, 1, 1]
HALF = NG // 2
RING = 4
NT = -(-N // P)
NE = -(-E // P)
TAIL_T = N - (NT - 1) * P
NAT_P, NAT = 125, 800
CW = 132
FAR = float(1 << 18)
NOWHERE = -1000.0
BIG = 2.0 ** 126
LAYERS = 3
EP = (E // (RUN + 1) + 2) * (RUN + 1)


class Step:

    def __init__(self, i, off):
        if i is not None and off < 0:
            i, off = i - 1, off + RING
        self.i, self.off = i, off
        self.t = off if i is None else RING * i + off
        self.b = off % 2
        self.r = off % RING
        self.there = i is not None or 0 <= off < NG
        self.last = i is None and off == NG - 1

    def at(self, d):
        return Step(self.i, self.off + d)

    def uses(self, ring):
        return self.off // ring if self.i is None else (RING // ring) * self.i + self.off // ring


def steps(eng, late, body):
    for t in range(RING):
        body(Step(None, t))
    with eng.Fori(1, NG // RING - 1) as i:
        for off in range(RING):
            body(Step(i, off))
    for t in range(NG - RING, NG + late):
        body(Step(None, t))


def wait(eng, sem, value):
    if not isinstance(value, int) or value > 0:
        eng.wait_ge(sem, value)


class Count:

    def __init__(self, sem):
        self.sem, self.base, self.per, self.i, self.n = sem, 0, 0, 0, 0

    def begin(self, per, i):
        self.per, self.i, self.n = per, i, 0

    def inc(self, instruction, by=1):
        instruction.then_inc(self.sem, by)
        self.n += by

    def now(self):
        return self.at(self.n)

    def at(self, n):
        return self.i * self.per + (self.base + n)

    def end(self, steps):
        assert self.n == self.per, (self.n, self.per)
        self.base += self.per * steps


def build(nc, x, src, dst, wl1, bl1, wr1, wlh, blh, wrh, w_gat, att_s, att_d, bias, out):
    ctx = ExitStack()
    with ctx:
        def sb(name, shape, dt=F32):
            return ctx.enter_context(nc.sbuf_tensor(name, shape, dt))

        def sem(name):
            return ctx.enter_context(nc.semaphore(name))

        tab = [nc.dram_tensor(f"tab{i}", [2 * NPAD, D], F32).ap() for i in range(2)]
        gen_h = nc.dram_tensor("gen_h", [NT * P, CW], F32).ap()
        gen_s = nc.dram_tensor("gen_s", [NT * P, CW], F32).ap()
        edges = [nc.dram_tensor(f"edges{i}", [EP], I32).ap() for i in range(2)]
        tab_c = nc.dram_tensor("tab_c", [NPAD, CW], F32).ap()
        x1_d = nc.dram_tensor("x1_d", [NPAD, D], F32).ap()

        ident = sb("ident", [P, P])
        ones = sb("ones", [P, P])
        iota_i = sb("iota_i", [P, RUN], I32)
        iota = sb("iota", [P, RUN])
        iota_c = sb("iota_c", [P, NW * P], BF16)
        iota_b = sb("iota_b", [P, TILE], BF16)
        part_i = sb("part_i", [P, 2], I32)
        part = sb("part", [P, 2])
        thr = sb("thr", [P, 2])
        eps = sb("eps", [P, 1])

        w_raw = sb("w_raw", [P, 7, P])
        wcat = sb("wcat", [P, LAYERS, 2 * D])
        w_t = sb("w_t", [P, P])
        wg = sb("wg", [P, D + 2])
        att = sb("att", [P, 2])
        b_bc = sb("b_bc", [P, LAYERS + 1, D])

        d_nat = sb("d_nat", [NAT_P, NAT], I32)
        d_nxt = sb("d_nxt", [NAT_P, NAT], I32)
        s_nat = sb("s_nat", [NAT_P, NAT], I32)
        cmp_n = sb("cmp_n", [NAT_P, NAT])
        cmp_m = sb("cmp_m", [NAT_P, NAT])
        first = sb("first", [NAT_P, P])
        pad = sb("pad", [2, (EP - E) // 2], I32)
        row_d = sb("row_d", [HALF, 2, NAT], I32)
        row_i = sb("row_i", [HALF, 2], I32)
        row_c = sb("row_c", [HALF, 2])
        in_row = sb("in_row", [HALF, 2])
        e_first = sb("e_first", [HALF, 2])
        start_i = sb("start_i", [HALF, 2], I32)
        run_s = sb("run_s", [HALF, 2, RUN + 1], I32)
        run_d = sb("run_d", [HALF, 2, RUN + 1], I32)
        w_a = sb("w_a", [HALF, RUN])
        w_b = sb("w_b", [HALF, RUN])
        w_valid = sb("w_valid", [HALF, RUN])
        w_int = sb("w_int", [HALF, 2, RUN], I32)
        qty = sb("qty", [HALF, 4, RUN])
        extra = sb("extra", [HALF, 1])
        stat = sb("stat", [P, 8])
        stat_sb = sb("stat_sb", [1, 8])
        flag_f = sb("flag_f", [1, 8])
        flag = sb("flag", [1, 1], I32)
        place = sb("place", [P, NG, CH])
        vals = sb("vals", [P, NG, CH, 4], BF16)
        cmask = sb("cmask", [P, 2, CH, TILE], BF16)
        placed = sb("placed", [P, NG, NW, 4])
        idx = sb("idx", [P, NG, NW], I32)
        dcol = sb("dcol", [P, NG, NW])
        empty = sb("empty", [P, NG * NW])

        ibuf = sb("ibuf", [P, RING, NW], I32)
        rows = sb("rows", [P, RING, NW, CW])
        own = sb("own", [P, 2, 2, 2 * D])
        xin = sb("xin", [P, 2, 2, D])
        mask = sb("mask", [P, 2, 4 * P])
        h = sb("h", [P, 2, 2 * D])
        h_t = sb("h_t", [P, 2, 2 * P])
        gu = sb("gu", [P, 2, 2, 2 * D])
        tsum = sb("tsum", [P, 2, D])
        zed = sb("zed", [P, 2, D])
        x1 = sb("x1", [P, 2, 2, D])
        x1b = sb("x1b", [P, 2, 2, D])
        cnt = sb("cnt", [P, 2])
        inv = sb("inv", [P, 2])
        bst = sb("bst", [P, 2, 6])
        mv = sb("mv", [P, 2, 2, 2])
        std = sb("std", [P, 2, 2])
        rstd = sb("rstd", [P, 2, 2])
        nmr = sb("nmr", [P, 2, 2])
        own_c = sb("own_c", [P, RING, 2, CW])
        x1c = sb("x1c", [P, RING, 2, D])
        cut = sb("cut", [P, 2, 4 * P], BF16)
        ident_b = sb("ident_b", [P, P], BF16)
        zb = sb("zb", [P, 2, 2, TILE])
        lr = sb("lr", [P, 2, 2, TILE])
        mx = sb("mx", [P, 2])
        zs = sb("zs", [P, 2, 2])
        ls = sb("ls", [P, 2, 2])
        nm = sb("nm", [P, 2, 2])
        dself = sb("dself", [P, 2, 2])
        pself = sb("pself", [P, 2, 2])
        den = sb("den", [P, 2, 2])
        ptwo = sb("ptwo", [P, 2])
        dsum = sb("dsum", [P, 2])
        rden = sb("rden", [P, 2])
        prob = sb("prob", [P, 2, 2, TILE])
        prob_t = sb("prob_t", [P, 2, 2, TILE])
        acc = sb("acc", [P, 2, D])
        res = sb("res", [P, 2, 2, D])

        low = sb("low", [P, P])
        se = sb("se", [P, 2], I32)
        g_row = sb("g_row", [P, CW])
        g_dst = sb("g_dst", [P, CW])
        g_sum = sb("g_sum", [P, CW])
        g_new = sb("g_new", [P, CW])
        g_node = sb("g_node", [P, CW])
        g_init = sb("g_init", [P, 2, CW])
        df = sb("df", [P, 1])
        wide = sb("wide", [P, P])
        same = sb("same", [P, P])
        tmp = sb("tmp", [P, P])
        g1 = sb("g1", [P, 8])
        w_idx = sb("w_idx", [P, 1], I32)
        g_x = sb("g_x", [P, D])
        g_x1 = sb("g_x1", [P, D])
        g_x1b = sb("g_x1b", [P, D])
        g_h = sb("g_h", [P, D])
        g_t = sb("g_t", [P, 2 * P])
        g_st = sb("g_st", [P, 6])
        g_mv = sb("g_mv", [P, 2])
        g_out = sb("g_out", [P, D])

        bank = [ctx.enter_context(nc.psum_tensor(f"bank{i}", [P, 512], F32)) for i in range(8)]
        ps_agg = [bank[0], bank[1]]
        ps_t = [bank[2], bank[3]]
        ps_g = [bank[4], bank[5]]
        ps_u = [bank[6], bank[7]]
        ps_place = bank[1]
        ps_z = [bank[0], bank[1]]
        ps_pt = [bank[4], bank[5]]
        ps_o = [bank[6], bank[7]]

        def pair(bk, w=D, stride=D):
            return bk[:, 0:2 * stride].rearrange("p (j w) -> p j w", j=2)[:, :, 0:w]

        names = ("const_g const_v prep_v prep_p prep_ld nat_ld nxt_ld snat_ld wt_ld att_ld bb_ld row_ld run_ld "
                 "wt_ps wt_cp first_ps idx_g cm_done cm_used pl_ps pl_cp prep_end "
                 "x_ld0 x_ld1 own_ld0 own_ld1 ibuf_cp mask_done agg_done cnt_v tsum_v inv_v z_v h_v "
                 "ln_v ln_a rs_v nmr_v h_a tr_done ht_cp dense_done g_cp u_cp st0 st1 x1_v x1b_v stx0 stx1 "
                 "turn cl0 cl1 cl2 cl3 cut_v zm_done z_a lr_v bn_v nm_v ex_a pt_done pt_cp pv_done "
                 "den_v acc_v res_v out0 out1 zrow ident_bv flag_v flag_ps wg_cp flag_rdy ge_ld0 ge_rows0 ge_st0 ge_ld1 ge_rows1 ge_st1 ge_ld2 ge_rows2 ge_st2 ge_ld3 ge_rows3 ge_st3 gn_ld0 gn_st0 gn_ld1 gn_st1 gn_ld2 gn_st2 gn_ld3 gn_st3 gn_ld4 gn_st4 ge_v ge_a ge_m gn_v gn_a gn_m low_g edge_st prep_seq turn_v turn_s cs_v cd_v").split()
        S = {n: sem(n) for n in names}
        row_ld = [[sem(f"row_ld{r}_{w}") for w in range(NW)] for r in range(RING)]

        block = ctx.enter_context(nc.Block())

        def tab_rows(t, p):
            return tab[p][bass.ds(t * (2 * TILE), 2 * TILE), :].rearrange("(j p r) d -> p j (r d)", j=2, r=2)

        def node_rows(a, t):
            return a[bass.ds(t * TILE, TILE), :].rearrange("(j p) d -> p j d", j=2)

        def sync_program(eng):
            wt = S["wt_ld"]
            eng.dma_start(w_raw[:, 0, :], wl1).then_inc(wt, 16)
            eng.dma_start(w_raw[:, 1, :], wr1).then_inc(wt, 16)
            for l in range(2):
                eng.dma_start(w_raw[:, 2 + 2 * l, :], wlh[l, :, :]).then_inc(wt, 16)
                eng.dma_start(w_raw[:, 3 + 2 * l, :], wrh[l, :, :]).then_inc(wt, 16)
            eng.dma_start(w_raw[:, 6, :], w_gat).then_inc(wt, 16)
            eng.dma_start(att[:, 0:1], att_s.rearrange("(p a) -> p a", a=1)).then_inc(wt, 16)
            eng.dma_start(att[:, 1:2], att_d.rearrange("(p a) -> p a", a=1)).then_inc(wt, 16)
            for n, b in enumerate([bl1, blh[0, :], blh[1, :], bias]):
                eng.dma_start(b_bc[:, n, :], b.partition_broadcast(P)).then_inc(wt, 16)
            eng.dma_start(d_nat[:, :], dst.rearrange("(p a) -> p a", a=NAT)).then_inc(S["nat_ld"], 16)
            eng.dma_start(s_nat[:, :], src.rearrange("(p a) -> p a", a=NAT)).then_inc(S["nat_ld"], 16)
            for a, to in zip((src, dst), edges):
                eng.dma_start(to[0:E].rearrange("(p a) -> p a", a=NAT), a.rearrange("(p a) -> p a", a=NAT)
                              ).then_inc(S["edge_st"], 16)
            eng.wait_ge(S["const_v"], 1)
            for to in edges:
                eng.dma_start(to[E:EP].rearrange("(p a) -> p a", p=2), pad[:, :]).then_inc(S["edge_st"], 16)
            eng.dma_start(d_nxt[0:NAT_P - 1, :],
                          dst[1:1 + (NAT_P - 1) * NAT].rearrange("(p a) -> p a", a=NAT)).then_inc(S["nxt_ld"], 16)
            eng.dma_start(d_nxt[NAT_P - 1:NAT_P, 0:NAT - 1],
                          dst[1 + (NAT_P - 1) * NAT:E].rearrange("(p a) -> p a", p=1)).then_inc(S["nxt_ld"], 16)

            eng.wait_ge(S["flag_rdy"], 1)
            ok = eng.value_load(flag[0:1, 0:1], min_val=0, max_val=1)
            with eng.If(ok):
                fast_sync(eng)
            with eng.Else():
                general_sync(eng)

        def fast_sync(eng):
            def load_x(s):
                ld = S[f"x_ld{s.b}"]
                if s.last:
                    eng.dma_start(xin[0:TAIL, s.b, 0, :], x[N - TAIL:N, :]).then_inc(ld, 16)
                else:
                    eng.dma_start(xin[:, s.b, :, :], node_rows(x, s.t)).then_inc(ld, 16)

            def store(o, ph):
                eng.wait_ge(S["g_cp"], ph * NG + o.t + 1)
                eng.wait_ge(S["u_cp"], ph * NG + o.t + 1)
                eng.dma_start(tab_rows(o.t, ph % 2), gu[:, o.b, :, :]).then_inc(S[f"st{o.b}"], 16)

            def phase0(s):
                for g in [s, s.at(1)] if s.i is None and s.t == 0 else [s.at(1)]:
                    if g.there:
                        wait(eng, S["h_a"], g.t - 1)
                        load_x(g)
                if s.at(-2).there:
                    store(s.at(-2), 0)
            eng.wait_ge(S["const_g"], 5)
            steps(eng, 2, phase0)

            for ph in range(1, LAYERS + 1):
                ka = (ph - 1) * NG
                for b in range(2):
                    eng.wait_ge(S[f"st{b}"], 16 * (ph * NG // 2))

                def load(g):
                    wait(eng, S["h_v"], ka + g.t - 1)
                    eng.dma_start(own[:, g.b, :, :], tab_rows(g.t, (ph - 1) % 2)).then_inc(S[f"own_ld{g.b}"], 16)
                    if ph == LAYERS:
                        wait(eng, S["x1_v"], g.t - 1)
                        load_x(g)

                def phase(s):
                    for g in [s, s.at(1)] if s.i is None and s.t == 0 else [s.at(1)]:
                        if g.there:
                            load(g)
                    if ph < LAYERS and s.at(-2).there:
                        store(s.at(-2), ph)
                    if ph == LAYERS and s.at(-1).there:
                        o = s.at(-1)
                        eng.wait_ge(S["x1b_v"], o.t + 1)
                        eng.dma_start(node_rows(x1_d, o.t), x1b[:, o.b, :, :]).then_inc(S[f"stx{o.b}"], 16)
                    if ph == LAYERS and s.at(-3).there:
                        o = s.at(-3)
                        eng.wait_ge(S["g_cp"], ph * NG + o.t + 1)
                        eng.dma_start(node_rows(tab_c, o.t), gu[:, o.b, :, 0:CW]).then_inc(S[f"st{o.b}"], 16)
                steps(eng, 3 if ph == LAYERS else 2, phase)

            for b in range(2):
                eng.wait_ge(S[f"st{b}"], 16 * ((LAYERS + 1) * NG // 2))
                eng.wait_ge(S[f"stx{b}"], 16 * (NG // 2))

            def phase_c(s):
                for g in [s, s.at(1)] if s.i is None and s.t == 0 else [s.at(1)]:
                    if g.there:
                        wait(eng, S["res_v"], g.t - RING + 1)
                        eng.dma_start(own_c[:, g.r, :, :], node_rows(tab_c, g.t)).then_inc(S[f"cl{g.r}"], 16)
                        eng.dma_start(x1c[:, g.r, :, :], node_rows(x1_d, g.t)).then_inc(S[f"cl{g.r}"], 16)
                o = s.at(-2)
                if o.there:
                    eng.wait_ge(S["res_v"], o.t + 1)
                    if o.last:
                        eng.dma_start(out[N - TAIL:N, :], res[0:TAIL, o.b, 0, :]).then_inc(S[f"out{o.b}"], 16)
                    else:
                        eng.dma_start(node_rows(out, o.t), res[:, o.b, :, :]).then_inc(S[f"out{o.b}"], 16)
            steps(eng, 2, phase_c)
            for b in range(2):
                eng.wait_ge(S[f"out{b}"], 16 * NG // 2)

        def gpsimd_program(eng):
            g = S["const_g"]
            eng.memset(ident[:, :], 0.0).then_inc(g, 1)
            eng.iota(iota_i[:, :], pattern=[[1, RUN]], base=0, channel_multiplier=0).then_inc(g, 1)
            eng.iota(part_i[:, :], pattern=[[P, 2]], base=0, channel_multiplier=1).then_inc(g, 1)
            eng.memset(xin[:, :, :, :], 0.0).then_inc(g, 1)
            eng.wait_ge(g, 1)
            eng.affine_select(out=ident[:, :], in_=ident[:, :], compare_op=ALU.not_equal, fill=1.0,
                              base=0, pattern=[[-1, P]], channel_multiplier=1).then_inc(g, 1)
            eng.memset(rows[:, :, :, :], 0.0).then_inc(S["zrow"], 1)
            eng.memset(low[:, :], 0.0).then_inc(S["low_g"], 1)
            eng.memset(g_row[:, :], 0.0).then_inc(S["low_g"], 1)
            eng.memset(g_dst[:, :], 0.0).then_inc(S["low_g"], 1)
            eng.memset(g_sum[:, :], 0.0).then_inc(S["low_g"], 1)
            eng.memset(g_new[:, :], 0.0).then_inc(S["low_g"], 1)
            eng.memset(g_node[:, :], 0.0).then_inc(S["low_g"], 1)
            eng.memset(g_x[:, :], 0.0).then_inc(S["low_g"], 1)
            eng.memset(g_init[:, :, :], 0.0).then_inc(S["low_g"], 1)
            eng.wait_ge(S["low_g"], 8)
            eng.affine_select(out=low[:, :], in_=low[:, :], compare_op=ALU.is_ge, fill=1.0,
                              base=0, pattern=[[1, P]], channel_multiplier=-1).then_inc(S["low_g"], 1)
            eng.memset(g_init[:, 1, D + 1:D + 2], -BIG).then_inc(S["low_g"], 1)
            eng.memset(g_node[:, D:D + 1], 1.0).then_inc(S["low_g"], 1)

            eng.wait_ge(S["prep_v"], 1)
            for q in range(2):
                eng.indirect_dma_start(out=row_d[:, q, :], out_offset=None,
                                       in_=dst.rearrange("(p a) -> p a", a=NAT),
                                       in_offset=bass.IndirectOffsetOnAxis(ap=row_i[:, q:q + 1], axis=0)
                                       ).then_inc(S["row_ld"], 16)
            eng.wait_ge(S["prep_v"], 2)
            eng.wait_ge(S["edge_st"], 64)
            view = [a.rearrange("(p a) -> p a", a=RUN + 1) for a in edges]
            for q in range(2):
                for a, to in zip(view, (run_s, run_d)):
                    eng.indirect_dma_start(out=to[:, q, :], out_offset=None, in_=a,
                                           in_offset=bass.IndirectOffsetOnAxis(ap=start_i[:, q:q + 1], axis=1)
                                           ).then_inc(S["run_ld"], 16)

            eng.wait_ge(S["flag_rdy"], 1)
            ok = eng.value_load(flag[0:1, 0:1], min_val=0, max_val=1)
            with eng.If(ok):
                fast_gpsimd(eng)
            with eng.Else():
                general_gpsimd(eng)

        def fast_gpsimd(eng):
            eng.wait_ge(S["zrow"], 2)
            for ph in range(1, LAYERS + 2):
                ka = (ph - 1) * NG
                for b in range(2):
                    eng.wait_ge(S[f"st{b}"], 16 * (ph * NG // 2))
                table = tab[(ph - 1) % 2] if ph <= LAYERS else tab_c
                width = D if ph <= LAYERS else CW
                last = 2 * NPAD - 1 if ph <= LAYERS else NPAD - 1

                def gathers(s):
                    if not s.there:
                        return
                    eng.wait_ge(S["ibuf_cp"], ka + s.t + 1)
                    if ph <= LAYERS:
                        wait(eng, S["agg_done"], ka + s.t - RING + 1)
                    else:
                        wait(eng, S["pv_done"], s.t - RING + 1)
                    if s.i is not None:
                        eng.sem_inc(S["turn"], 1)
                    for w in range(NW):
                        eng.indirect_dma_start(out=rows[:, s.r, w, 0:width], out_offset=None, in_=table,
                                               in_offset=bass.IndirectOffsetOnAxis(ap=ibuf[:, s.r, w:w + 1], axis=0),
                                               bounds_check=last, oob_is_err=False
                                               ).then_inc(row_ld[s.r][w], 16)
                if ph == LAYERS + 1:
                    eng.wait_ge(S["agg_done"], LAYERS * NG)
                steps(eng, 0, gathers)

        def scalar_program(eng):
            for n in range(7):
                eng.wait_ge(S["wt_ps"], n + 1)
                to = wcat[:, n // 2, (n % 2) * D:(n % 2 + 1) * D] if n < 6 else w_t[:, :]
                eng.activation(to, bank[n][:, 0:P], ACT.Copy).then_inc(S["wt_cp"], 1)
            eng.activation(wg[:, 0:D], w_raw[:, 6, :], ACT.Copy).then_inc(S["wt_cp"], 1)
            eng.wait_ge(S["wt_ps"], 8)
            eng.activation(wg[:, D:D + 2], bank[0][:, 0:2], ACT.Copy).then_inc(S["wg_cp"], 1)

            for q in range(2):
                for k in range(4):
                    n = 4 * q + k
                    eng.wait_ge(S["prep_p"], n + 1)
                    view = bank[n % 4 + 2][:, 0:CH * HALF].rearrange("p (c t) -> p t c", c=CH)
                    to = place[:, q * HALF:(q + 1) * HALF, :] if k == 0 else \
                        vals[:, q * HALF:(q + 1) * HALF, :, k - 1]
                    eng.activation(to, view, ACT.Copy).then_inc(S["pl_cp"], 1)

            eng.wait_ge(S["flag_rdy"], 1)
            ok = eng.value_load(flag[0:1, 0:1], min_val=0, max_val=1)
            with eng.If(ok):
                fast_scalar(eng)
            with eng.Else():
                general_scalar(eng)

        def fast_scalar(eng):
            def norm_scale(g, k):
                eng.wait_ge(S["ln_v"], k + 1)
                eng.activation(std[:, g.b, :], mv[:, g.b, :, 1], ACT.Sqrt, bias=eps[:, 0:1]).then_inc(S["ln_a"], 1)

            def norm(g, k, kb, tile):
                eng.wait_ge(S["nmr_v"], k + 1)
                wait(eng, S["tr_done"], kb + g.t - 1)
                for j in range(2):
                    a = eng.activation(h[:, g.b, j * D:(j + 1) * D], tile[:, g.b, j, :], ACT.Relu,
                                       bias=nmr[:, g.b, j:j + 1], scale=rstd[:, g.b, j:j + 1])
                a.then_inc(S["h_a"], 1)

            def ht_copy(g, kb):
                eng.wait_ge(S["tr_done"], kb + g.t + 1)
                wait(eng, S["dense_done"], kb + g.t - 1)
                eng.activation(h_t[:, g.b, :], ps_t[g.b][:, 0:2 * P], ACT.Copy).then_inc(S["ht_cp"], 1)

            def g_copy(g, kb, width=D):
                eng.wait_ge(S["dense_done"], kb + g.t + 1)
                wait(eng, S[f"st{g.b}"], 16 * (kb // 2 + g.uses(2)))
                eng.activation(gu[:, g.b, :, 0:width], pair(ps_g[g.b], width, TILE), ACT.Copy).then_inc(S["g_cp"], 1)

            def phase0(s):
                if s.at(-1).there:
                    norm(s.at(-1), s.t - 1, 0, xin)
                if s.at(-2).there:
                    g_copy(s.at(-2), 0)
                if s.there:
                    eng.wait_ge(S["pl_ps"], s.t + 1)
                    eng.activation(placed[:, bass.ds(s.t, 1), :, :].rearrange("p t w v -> p (t w v)"),
                                   ps_place[:, s.b * 16:s.b * 16 + NW * 4], ACT.Copy).then_inc(S["prep_end"], 1)
                    norm_scale(s, s.t)
                if s.at(-1).there:
                    ht_copy(s.at(-1), 0)
            steps(eng, 2, phase0)

            def idx_copy(g, ph):
                ka = (ph - 1) * NG
                for w in range(NW):
                    wait(eng, row_ld[g.r][w], 16 * (ka // RING + g.uses(RING)))
                frm = idx[:, bass.ds(g.t, 1), :].rearrange("p t w -> p (t w)")
                eng.activation(ibuf[:, g.r, :], frm, ACT.Copy,
                               scale=1.0 if ph <= LAYERS else 0.5).then_inc(S["ibuf_cp"], 1)

            eng.wait_ge(S["idx_g"], 1)
            for ph in range(1, LAYERS + 1):
                kb = ph * NG
                late = 1 if ph == LAYERS else 0

                def phase(s):
                    for g in [s, s.at(1), s.at(2)] if s.i is None and s.t == 0 else [s.at(2)]:
                        if g.there:
                            idx_copy(g, ph)
                    if ph == LAYERS and s.at(-1).there:
                        norm(s.at(-1), NG + s.t - 1, kb, x1)
                    if s.at(-2 - late).there:
                        g_copy(s.at(-2 - late), kb, D if ph < LAYERS else D + 2)
                    if s.at(-1 - late).there:
                        ht_copy(s.at(-1 - late), kb)
                    if ph == LAYERS and s.there:
                        norm_scale(s, NG + s.t)
                steps(eng, 2 + late, phase)

            def phase_c(s):
                for g in [s, s.at(1), s.at(2)] if s.i is None and s.t == 0 else [s.at(2)]:
                    if g.there:
                        idx_copy(g, LAYERS + 1)
                o = s.at(-1)
                if o.there:
                    eng.wait_ge(S["nm_v"], o.t + 1)
                    wait(eng, S["pt_done"], o.t - 1)
                    wait(eng, S["res_v"], o.t - 1)
                    for j in range(2):
                        eng.activation(prob[:, o.b, j, :], lr[:, o.b, j, :], ACT.Exp, bias=nm[:, o.b, j:j + 1],
                                       accum_out=den[:, o.b, j:j + 1])
                    eng.activation(pself[:, o.b, :], dself[:, o.b, :], ACT.Exp).then_inc(S["ex_a"], 1)
                if s.there:
                    eng.wait_ge(S[f"cl{s.r}"], 32 * (s.uses(RING) + 1))
                    eng.wait_ge(S["zm_done"], s.t + 1)
                    wait(eng, S["lr_v"], s.t - 1)
                    for j in range(2):
                        a = eng.activation(zb[:, s.b, j, :], ps_z[s.b][:, j * TILE:(j + 1) * TILE], ACT.Identity,
                                           bias=own_c[:, s.r, j, D + 1:D + 2])
                    a.then_inc(S["z_a"], 1)
                o = s.at(-2)
                if o.there:
                    eng.wait_ge(S["pt_done"], o.t + 1)
                    wait(eng, S["pv_done"], o.t - 1)
                    eng.activation(prob_t[:, o.b, :, :].rearrange("p j e -> p (j e)"), ps_pt[o.b][:, :],
                                   ACT.Copy).then_inc(S["pt_cp"], 1)
            steps(eng, 2, phase_c)

        def tensor_program(eng):
            eng.wait_ge(S["const_g"], 5)
            eng.wait_ge(S["wt_ld"], 16 * 13)
            for n in range(7):
                eng.transpose(bank[n][:, 0:P], w_raw[:, n, :], ident[:, :]).then_inc(S["wt_ps"], 1)
            eng.wait_ge(S["wt_cp"], 7)
            eng.matmul(bank[0][:, 0:2], w_t[:, :], att[:, :], start=True, stop=True).then_inc(S["wt_ps"], 1)
            eng.wait_ge(S["prep_ld"], 1)
            eng.transpose(bank[7][:, 0:NAT_P], first[:, :], ident[0:NAT_P, 0:NAT_P]).then_inc(S["first_ps"], 1)
            eng.wait_ge(S["wt_cp"], 8)
            for q in range(2):
                for k in range(4):
                    n = 4 * q + k
                    eng.wait_ge(S["prep_v"], 3 + q)
                    if n >= 4:
                        eng.wait_ge(S["pl_cp"], n - 3)
                    for c in range(CH):
                        m = eng.transpose(bank[n % 4 + 2][:, c * HALF:(c + 1) * HALF],
                                          qty[:, k, c * P:(c + 1) * P], ident[0:HALF, 0:HALF])
                    m.then_inc(S["prep_p"], 1)
            eng.wait_ge(S["flag_v"], 1)
            eng.matmul(bank[1][0:1, 0:8], ones[:, 0:1], stat[:, :], start=True, stop=True).then_inc(S["flag_ps"], 1)

            eng.wait_ge(S["flag_rdy"], 1)
            ok = eng.value_load(flag[0:1, 0:1], min_val=0, max_val=1)
            with eng.If(ok):
                fast_tensor(eng)
            with eng.Else():
                general_tensor(eng)

        def fast_tensor(eng):
            eng.wait_ge(S["pl_cp"], 8)

            def placing(s):
                eng.wait_ge(S["cm_done"], s.t + 1)
                wait(eng, S["prep_end"], s.t - 1)
                for w in range(NW):
                    cs = [c for c in range(CH) if w - BAND[c] in (0, 1)]
                    for c in cs:
                        a = (w - BAND[c]) * P
                        m = eng.matmul(ps_place[:, s.b * 16 + 4 * w:s.b * 16 + 4 * w + 3], cmask[:, s.b, c, a:a + P],
                                       vals[:, bass.ds(s.t, 1), c, 0:3].rearrange("p t v -> p (t v)"),
                                       start=(c == cs[0]), stop=(c == cs[-1]))
                m.then_inc(S["pl_ps"], 1)

            def turn_h(g, kb, ready, n):
                eng.wait_ge(ready, n)
                wait(eng, S["ht_cp"], kb + g.t - 1)
                for j in range(2):
                    m = eng.transpose(ps_t[g.b][:, j * P:(j + 1) * P], h[:, g.b, j * D:(j + 1) * D], ident[:, :])
                m.then_inc(S["tr_done"], 1)

            def dense(g, kb, w_g, w_u, width):
                eng.wait_ge(S["ht_cp"], kb + g.t + 1)
                wait(eng, S["g_cp"], kb + g.t - 1)
                if w_u is not None:
                    wait(eng, S["u_cp"], kb + g.t - 1)
                for j in range(2):
                    m = eng.matmul(ps_g[g.b][:, j * TILE:j * TILE + width], h_t[:, g.b, j * P:(j + 1) * P], w_g,
                                   start=True, stop=True)
                    if w_u is not None:
                        m = eng.matmul(ps_u[g.b][:, j * TILE:j * TILE + D], h_t[:, g.b, j * P:(j + 1) * P], w_u,
                                       start=True, stop=True)
                m.then_inc(S["dense_done"], 1)

            def phase0(s):
                o = s.at(-1)
                if o.there:
                    turn_h(o, 0, S["h_a"], s.t)
                if s.there:
                    placing(s)
                if o.there:
                    dense(o, 0, wcat[:, 0, 0:D], wcat[:, 0, D:2 * D], D)
            steps(eng, 2, phase0)

            for ph in range(1, LAYERS + 1):
                kb = ph * NG
                ka = (ph - 1) * NG

                def phase(s):
                    if s.there:
                        eng.wait_ge(S["mask_done"], ka + s.t + 1)
                        wait(eng, S["tsum_v"], ka + s.t - 1)
                        for w, j, m0 in ((0, 0, 0), (1, 0, 1), (1, 1, 2), (2, 1, 3)):
                            if m0 != 2:
                                eng.wait_ge(row_ld[s.r][w], 16 * (ka // RING + s.uses(RING) + 1))
                            m = eng.matmul(ps_agg[s.b][:, j * TILE:j * TILE + D + 1],
                                           mask[:, s.b, m0 * P:(m0 + 1) * P], rows[:, s.r, w, 0:D + 1],
                                           start=(m0 % 2 == 0), stop=(m0 % 2 == 1))
                        m.then_inc(S["agg_done"], 1)
                    o = s.at(-1 if ph < LAYERS else -2)
                    if o.there:
                        if ph < LAYERS:
                            turn_h(o, kb, S["h_v"], ka + o.t + 1)
                            dense(o, kb, wcat[:, ph, 0:D], wcat[:, ph, D:2 * D], D)
                        else:
                            turn_h(o, kb, S["h_a"], NG + o.t + 1)
                            dense(o, kb, wg[:, :], None, D + 2)
                steps(eng, 3 if ph == LAYERS else 2, phase)

            eng.wait_ge(S["g_cp"], (LAYERS + 1) * NG)
            eng.wait_ge(S["tsum_v"], LAYERS * NG)
            eng.wait_ge(S["ident_bv"], 1)

            def phase_c(s):
                if s.there:
                    eng.wait_ge(S["cut_v"], s.t + 1)
                    wait(eng, S["z_a"], s.t - 1)
                    for w, j, m0 in ((0, 0, 0), (1, 0, 1), (1, 1, 2), (2, 1, 3)):
                        if m0 != 2:
                            eng.wait_ge(row_ld[s.r][w], 16 * (LAYERS * NG // RING + s.uses(RING) + 1))
                        to = ps_z[s.b][:, m0 * P:(m0 + 1) * P]
                        eng.matmul(to, rows[:, s.r, w, D:D + 1].to_broadcast([P, P]), ident[:, :],
                                   start=True, stop=False)
                        m = eng.matmul(to, cut[:, s.b, m0 * P:(m0 + 1) * P], ident_b[:, :], start=False, stop=True)
                    m.then_inc(S["zm_done"], 1)
                o = s.at(-2)
                if o.there:
                    eng.wait_ge(S["ex_a"], o.t + 1)
                    wait(eng, S["pt_cp"], o.t - 1)
                    for j in range(2):
                        for w in range(2):
                            m = eng.transpose(ps_pt[o.b][:, (2 * j + w) * P:(2 * j + w + 1) * P],
                                              prob[:, o.b, j, w * P:(w + 1) * P], ident[:, :])
                    m.then_inc(S["pt_done"], 1)
                    eng.wait_ge(S["pt_cp"], o.t + 1)
                    wait(eng, S["acc_v"], o.t - 1)
                    for j in range(2):
                        for w in range(2):
                            m = eng.matmul(ps_o[o.b][:, j * D:(j + 1) * D], prob_t[:, o.b, j, w * P:(w + 1) * P],
                                           rows[:, o.r, j + w, 0:D], start=(w == 0), stop=(w == 1))
                    m.then_inc(S["pv_done"], 1)
            steps(eng, 2, phase_c)

        def vector_program(eng):
            eng.memset(pad[:, :], BEYOND)
            eng.memset(d_nxt[:, :], N).then_inc(S["const_v"], 1)
            eng.memset(ones[:, :], 1.0).then_inc(S["const_v"], 1)
            eng.memset(eps[:, :], 1e-5).then_inc(S["const_v"], 1)
            eng.memset(stat[:, :], 0.0).then_inc(S["const_v"], 1)
            eng.wait_ge(S["const_g"], 5)
            seq = [0]

            def op(ins):
                seq[0] += 1
                ins.then_inc(S["prep_seq"], 1)
                eng.wait_ge(S["prep_seq"], seq[0])
            op(eng.tensor_copy(iota[:, :], iota_i[:, :]))
            op(eng.tensor_copy(part[:, :], part_i[:, :]))
            op(eng.tensor_scalar(iota_c[:, :], iota[:, 0:NW * P], -128.0, None, ALU.add))
            op(eng.tensor_scalar(iota_b[:, :], iota[:, 0:TILE], 0.0, None, ALU.add))
            eng.tensor_copy(ident_b[:, :], ident[:, :]).then_inc(S["ident_bv"], 1)
            op(eng.tensor_scalar(thr[:, 0:1], part[:, 0:1], float(TILE), None, ALU.mult))
            op(eng.tensor_scalar(thr[:, 1:2], part[:, 0:1], float(HALF), float(TILE), ALU.add, ALU.mult))
            eng.wait_ge(S["zrow"], 1)
            eng.memset(rows[:, :, :, D:D + 1], 1.0).then_inc(S["zrow"], 1)

            eng.wait_ge(S["nat_ld"], 32)
            op(eng.tensor_scalar(first[:, :], ones[0:NAT_P, :], d_nat[:, 0:1], None, ALU.mult))
            eng.sem_inc(S["prep_ld"], 1)
            eng.wait_ge(S["nxt_ld"], 32)
            op(eng.tensor_tensor(cmp_n[:, :], d_nat[:, :], d_nxt[:, :], ALU.is_gt))
            op(eng.tensor_reduce(stat[0:NAT_P, 0:1], cmp_n[:, :], AX.X, ALU.add))
            op(eng.tensor_tensor(cmp_n[:, :], d_nat[:, :], d_nxt[:, :], ALU.not_equal))
            op(eng.tensor_reduce(stat[0:NAT_P, 1:2], cmp_n[:, :], AX.X, ALU.add))
            op(eng.tensor_tensor(cmp_m[:, :], s_nat[:, :], d_nat[:, :], ALU.not_equal))
            op(eng.tensor_tensor(cmp_m[:, :], cmp_m[:, :], cmp_n[:, :], ALU.mult))
            op(eng.tensor_reduce(stat[0:NAT_P, 2:3], cmp_m[:, :], AX.X, ALU.add))

            eng.wait_ge(S["first_ps"], 1)
            for q in range(2):
                op(eng.tensor_scalar(cmp_n[0:HALF, 0:NAT_P], bank[7][0:HALF, 0:NAT_P], thr[0:HALF, q:q + 1], None,
                                     ALU.is_lt))
                op(eng.tensor_reduce(row_c[:, q:q + 1], cmp_n[0:HALF, 0:NAT_P], AX.X, ALU.add))
            op(eng.tensor_scalar(row_c[:, :], row_c[:, :], -1.0, 0.0, ALU.add, ALU.max))
            op(eng.tensor_copy(row_i[:, :], row_c[:, :]))
            eng.sem_inc(S["prep_v"], 1)
            eng.wait_ge(S["row_ld"], 32)
            for q in range(2):
                op(eng.tensor_scalar(cmp_n[0:HALF, :], row_d[:, q, :], thr[0:HALF, q:q + 1], None, ALU.is_lt))
                op(eng.tensor_reduce(in_row[:, q:q + 1], cmp_n[0:HALF, :], AX.X, ALU.add))
            op(eng.scalar_tensor_tensor(e_first[:, :], row_c[:, :], float(NAT), in_row[:, :], ALU.mult, ALU.add))
            op(eng.tensor_copy(start_i[:, :], e_first[:, :]))
            eng.sem_inc(S["prep_v"], 1)
            eng.wait_ge(S["run_ld"], 64)
            for q in range(2):
                if q == 1:
                    eng.wait_ge(S["prep_p"], 4)
                drel = qty[:, 3, :]
                op(eng.tensor_tensor(w_valid[:, :], run_d[:, q, 0:RUN], run_d[:, q, 1:RUN + 1], ALU.is_equal))
                op(eng.tensor_scalar(drel, run_d[:, q, 0:RUN], thr[0:HALF, q:q + 1], None, ALU.subtract))
                op(eng.scalar_tensor_tensor(w_valid[:, :], drel, 0.0, w_valid[:, :], ALU.is_ge, ALU.mult))
                op(eng.scalar_tensor_tensor(w_valid[:, :], drel, float(TILE), w_valid[:, :], ALU.is_lt, ALU.mult))
                op(eng.tensor_reduce(stat[0:HALF, 3 + q:4 + q], w_valid[:, :], AX.X, ALU.add))
                op(eng.scalar_tensor_tensor(w_a[:, :], iota[0:HALF, :], float(OFF), drel, ALU.add, ALU.subtract))
                op(eng.tensor_scalar(w_b[:, :], drel, float(P), float(P), ALU.is_ge, ALU.mult))
                op(eng.tensor_tensor(w_b[:, :], w_a[:, :], w_b[:, :], ALU.subtract))
                op(eng.scalar_tensor_tensor(qty[:, 1, :], w_b[:, :], 0.0, w_valid[:, :], ALU.is_lt, ALU.mult))
                op(eng.scalar_tensor_tensor(qty[:, 2, :], w_b[:, :], float(TILE), w_valid[:, :], ALU.is_ge, ALU.mult))
                op(eng.tensor_tensor(qty[:, 1, :], qty[:, 1, :], qty[:, 2, :], ALU.add))
                op(eng.tensor_reduce(stat[0:HALF, 5 + q:6 + q], qty[:, 1, :], AX.X, ALU.add))
                for c in range(CH):
                    cc = slice(c * P, (c + 1) * P)
                    op(eng.tensor_scalar(w_b[:, cc], w_a[:, cc], float(-BAND[c] * P), None, ALU.add))
                op(eng.scalar_tensor_tensor(qty[:, 1, :], w_b[:, :], 0.0, w_valid[:, :], ALU.is_lt, ALU.mult))
                op(eng.scalar_tensor_tensor(qty[:, 2, :], w_b[:, :], float(TILE), w_valid[:, :], ALU.is_ge, ALU.mult))
                op(eng.tensor_tensor(qty[:, 1, :], qty[:, 1, :], qty[:, 2, :], ALU.add))
                op(eng.tensor_reduce(stat[0:HALF, 7:8] if q else extra[:, :], qty[:, 1, :], AX.X, ALU.add))
                if q:
                    op(eng.tensor_tensor(stat[0:HALF, 7:8], stat[0:HALF, 7:8], extra[:, :], ALU.add))
                op(eng.scalar_tensor_tensor(w_a[:, :], w_a[:, :], -128.0 - NOWHERE, w_valid[:, :], ALU.add, ALU.mult))
                op(eng.tensor_scalar(qty[:, 0, :], w_a[:, :], NOWHERE, None, ALU.add))
                op(eng.tensor_scalar(drel, drel, 1.0, None, ALU.add))
                op(eng.tensor_scalar(w_int[:, 0, :], run_s[:, q, 0:RUN], 8, None, ALU.logical_shift_right))
                op(eng.tensor_scalar(w_int[:, 1, :], run_s[:, q, 0:RUN], 255, None, ALU.bitwise_and))
                op(eng.tensor_copy(qty[:, 1:3, :], w_int[:, :, :]))
                eng.sem_inc(S["prep_v"], 1)
            eng.sem_inc(S["flag_v"], 1)

            eng.wait_ge(S["flag_ps"], 1)
            op(eng.tensor_copy(stat_sb[:, :], bank[1][0:1, 0:8]))
            op(eng.tensor_tensor(flag_f[:, 0:1], stat_sb[:, 0:1], stat_sb[:, 2:3], ALU.add))
            op(eng.tensor_tensor(flag_f[:, 1:2], stat_sb[:, 5:6], stat_sb[:, 6:7], ALU.add))
            op(eng.tensor_tensor(flag_f[:, 0:1], flag_f[:, 0:1], flag_f[:, 1:2], ALU.add))
            op(eng.tensor_tensor(flag_f[:, 0:1], flag_f[:, 0:1], stat_sb[:, 7:8], ALU.add))
            op(eng.tensor_scalar(flag_f[:, 0:1], flag_f[:, 0:1], 0.0, None, ALU.is_equal))
            op(eng.tensor_scalar(flag_f[:, 1:2], stat_sb[:, 1:2], float(N), None, ALU.is_equal))
            op(eng.tensor_tensor(flag_f[:, 2:3], stat_sb[:, 3:4], stat_sb[:, 4:5], ALU.add))
            op(eng.tensor_scalar(flag_f[:, 2:3], flag_f[:, 2:3], float(E - N), None, ALU.is_equal))
            op(eng.tensor_tensor(flag_f[:, 0:1], flag_f[:, 0:1], flag_f[:, 1:2], ALU.mult))
            op(eng.tensor_tensor(flag[:, :], flag_f[:, 0:1], flag_f[:, 2:3], ALU.mult))
            eng.sem_inc(S["flag_rdy"], 1)
            ok = eng.value_load(flag[0:1, 0:1], min_val=0, max_val=1)
            eng.wait_ge(S["wt_ld"], 16 * 13)
            with eng.If(ok):
                fast_vector(eng, op)
            with eng.Else():
                general_vector(eng)

        def fast_vector(eng, op):
            eng.wait_ge(S["pl_cp"], 8)

            def place_mask(s):
                wait(eng, S["pl_ps"], s.t - 1)
                for c in range(CH):
                    m = eng.tensor_scalar(cmask[:, s.b, c, :], iota_c[:, BAND[c] * P:BAND[c] * P + TILE],
                                          place[:, bass.ds(s.t, 1), c:c + 1].rearrange("p t c -> p (t c)"),
                                          None, ALU.is_equal)
                m.then_inc(S["cm_done"], 1)

            def stats(g, k, tile):
                for j in range(2):
                    m = eng.bn_stats(bst[:, j, :], tile[:, g.b, j, :])
                m.then_inc(S["bn_v"], 1)
                eng.wait_ge(S["bn_v"], k + 1)
                if g.i is not None:
                    eng.sem_inc(S["turn_v"], 1)
                for j in range(2):
                    m = eng.bn_aggr(mv[:, g.b, j, :], bst[:, j, :])
                m.then_inc(S["ln_v"], 1)

            def scale(g, k):
                eng.wait_ge(S["ln_a"], k + 1)
                wait(eng, S["h_a"], k - 1)
                eng.reciprocal(rstd[:, g.b, :], std[:, g.b, :]).then_inc(S["rs_v"], 1)
                eng.wait_ge(S["rs_v"], k + 1)
                eng.scalar_tensor_tensor(nmr[:, g.b, :], mv[:, g.b, :, 0], -1.0, rstd[:, g.b, :], ALU.mult,
                                         ALU.mult).then_inc(S["nmr_v"], 1)

            def u_copy(g, kb, layer):
                eng.wait_ge(S["dense_done"], kb + g.t + 1)
                wait(eng, S[f"st{g.b}"], 16 * (kb // 2 + g.uses(2)))
                eng.tensor_tensor(gu[:, g.b, :, D:2 * D], pair(ps_u[g.b], D, TILE),
                                  b_bc[:, layer, :].unsqueeze(1).to_broadcast([P, 2, D]), ALU.add
                                  ).then_inc(S["u_cp"], 1)

            def phase0(s):
                if s.at(-1).there:
                    scale(s.at(-1), s.t - 1)
                if s.there:
                    place_mask(s)
                if s.at(-2).there:
                    u_copy(s.at(-2), 0, 0)
                if s.there:
                    eng.wait_ge(S[f"x_ld{s.b}"], 16 * (s.uses(2) + 1))
                    stats(s, s.t, xin)
            steps(eng, 2, phase0)

            eng.wait_ge(S["prep_end"], NG)
            pv = placed[:, :, :, :].rearrange("p t w v -> p (t w) v")
            idx_f = idx[:, :, :].rearrange("p t w -> p (t w)")
            dc_f = dcol[:, :, :].rearrange("p t w -> p (t w)")
            op(eng.tensor_scalar(dc_f, pv[:, :, 2], -1.0, None, ALU.add))
            op(eng.tensor_scalar(empty[:, :], dc_f, 0.0, FAR, ALU.is_lt, ALU.mult))
            op(eng.scalar_tensor_tensor(empty[:, :], pv[:, :, 1], 2.0, empty[:, :], ALU.mult, ALU.add))
            op(eng.scalar_tensor_tensor(idx_f, pv[:, :, 0], 512.0, empty[:, :], ALU.mult, ALU.add))
            eng.sem_inc(S["idx_g"], 1)

            def masks(g, to, io, done, k, value):
                for w, a, b, at in ((0, 0, P, 0), (1, 0, TILE, P), (2, P, TILE, 3 * P)):
                    node = dcol[:, bass.ds(g.t, 1), w:w + 1].rearrange("p t w -> p (t w)")
                    if value is None:
                        m = eng.tensor_scalar(to[:, g.b, at:at + b - a], io[:, a:b], node, None, ALU.is_equal)
                    else:
                        m = eng.tensor_scalar(to[:, g.b, at:at + b - a], io[:, a:b], node, value, ALU.not_equal,
                                              ALU.mult)
                m.then_inc(S[done], 1)

            for ph in range(1, LAYERS + 1):
                ka = (ph - 1) * NG
                kb = ph * NG

                def phase(s):
                    for g in [s, s.at(1)] if s.i is None and s.t == 0 else [s.at(1)]:
                        if g.there:
                            wait(eng, S["agg_done"], ka + g.t - 1)
                            masks(g, mask, iota, "mask_done", ka, None)
                    if ph < LAYERS and s.at(-2).there:
                        u_copy(s.at(-2), kb, ph)
                    if ph == LAYERS and s.at(-1).there:
                        scale(s.at(-1), NG + s.t - 1)
                    if not s.there:
                        return
                    k = ka + s.t
                    eng.wait_ge(S["agg_done"], k + 1)
                    acc_ps = pair(ps_agg[s.b], D + 1, TILE)
                    eng.tensor_scalar(cnt[:, :], acc_ps[:, :, D], 1.0, None, ALU.add).then_inc(S["cnt_v"], 1)
                    eng.wait_ge(S[f"own_ld{s.b}"], 16 * (ka // 2 + s.uses(2) + 1))
                    eng.tensor_tensor(tsum[:, :, :], acc_ps[:, :, 0:D], own[:, s.b, :, 0:D], ALU.add
                                      ).then_inc(S["tsum_v"], 1)
                    eng.wait_ge(S["cnt_v"], k + 1)
                    eng.reciprocal(inv[:, :], cnt[:, :]).then_inc(S["inv_v"], 1)
                    eng.wait_ge(S["tsum_v"], k + 1)
                    eng.wait_ge(S["inv_v"], k + 1)
                    for j in range(2):
                        m = eng.scalar_tensor_tensor(zed[:, j, :], tsum[:, j, :], inv[:, j:j + 1],
                                                     own[:, s.b, j, D:2 * D], ALU.mult, ALU.add)
                    m.then_inc(S["z_v"], 1)
                    eng.wait_ge(S["z_v"], k + 1)
                    if ph < LAYERS:
                        to = h[:, s.b, :].rearrange("p (j d) -> p j d", j=2)
                        eng.wait_ge(S["tr_done"], kb + s.t - 1)
                    else:
                        to = tsum[:, :, :]
                    eng.scalar_tensor_tensor(to, zed[:, :, :], 0.01, zed[:, :, :], ALU.mult, ALU.max
                                             ).then_inc(S["h_v"], 1)
                    if ph == LAYERS:
                        eng.wait_ge(S["h_v"], k + 1)
                        eng.wait_ge(S[f"x_ld{s.b}"], 16 * (NG // 2 + s.uses(2) + 1))
                        wait(eng, S["h_a"], NG + s.t - 1)
                        eng.tensor_tensor(x1[:, s.b, :, :], tsum[:, :, :], xin[:, s.b, :, :], ALU.add
                                          ).then_inc(S["x1_v"], 1)
                        eng.wait_ge(S["x1_v"], s.t + 1)
                        stats(s, NG + s.t, x1)
                        wait(eng, S[f"stx{s.b}"], 16 * s.uses(2))
                        eng.tensor_tensor(x1b[:, s.b, :, :], x1[:, s.b, :, :],
                                          b_bc[:, LAYERS, :].unsqueeze(1).to_broadcast([P, 2, D]), ALU.add
                                          ).then_inc(S["x1b_v"], 1)
                steps(eng, 3 if ph == LAYERS else 2, phase)

            def phase_c(s):
                for g in [s, s.at(1)] if s.i is None and s.t == 0 else [s.at(1)]:
                    if g.there:
                        wait(eng, S["zm_done"], g.t - 1)
                        masks(g, cut, iota_b, "cut_v", 0, -BIG)
                o = s.at(-2)
                if o.there:
                    k = o.t
                    eng.wait_ge(S["ex_a"], k + 1)
                    eng.tensor_scalar(ptwo[:, :], pself[:, o.b, :], 2.0, None, ALU.mult).then_inc(S["cd_v"], 1)
                    eng.wait_ge(S["cd_v"], 3 * k + 1)
                    eng.scalar_tensor_tensor(dsum[:, :], den[:, o.b, :], 1e-16, ptwo[:, :], ALU.add, ALU.add
                                             ).then_inc(S["cd_v"], 1)
                    eng.wait_ge(S["pv_done"], k + 1)
                    for j in range(2):
                        m = eng.scalar_tensor_tensor(acc[:, j, :], own_c[:, o.r, j, 0:D], ptwo[:, j:j + 1],
                                                     ps_o[o.b][:, j * D:(j + 1) * D], ALU.mult, ALU.add)
                    m.then_inc(S["acc_v"], 1)
                    eng.wait_ge(S["cd_v"], 3 * k + 2)
                    eng.reciprocal(rden[:, :], dsum[:, :]).then_inc(S["cd_v"], 1)
                    eng.wait_ge(S["cd_v"], 3 * k + 3)
                    eng.wait_ge(S["acc_v"], k + 1)
                    wait(eng, S[f"out{o.b}"], 16 * o.uses(2))
                    for j in range(2):
                        m = eng.scalar_tensor_tensor(res[:, o.b, j, :], acc[:, j, :], rden[:, j:j + 1],
                                                     x1c[:, o.r, j, :], ALU.mult, ALU.add)
                    m.then_inc(S["res_v"], 1)
                if s.there:
                    k = s.t
                    oc = own_c[:, s.r, :, :]
                    eng.wait_ge(S[f"cl{s.r}"], 32 * (s.uses(RING) + 1))
                    eng.tensor_tensor(zs[:, 0, :], oc[:, :, D], oc[:, :, D + 1], ALU.add).then_inc(S["cs_v"], 1)
                    eng.wait_ge(S["z_a"], k + 1)
                    eng.tensor_reduce(mx[:, :], zb[:, s.b, :, :], AX.X, ALU.max).then_inc(S["cs_v"], 1)
                    wait(eng, S["ex_a"], k - 1)
                    eng.scalar_tensor_tensor(lr[:, s.b, :, :], zb[:, s.b, :, :], 0.2, zb[:, s.b, :, :], ALU.mult,
                                             ALU.max).then_inc(S["lr_v"], 1)
                    eng.wait_ge(S["cs_v"], 4 * k + 2)
                    eng.tensor_tensor(zs[:, 1, :], mx[:, :], zs[:, 0, :], ALU.max).then_inc(S["cs_v"], 1)
                    eng.wait_ge(S["cs_v"], 4 * k + 3)
                    eng.scalar_tensor_tensor(ls[:, :, :], zs[:, :, :], 0.2, zs[:, :, :], ALU.mult, ALU.max
                                             ).then_inc(S["cs_v"], 1)
                    eng.wait_ge(S["cs_v"], 4 * k + 4)
                    eng.tensor_scalar(nm[:, s.b, :], ls[:, 1, :], -1.0, None, ALU.mult)
                    eng.tensor_tensor(dself[:, s.b, :], ls[:, 0, :], ls[:, 1, :], ALU.subtract
                                      ).then_inc(S["nm_v"], 1)
            steps(eng, 2, phase_c)

        def tile_of(a, t, w=None):
            rows_ = a[bass.ds(t * P, P), :] if not isinstance(t, int) else a[t * P:(t + 1) * P, :]
            return rows_ if w is None else rows_[:, 0:w]

        def node_loop(eng, body):
            with eng.Fori(0, NT - 1) as t:
                body(t, P)
            body(NT - 1, TAIL_T)

        def general_sync(eng):
            vec = {0: 4, 1: 5, 2: 5, 3: 12, 4: 12}
            v_base = 0
            eng.wait_ge(S["low_g"], 11)
            for ph in range(LAYERS + 2):
                ld, st = Count(S[f"gn_ld{ph}"]), Count(S[f"gn_st{ph}"])
                if ph:
                    eng.wait_ge(S[f"ge_st{ph - 1}"], 16 * NE)
                loads = {0: 1, 3: 3, 4: 3}.get(ph, 2)
                stores = {0: 2, 3: 3, 4: 1}.get(ph, 2)

                def body(t, n):
                    ld.begin(16 * loads, t)
                    st.begin(16 * stores, t)
                    if ph in (0, 3):
                        ld.inc(eng.dma_start(g_x[0:n, :], x[bass.ds(t * P, n), :]), 16)
                    if ph:
                        ld.inc(eng.dma_start(g_sum[:, :], tile_of(gen_s, t)), 16)
                        ld.inc(eng.dma_start(g_row[:, :], tile_of(gen_h if ph <= 3 else tab_c, t)), 16)
                    if ph == 4:
                        ld.inc(eng.dma_start(g_x1b[:, :], tile_of(x1_d, t)), 16)
                    if ph == 0:
                        eng.wait_ge(S["gn_a"], 2 * t + 2)
                    else:
                        eng.wait_ge(S["gn_v"], t * vec[ph] + (v_base + vec[ph]))
                    if ph <= 2:
                        st.inc(eng.dma_start(tile_of(gen_h, t), g_node[:, :]), 16)
                    if ph == 3:
                        st.inc(eng.dma_start(tile_of(tab_c, t), g_node[:, :]), 16)
                        st.inc(eng.dma_start(tile_of(x1_d, t), g_x1b[:, :]), 16)
                    if ph <= 3:
                        st.inc(eng.dma_start(tile_of(gen_s, t), g_init[:, int(ph == 3), :]), 16)
                    else:
                        st.inc(eng.dma_start(out[bass.ds(t * P, n), :], g_out[0:n, :]), 16)
                    eng.wait_ge(S[f"gn_st{ph}"], st.now())
                    eng.sem_inc(S["turn_s"], 1)
                node_loop(eng, body)
                ld.end(NT)
                st.end(NT)
                v_base += vec[ph] * NT

        def general_gpsimd(eng):
            stored = {0: 32, 1: 32, 2: 32, 3: 48}
            v_base = 0
            for ph in range(LAYERS + 1):
                ld, rw, st = Count(S[f"ge_ld{ph}"]), Count(S[f"ge_rows{ph}"]), Count(S[f"ge_st{ph}"])
                eng.wait_ge(S[f"gn_st{ph}"], stored[ph] * NT)
                table = gen_h if ph < LAYERS else tab_c[0:NT * P, :]
                k = 3 if ph == LAYERS else 2
                v_n = 7 + 1 if ph < LAYERS else 18
                with eng.Fori(0, NE) as i:
                    ld.begin(32, i)
                    rw.begin(16 * k, i)
                    st.begin(16, i)
                    for c in range(2):
                        ld.inc(eng.dma_start(se[:, c:c + 1],
                                             edges[c][bass.ds(i * P, P)].rearrange("(p a) -> p a", a=1)), 16)
                    eng.wait_ge(S[f"ge_ld{ph}"], ld.now())
                    eng.sem_inc(S["turn"], 1)
                    for to, frm, c in ((g_row, table, 0), (g_sum, gen_s, 1), (g_dst, table, 1))[:k]:
                        rw.inc(eng.indirect_dma_start(out=to[:, :], out_offset=None, in_=frm,
                                                      in_offset=bass.IndirectOffsetOnAxis(ap=se[:, c:c + 1], axis=0),
                                                      bounds_check=N - 1, oob_is_err=False), 16)
                    eng.wait_ge(S["ge_v"], i * v_n + (v_base + v_n))
                    eng.sem_inc(S["turn"], 1)
                    st.inc(eng.indirect_dma_start(out=gen_s, out_offset=bass.IndirectOffsetOnAxis(ap=w_idx[:, :], axis=0),
                                                  in_=g_new[:, :], in_offset=None,
                                                  bounds_check=N - 1, oob_is_err=False), 16)
                    eng.wait_ge(S[f"ge_st{ph}"], st.now())
                    eng.sem_inc(S["turn"], 1)
                for c in (ld, rw, st):
                    c.end(NE)
                v_base += v_n * NE

        def general_scalar(eng):
            nd, v, m = Count(S["gn_a"]), Count(S["gn_v"]), Count(S["gn_m"])

            def after(sem, n):
                eng.wait_ge(sem, n)

            v_base, m_base, a_base = 0, 0, 0
            ge_v_base = ge_m_base = 0
            for ph in range(LAYERS + 2):
                vn = {0: 4, 1: 5, 2: 5, 3: 12, 4: 12}[ph]
                mn = {0: 0, 1: 2, 2: 2, 3: 4, 4: 0}[ph]
                an = {0: 2, 1: 1, 2: 1, 3: 4, 4: 1}[ph]
                if ph == LAYERS + 1:
                    with eng.Fori(0, NE) as i:
                        eng.wait_ge(S["ge_v"], i * 18 + (8 * NE * LAYERS + 16))
                        eng.activation(g1[:, 6:7], g1[:, 5:6], ACT.Exp).then_inc(S["ge_a"], 1)
                        eng.activation(same[:, :], tmp[:, :], ACT.Exp, bias=g1[:, 4:5], accum_out=g1[:, 7:8]
                                       ).then_inc(S["ge_a"], 1)
                        eng.wait_ge(S["ge_m"], i * 4 + (2 * NE * LAYERS + 3))
                        eng.activation(wide[:, :], bank[2][:, 0:P], ACT.Copy).then_inc(S["ge_a"], 1)

                def body(t, n):
                    def a(ins):
                        ins.then_inc(S["gn_a"], 1)

                    def v_at(n):
                        eng.wait_ge(S["gn_v"], t * vn + (v_base + n))

                    def m_at(n):
                        eng.wait_ge(S["gn_m"], t * mn + (m_base + n))
                    if ph == 0:
                        v_at(2)
                        a(eng.activation(g1[:, 0:1], g_mv[:, 1:2], ACT.Sqrt, bias=eps[:, 0:1]))
                        v_at(4)
                        a(eng.activation(g_node[:, 0:D], g_x[:, :], ACT.Relu, bias=g1[:, 2:3], scale=g1[:, 1:2]))
                    elif ph <= LAYERS:
                        m_at(1)
                        a(eng.activation(g_t[:, :], bank[0][:, 0:2 * P], ACT.Copy))
                        if ph == LAYERS:
                            v_at(9)
                            a(eng.activation(g1[:, 0:1], g_mv[:, 1:2], ACT.Sqrt, bias=eps[:, 0:1]))
                            v_at(11)
                            a(eng.activation(g_h[:, :], g_x1[:, :], ACT.Relu, bias=g1[:, 2:3], scale=g1[:, 1:2]))
                            m_at(3)
                            a(eng.activation(g_t[:, 0:P], bank[0][:, 0:P], ACT.Copy))
                    else:
                        v_at(5)
                        a(eng.activation(g1[:, 4:6], g1[:, 2:4], ACT.Exp))
                node_loop(eng, body)
                v_base += vn * NT
                m_base += mn * NT

        def general_tensor(eng):
            v_base = a_base = 0
            for ph in range(LAYERS + 2):
                vn = {0: 4, 1: 5, 2: 5, 3: 12, 4: 12}[ph]
                an = {0: 2, 1: 1, 2: 1, 3: 4, 4: 1}[ph]
                if 1 <= ph <= LAYERS:
                    kb = NE * (ph - 1)
                    with eng.Fori(0, NE) as i:
                        eng.wait_ge(S["ge_v"], i * 8 + (8 * kb + 2))
                        eng.transpose(bank[0][:, 0:P], wide[:, :], ident[:, :]).then_inc(S["ge_m"], 1)
                        eng.wait_ge(S["ge_v"], i * 8 + (8 * kb + 3))
                        eng.wait_ge(S[f"ge_rows{ph - 1}"], i * 32 + 32)
                        eng.matmul(bank[1][:, 0:D + 1], same[:, :], g_row[:, 0:D + 1], start=True, stop=True
                                   ).then_inc(S["ge_m"], 1)
                if ph == LAYERS + 1:
                    vb, ab, mb = 8 * NE * LAYERS, 0, 0
                    with eng.Fori(0, NE) as i:
                        eng.wait_ge(S["ge_v"], i * 18 + (vb + 2))
                        eng.transpose(bank[0][:, 0:P], wide[:, :], ident[:, :]).then_inc(S["ge_m"], 1)
                        eng.wait_ge(S["ge_v"], i * 18 + (vb + 10))
                        eng.transpose(bank[1][:, 0:P], tmp[:, :], ident[:, :]).then_inc(S["ge_m"], 1)
                        eng.wait_ge(S["ge_a"], i * 3 + 2)
                        eng.transpose(bank[2][:, 0:P], same[:, :], ident[:, :]).then_inc(S["ge_m"], 1)
                        eng.wait_ge(S["ge_a"], i * 3 + 3)
                        eng.matmul(bank[3][:, 0:D], wide[:, :], g_row[:, 0:D], start=True, stop=True
                                   ).then_inc(S["ge_m"], 1)

                def body(t, n):
                    if ph in (1, 2, 3):
                        eng.wait_ge(S["gn_v"], t * vn + (v_base + 3))
                        eng.transpose(bank[0][:, 0:P], g_h[:, :], ident[:, :])
                        eng.transpose(bank[0][:, P:2 * P], g_row[:, 0:D], ident[:, :]).then_inc(S["gn_m"], 1)
                        eng.wait_ge(S["gn_a"], t * an + (a_base + 1))
                        eng.matmul(bank[1][:, 0:D], g_t[:, 0:P], wcat[:, ph - 1, 0:D], start=True, stop=False)
                        eng.matmul(bank[1][:, 0:D], g_t[:, P:2 * P], wcat[:, ph - 1, D:2 * D], start=False, stop=True
                                   ).then_inc(S["gn_m"], 1)
                    if ph == 3:
                        eng.wait_ge(S["gn_a"], t * an + (a_base + 3))
                        eng.transpose(bank[0][:, 0:P], g_h[:, :], ident[:, :]).then_inc(S["gn_m"], 1)
                        eng.wait_ge(S["gn_a"], t * an + (a_base + 4))
                        eng.matmul(bank[2][:, 0:D + 2], g_t[:, 0:P], wg[:, :], start=True, stop=True
                                   ).then_inc(S["gn_m"], 1)
                if ph in (1, 2, 3):
                    node_loop(eng, body)
                v_base += vn * NT
                a_base += an * NT

        def general_vector(eng):
            ev, nv = Count(S["ge_v"]), Count(S["gn_v"])
            m_base = a_base = 0
            eng.wait_ge(S["low_g"], 11)

            def edge_ids(o, i, kb):
                eng.wait_ge(S[f"ge_ld{kb // NE}"], i * 32 + 32)
                o(eng.tensor_copy(df[:, :], se[:, 1:2]))
                o(eng.tensor_scalar(wide[:, :], ones[:, :], df[:, 0:1], None, ALU.mult))

            def first_of(o):
                o(eng.tensor_tensor(tmp[:, :], same[:, :], low[:, :], ALU.mult))
                o(eng.tensor_reduce(g1[:, 0:1], tmp[:, :], AX.X, ALU.max))
                o(eng.tensor_scalar(g1[:, 1:2], g1[:, 0:1], FAR, None, ALU.mult))
                o(eng.tensor_tensor(w_idx[:, :], g1[:, 1:2], df[:, :], ALU.add))

            def sums(ph):
                kb = NE * (ph - 1)
                with eng.Fori(0, NE) as i:
                    ev.begin(8, i)

                    def o(ins):
                        ev.inc(ins)
                        eng.wait_ge(S["ge_v"], ev.now())
                    edge_ids(o, i, kb)
                    eng.wait_ge(S["ge_m"], i * 2 + (2 * kb + 1))
                    o(eng.tensor_scalar(same[:, :], bank[0][:, 0:P], df[:, 0:1], None, ALU.is_equal))
                    first_of(o)
                    eng.wait_ge(S["ge_m"], i * 2 + (2 * kb + 2))
                    eng.wait_ge(S[f"ge_rows{ph - 1}"], i * 32 + 32)
                    o(eng.tensor_tensor(g_new[:, 0:D + 1], g_sum[:, 0:D + 1], bank[1][:, 0:D + 1], ALU.add))
                ev.end(NE)

            def attention_sums():
                kb = NE * LAYERS
                with eng.Fori(0, NE) as i:
                    ev.begin(18, i)

                    def o(ins):
                        ev.inc(ins)
                        eng.wait_ge(S["ge_v"], ev.now())
                    edge_ids(o, i, kb)
                    eng.wait_ge(S["ge_m"], i * 4 + (2 * kb + 1))
                    o(eng.tensor_scalar(same[:, :], bank[0][:, 0:P], df[:, 0:1], None, ALU.is_equal))
                    first_of(o)
                    eng.wait_ge(S[f"ge_rows{LAYERS}"], i * 48 + 48)
                    o(eng.tensor_tensor(g1[:, 0:1], g_row[:, D:D + 1], g_dst[:, D + 1:D + 2], ALU.add))
                    o(eng.scalar_tensor_tensor(g1[:, 1:2], g1[:, 0:1], 0.2, g1[:, 0:1], ALU.mult, ALU.max))
                    o(eng.tensor_scalar(tmp[:, :], ones[:, :], g1[:, 1:2], None, ALU.mult))
                    eng.wait_ge(S["ge_m"], i * 4 + (2 * kb + 2))
                    o(eng.tensor_scalar(wide[:, :], same[:, :], -1.0, BIG, ALU.add, ALU.mult))
                    o(eng.tensor_tensor(tmp[:, :], bank[1][:, 0:P], wide[:, :], ALU.add))
                    o(eng.tensor_reduce(g1[:, 2:3], tmp[:, :], AX.X, ALU.max))
                    o(eng.tensor_tensor(g_new[:, D + 1:D + 2], g1[:, 2:3], g_sum[:, D + 1:D + 2], ALU.max))
                    o(eng.tensor_scalar(g1[:, 4:5], g_new[:, D + 1:D + 2], -1.0, None, ALU.mult))
                    o(eng.tensor_tensor(g1[:, 5:6], g_sum[:, D + 1:D + 2], g_new[:, D + 1:D + 2], ALU.subtract))
                    eng.wait_ge(S["ge_a"], i * 3 + 2)
                    o(eng.scalar_tensor_tensor(g_new[:, D:D + 1], g_sum[:, D:D + 1], g1[:, 6:7], g1[:, 7:8],
                                               ALU.mult, ALU.add))
                    eng.wait_ge(S["ge_m"], i * 4 + (2 * kb + 4))
                    o(eng.scalar_tensor_tensor(g_new[:, 0:D], g_sum[:, 0:D], g1[:, 6:7], bank[3][:, 0:D],
                                               ALU.mult, ALU.add))
                ev.end(NE)

            for ph in range(LAYERS + 2):
                if 1 <= ph <= LAYERS:
                    sums(ph)
                if ph == LAYERS + 1:
                    attention_sums()
                vn = {0: 4, 1: 5, 2: 5, 3: 12, 4: 12}[ph]
                mn = {0: 0, 1: 2, 2: 2, 3: 4, 4: 0}[ph]
                an = {0: 2, 1: 1, 2: 1, 3: 4, 4: 1}[ph]
                ln = 16 * {0: 1, 3: 3, 4: 3}.get(ph, 2)

                def body(t, n):
                    nv.begin(vn, t)

                    def o(ins):
                        nv.inc(ins)
                        eng.wait_ge(S["gn_v"], nv.now())

                    def stats_of(tile):
                        o(eng.bn_stats(g_st[:, :], tile))
                        if n == P:
                            eng.sem_inc(S["turn_v"], 1)
                        o(eng.bn_aggr(g_mv[:, :], g_st[:, :]))

                    def scale_of(a_at):
                        eng.wait_ge(S["gn_a"], t * an + (a_base + a_at))
                        o(eng.reciprocal(g1[:, 1:2], g1[:, 0:1]))
                        o(eng.scalar_tensor_tensor(g1[:, 2:3], g_mv[:, 0:1], -1.0, g1[:, 1:2], ALU.mult, ALU.mult))
                    eng.wait_ge(S[f"gn_ld{ph}"], t * ln + ln)
                    if ph == 0:
                        stats_of(g_x[:, :])
                        scale_of(1)
                    elif ph <= LAYERS:
                        o(eng.tensor_scalar(g1[:, 0:1], g_sum[:, D:D + 1], 1.0, None, ALU.max))
                        o(eng.reciprocal(g1[:, 1:2], g1[:, 0:1]))
                        o(eng.tensor_scalar(g_h[:, :], g_sum[:, 0:D], g1[:, 1:2], None, ALU.mult))
                        eng.wait_ge(S["gn_m"], t * mn + (m_base + 2))
                        o(eng.tensor_tensor(tmp[:, :], bank[1][:, 0:D], b_bc[:, ph - 1, :], ALU.add))
                        to = g_node[:, 0:D] if ph < LAYERS else wide[:, :]
                        o(eng.scalar_tensor_tensor(to, tmp[:, :], 0.01, tmp[:, :], ALU.mult, ALU.max))
                        if ph == LAYERS:
                            o(eng.tensor_tensor(g_x1[:, :], wide[:, :], g_x[:, :], ALU.add))
                            o(eng.tensor_tensor(g_x1b[:, :], g_x1[:, :], b_bc[:, LAYERS, :], ALU.add))
                            stats_of(g_x1[:, :])
                            scale_of(2)
                            eng.wait_ge(S["gn_m"], t * mn + (m_base + 4))
                            o(eng.tensor_copy(g_node[:, 0:D + 2], bank[2][:, 0:D + 2]))
                    else:
                        o(eng.tensor_tensor(g1[:, 0:1], g_row[:, D:D + 1], g_row[:, D + 1:D + 2], ALU.add))
                        o(eng.scalar_tensor_tensor(g1[:, 1:2], g1[:, 0:1], 0.2, g1[:, 0:1], ALU.mult, ALU.max))
                        o(eng.tensor_tensor(g1[:, 0:1], g1[:, 1:2], g_sum[:, D + 1:D + 2], ALU.max))
                        o(eng.tensor_tensor(g1[:, 2:3], g_sum[:, D + 1:D + 2], g1[:, 0:1], ALU.subtract))
                        o(eng.tensor_tensor(g1[:, 3:4], g1[:, 1:2], g1[:, 0:1], ALU.subtract))
                        eng.wait_ge(S["gn_a"], t * an + (a_base + 1))
                        o(eng.tensor_scalar(g1[:, 6:7], g1[:, 5:6], 1e-16, None, ALU.add))
                        o(eng.scalar_tensor_tensor(g1[:, 7:8], g_sum[:, D:D + 1], g1[:, 4:5], g1[:, 6:7],
                                                   ALU.mult, ALU.add))
                        o(eng.reciprocal(g1[:, 0:1], g1[:, 7:8]))
                        o(eng.tensor_scalar(tmp[:, :], g_sum[:, 0:D], g1[:, 4:5], None, ALU.mult))
                        o(eng.scalar_tensor_tensor(wide[:, :], g_row[:, 0:D], g1[:, 5:6], tmp[:, :], ALU.mult, ALU.add))
                        o(eng.tensor_scalar(tmp[:, :], wide[:, :], g1[:, 0:1], None, ALU.mult))
                        o(eng.tensor_tensor(g_out[:, :], tmp[:, :], g_x1b[:, :], ALU.add))
                node_loop(eng, body)
                nv.end(NT)
                m_base += mn * NT
                a_base += an * NT

        block.sync(sync_program)
        block.gpsimd(gpsimd_program)
        block.scalar(scalar_program)
        block.tensor(tensor_program)
        block.vector(vector_program)

_INS = ['x', 'src', 'dst', 'L0_gnn_Wl1', 'L0_gnn_bl1', 'L0_gnn_Wr1', 'L0_gnn_Wlh', 'L0_gnn_blh', 'L0_gnn_Wrh',
        'L1_gnn_W', 'L1_gnn_att_src', 'L1_gnn_att_dst', 'L1_gnn_bias']


def kernel(**inputs):
    import numpy as _np
    import concourse.bacc as _bacc
    from concourse import mybir as _mybir
    from concourse.bass_utils import run_bass_kernel_spmd as _run

    nc = _bacc.Bacc("TRN2", target_bir_lowering=False, num_devices=1)
    arrays, args = {}, []
    for name in _INS:
        a = _np.ascontiguousarray(inputs[name])
        arrays[f"in_{name}"] = a
        args.append(nc.dram_tensor(f"in_{name}", a.shape, _mybir.dt.from_np(a.dtype), kind="ExternalInput").ap())
    args.append(nc.dram_tensor("out_0", (N, D), _mybir.dt.float32, kind="ExternalOutput").ap())
    build(nc, *args)
    return _run(nc, [arrays], core_ids=[0]).results[0]["out_0"]
```

```python
import concourse.bass as bass
from concourse import mybir
from contextlib import ExitStack

F32 = mybir.dt.float32
BF16 = mybir.dt.bfloat16
I32 = mybir.dt.int32
ALU = mybir.AluOpType
ACT = mybir.ActivationFunctionType
AX = mybir.AxisListType

P = 128
N = 50000
E = 100000
D = 128
TILE = 2 * P
NG = -(-N // TILE)
NPAD = NG * TILE
TAIL = N - (NG - 1) * TILE
BEYOND = 1 << 20
NW = 3
OFF = 56
CH = 5
RUN = CH * P
BAND = [0, 0, 1, 1, 1]
HALF = NG // 2
UNROLL = 8
RING = 4
DEEP = 8
NT = -(-N // P)
NE = -(-E // P)
TAIL_T = N - (NT - 1) * P
NAT_P, NAT = 125, 800
CW = 132
FAR = float(1 << 18)
NOWHERE = -1000.0
BIG = 2.0 ** 126
CUT = 2.0 ** 100
LAYERS = 3
EP = (E // (RUN + 1) + 2) * (RUN + 1)


class Step:

    def __init__(self, i, off):
        if i is not None and off < 0:
            i, off = i - 1, off + UNROLL
        self.i, self.off = i, off
        self.t = off if i is None else UNROLL * i + off
        self.b = off % 2
        self.r = off % RING
        self.q = off % DEEP
        self.there = i is not None or 0 <= off < NG
        self.last = i is None and off == NG - 1

    def at(self, d):
        return Step(self.i, self.off + d)

    def uses(self, ring):
        return self.off // ring if self.i is None else (UNROLL // ring) * self.i + self.off // ring


def steps(eng, late, body):
    for t in range(UNROLL):
        body(Step(None, t))
    with eng.Fori(1, NG // UNROLL) as i:
        for off in range(UNROLL):
            body(Step(i, off))
    for t in range(NG // UNROLL * UNROLL, NG + late):
        body(Step(None, t))


def ahead(s, d):
    return [s.at(k) for k in range(d + 1)] if s.i is None and s.t == 0 else [s.at(d)]


def in_phase(q):
    return NG // DEEP + (q < NG % DEEP)


def wait(eng, sem, value):
    if not isinstance(value, int) or value > 0:
        eng.wait_ge(sem, value)


class Count:

    def __init__(self, sem):
        self.sem, self.base, self.per, self.i, self.n = sem, 0, 0, 0, 0

    def begin(self, per, i):
        self.per, self.i, self.n = per, i, 0

    def inc(self, instruction, by=1):
        instruction.then_inc(self.sem, by)
        self.n += by

    def now(self):
        return self.at(self.n)

    def at(self, n):
        return self.i * self.per + (self.base + n)

    def end(self, steps):
        assert self.n == self.per, (self.n, self.per)
        self.base += self.per * steps


def build(nc, x, src, dst, wl1, bl1, wr1, wlh, blh, wrh, w_gat, att_s, att_d, bias, out):
    ctx = ExitStack()
    with ctx:
        def sb(name, shape, dt=F32):
            return ctx.enter_context(nc.sbuf_tensor(name, shape, dt))

        def sem(name):
            return ctx.enter_context(nc.semaphore(name))

        tab = [nc.dram_tensor(f"tab{i}", [2 * NPAD, D], F32).ap() for i in range(2)]
        gen_h = nc.dram_tensor("gen_h", [NT * P, CW], F32).ap()
        gen_s = nc.dram_tensor("gen_s", [NT * P, CW], F32).ap()
        edges = [nc.dram_tensor(f"edges{i}", [EP], I32).ap() for i in range(2)]
        tab_c = nc.dram_tensor("tab_c", [NPAD, CW], F32).ap()
        x1_d = nc.dram_tensor("x1_d", [NPAD, D], F32).ap()

        ident = sb("ident", [P, P])
        ones = sb("ones", [P, P])
        iota_i = sb("iota_i", [P, RUN], I32)
        iota = sb("iota", [P, RUN])
        iota_c = sb("iota_c", [P, NW * P], BF16)
        iota_b = sb("iota_b", [P, TILE], BF16)
        part_i = sb("part_i", [P, 2], I32)
        part = sb("part", [P, 2])
        thr = sb("thr", [P, 2])
        eps = sb("eps", [P, 1])

        w_raw = sb("w_raw", [P, 7, P])
        wcat = sb("wcat", [P, LAYERS, 2 * D])
        w_t = sb("w_t", [P, P])
        wg = sb("wg", [P, D + 2])
        att = sb("att", [P, 2])
        b_bc = sb("b_bc", [P, LAYERS + 1, D])

        d_nat = sb("d_nat", [NAT_P, NAT], I32)
        d_nxt = sb("d_nxt", [NAT_P, NAT], I32)
        s_nat = sb("s_nat", [NAT_P, NAT], I32)
        cmp_n = sb("cmp_n", [NAT_P, NAT])
        cmp_m = sb("cmp_m", [NAT_P, NAT])
        first = sb("first", [NAT_P, P])
        pad = sb("pad", [2, (EP - E) // 2], I32)
        row_d = sb("row_d", [HALF, 2, NAT], I32)
        row_i = sb("row_i", [HALF, 2], I32)
        row_c = sb("row_c", [HALF, 2])
        in_row = sb("in_row", [HALF, 2])
        e_first = sb("e_first", [HALF, 2])
        start_i = sb("start_i", [HALF, 2], I32)
        run_s = sb("run_s", [HALF, 2, RUN + 1], I32)
        run_d = sb("run_d", [HALF, 2, RUN + 1], I32)
        w_a = sb("w_a", [HALF, RUN])
        w_b = sb("w_b", [HALF, RUN])
        w_valid = sb("w_valid", [HALF, RUN])
        w_int = sb("w_int", [HALF, 2, RUN], I32)
        qty = sb("qty", [HALF, 4, RUN])
        extra = sb("extra", [HALF, 1])
        stat = sb("stat", [P, 8])
        stat_sb = sb("stat_sb", [1, 8])
        flag_f = sb("flag_f", [1, 8])
        flag = sb("flag", [1, 1], I32)
        place = sb("place", [P, NG, CH])
        vals = sb("vals", [P, NG, CH, 4], BF16)
        cmask = sb("cmask", [P, 2, CH, TILE], BF16)
        placed = sb("placed", [P, NG, NW, 4])
        idx = sb("idx", [P, NG, NW], I32)
        dcol = sb("dcol", [P, NG, NW])
        empty = sb("empty", [P, NG * NW])

        ibuf = sb("ibuf", [P, DEEP, NW], I32)
        rows = sb("rows", [P, DEEP, NW, CW])
        own = sb("own", [P, RING, 2, 2 * D])
        xin = sb("xin", [P, RING, 2, D])
        mask = sb("mask", [P, 2, 4 * P])
        h = sb("h", [P, 2, 2 * D])
        h_t = sb("h_t", [P, 2, 2 * P])
        gu = sb("gu", [P, RING, 2, 2 * D])
        act = sb("act", [P, 2, D])
        zed = sb("zed", [P, 2, D])
        x1 = sb("x1", [P, 2, 2, D])
        x1b = sb("x1b", [P, 2, 2, D])
        cnt = sb("cnt", [P, 2])
        inv = sb("inv", [P, NG, 2])
        bst = sb("bst", [P, 2, 6])
        mv = sb("mv", [P, 2, 2, 2])
        std = sb("std", [P, 2, 2])
        rstd = sb("rstd", [P, 2, 2])
        nmr = sb("nmr", [P, 2, 2])
        own_c = sb("own_c", [P, DEEP, 2, CW])
        x1c = sb("x1c", [P, DEEP, 2, D])
        cut = sb("cut", [P, RING, 4 * P], BF16)
        ident_b = sb("ident_b", [P, P], BF16)
        ident_2 = sb("ident_2", [P, P])
        node_of = sb("node_of", [P, 2, 4 * P])
        mx = sb("mx", [P, 2])
        top = sb("top", [P, 2])
        zs = sb("zs", [P, 2, 2])
        adm = sb("adm", [P, 2, 3, 2])
        dself = sb("dself", [P, 2, 2])
        pself = sb("pself", [P, 2, 2])
        own_p = sb("own_p", [P, 2, 2, D + 3])
        ez = sb("ez", [P, NW])
        el = sb("el", [P, NW])
        ed = sb("ed", [P, 2, NW])
        prob = sb("prob", [P, 2, 4 * P])
        dsum = sb("dsum", [P, 2])
        rden = sb("rden", [P, 2])
        res = sb("res", [P, 2, 2, D])

        low = sb("low", [P, P])
        se = sb("se", [P, 2], I32)
        g_row = sb("g_row", [P, CW])
        g_dst = sb("g_dst", [P, CW])
        g_sum = sb("g_sum", [P, CW])
        g_new = sb("g_new", [P, CW])
        g_node = sb("g_node", [P, CW])
        g_init = sb("g_init", [P, 2, CW])
        df = sb("df", [P, 1])
        wide = sb("wide", [P, P])
        same = sb("same", [P, P])
        tmp = sb("tmp", [P, P])
        g1 = sb("g1", [P, 8])
        w_idx = sb("w_idx", [P, 1], I32)
        g_x = sb("g_x", [P, D])
        g_x1 = sb("g_x1", [P, D])
        g_x1b = sb("g_x1b", [P, D])
        g_h = sb("g_h", [P, D])
        g_t = sb("g_t", [P, 2 * P])
        g_st = sb("g_st", [P, 6])
        g_mv = sb("g_mv", [P, 2])
        g_out = sb("g_out", [P, D])

        bank = [ctx.enter_context(nc.psum_tensor(f"bank{i}", [P, 512], F32)) for i in range(8)]
        ps_agg = [bank[0], bank[1]]
        ps_t = [bank[2], bank[3]]
        ps_g = [bank[4], bank[5]]
        ps_u = [bank[6], bank[7]]
        ps_place = [bank[0], bank[1]]
        ps_z = [bank[0], bank[1]]
        ps_e = [bank[4], bank[5]]
        ps_o = [bank[6], bank[7]]

        def pair(bk, w=D, stride=D):
            return bk[:, 0:2 * stride].rearrange("p (j w) -> p j w", j=2)[:, :, 0:w]

        names = ("const_g const_v prep_v prep_p prep_ld nat_ld nxt_ld wt_ld row_ld run_ld "
                 "wt_ps wt_cp first_ps idx_g cm_done pl_ps pl_cp prep_end "
                 "x_ld0 x_ld1 x_ld2 x_ld3 own_ld0 own_ld1 own_ld2 own_ld3 ibuf_cp mask_done agg_done cnt_v inv_v "
                 "z_v h_v ln_v ln_a rs_v nmr_v h_a tr_done ht_cp dense_done g_cp u_cp st0 st1 st2 "
                 "st3 x1_v x1b_v stx0 stx1 "
                 "one_v turn cl0 cl1 cl2 cl3 cl4 cl5 cl6 cl7 cut_v zm_done mx_v mt_a ad_a nm_v br_done ed_v "
                 "ls_v pf_a os_a pr_a "
                 "pv_done res_v cs_v es_v cd_v bn_v out0 out1 zrow ident_bv flag_v flag_ps wg_cp flag_rdy "
                 "ge_ld0 ge_rows0 ge_st0 ge_ld1 ge_rows1 ge_st1 ge_ld2 ge_rows2 ge_st2 ge_ld3 ge_rows3 ge_st3 "
                 "gn_ld0 gn_st0 gn_ld1 gn_st1 gn_ld2 gn_st2 gn_ld3 gn_st3 gn_ld4 gn_st4 ge_v ge_a ge_m gn_v gn_a "
                 "gn_m low_g edge_st prep_seq turn_v turn_s").split()
        S = {n: sem(n) for n in names}
        row_ld = [sem(f"row_ld{q}") for q in range(DEEP)]

        def rows_there(eng, g, ph):
            eng.wait_ge(row_ld[g.q], 16 * NW * ((ph - 1) * in_phase(g.q) + g.uses(DEEP) + 1))

        block = ctx.enter_context(nc.Block())

        def tab_rows(t, p):
            return tab[p][bass.ds(t * (2 * TILE), 2 * TILE), :].rearrange("(j p r) d -> p j (r d)", j=2, r=2)

        def node_rows(a, t):
            return a[bass.ds(t * TILE, TILE), :].rearrange("(j p) d -> p j d", j=2)

        def sync_program(eng):
            wt = S["wt_ld"]
            eng.dma_start(w_raw[:, 0, :], wl1).then_inc(wt, 16)
            eng.dma_start(w_raw[:, 1, :], wr1).then_inc(wt, 16)
            for l in range(2):
                eng.dma_start(w_raw[:, 2 + 2 * l, :], wlh[l, :, :]).then_inc(wt, 16)
                eng.dma_start(w_raw[:, 3 + 2 * l, :], wrh[l, :, :]).then_inc(wt, 16)
            eng.dma_start(w_raw[:, 6, :], w_gat).then_inc(wt, 16)
            eng.dma_start(att[:, 0:1], att_s.rearrange("(p a) -> p a", a=1)).then_inc(wt, 16)
            eng.dma_start(att[:, 1:2], att_d.rearrange("(p a) -> p a", a=1)).then_inc(wt, 16)
            for n, b in enumerate([bl1, blh[0, :], blh[1, :], bias]):
                eng.dma_start(b_bc[:, n, :], b.partition_broadcast(P)).then_inc(wt, 16)
            eng.dma_start(d_nat[:, :], dst.rearrange("(p a) -> p a", a=NAT)).then_inc(S["nat_ld"], 16)
            eng.dma_start(s_nat[:, :], src.rearrange("(p a) -> p a", a=NAT)).then_inc(S["nat_ld"], 16)
            for a, to in zip((src, dst), edges):
                eng.dma_start(to[0:E].rearrange("(p a) -> p a", a=NAT), a.rearrange("(p a) -> p a", a=NAT)
                              ).then_inc(S["edge_st"], 16)
            eng.wait_ge(S["const_v"], 1)
            for to in edges:
                eng.dma_start(to[E:EP].rearrange("(p a) -> p a", p=2), pad[:, :]).then_inc(S["edge_st"], 16)
            eng.dma_start(d_nxt[0:NAT_P - 1, :],
                          dst[1:1 + (NAT_P - 1) * NAT].rearrange("(p a) -> p a", a=NAT)).then_inc(S["nxt_ld"], 16)
            eng.dma_start(d_nxt[NAT_P - 1:NAT_P, 0:NAT - 1],
                          dst[1 + (NAT_P - 1) * NAT:E].rearrange("(p a) -> p a", p=1)).then_inc(S["nxt_ld"], 16)

            eng.wait_ge(S["flag_rdy"], 1)
            ok = eng.value_load(flag[0:1, 0:1], min_val=0, max_val=1)
            with eng.If(ok):
                fast_sync(eng)
            with eng.Else():
                general_sync(eng)

        def fast_sync(eng):
            def load_x(s):
                ld = S[f"x_ld{s.r}"]
                if s.last:
                    eng.dma_start(xin[0:TAIL, s.r, 0, :], x[N - TAIL:N, :]).then_inc(ld, 16)
                else:
                    eng.dma_start(xin[:, s.r, :, :], node_rows(x, s.t)).then_inc(ld, 16)

            def store(o, ph):
                eng.wait_ge(S["g_cp"], ph * NG + o.t + 1)
                eng.wait_ge(S["u_cp"], ph * NG + o.t + 1)
                eng.dma_start(tab_rows(o.t, ph % 2), gu[:, o.r, :, :]).then_inc(S[f"st{o.r}"], 16)

            def phase0(s):
                for g in ahead(s, 2):
                    if g.there:
                        wait(eng, S["h_a"], g.t - RING + 1)
                        load_x(g)
                if s.at(-5).there:
                    store(s.at(-5), 0)
            eng.wait_ge(S["const_g"], 5)
            steps(eng, 5, phase0)

            for ph in range(1, LAYERS + 1):
                ka = (ph - 1) * NG
                for r in range(RING):
                    eng.wait_ge(S[f"st{r}"], 16 * (ph * NG // RING))

                def load(g):
                    wait(eng, S["h_v"], ka + g.t - RING + 1)
                    eng.dma_start(own[:, g.r, :, :], tab_rows(g.t, (ph - 1) % 2)).then_inc(S[f"own_ld{g.r}"], 16)
                    if ph == LAYERS:
                        wait(eng, S["x1_v"], g.t - RING + 1)
                        load_x(g)

                def phase(s):
                    for g in ahead(s, 2):
                        if g.there:
                            load(g)
                    if ph < LAYERS and s.at(-3).there:
                        store(s.at(-3), ph)
                    if ph == LAYERS and s.at(-1).there:
                        o = s.at(-1)
                        eng.wait_ge(S["x1b_v"], o.t + 1)
                        eng.dma_start(node_rows(x1_d, o.t), x1b[:, o.b, :, :]).then_inc(S[f"stx{o.b}"], 16)
                    if ph == LAYERS and s.at(-5).there:
                        o = s.at(-5)
                        eng.wait_ge(S["g_cp"], ph * NG + o.t + 1)
                        eng.dma_start(node_rows(tab_c, o.t), gu[:, o.r, :, 0:CW]).then_inc(S[f"st{o.r}"], 16)
                if ph == LAYERS:
                    eng.wait_ge(S["h_a"], NG)
                    eng.wait_ge(S["one_v"], 1)
                steps(eng, 5 if ph == LAYERS else 3, phase)

            for r in range(RING):
                eng.wait_ge(S[f"st{r}"], 16 * ((LAYERS + 1) * NG // RING))
            for b in range(2):
                eng.wait_ge(S[f"stx{b}"], 16 * (NG // 2))

            def phase_c(s):
                for g in ahead(s, 3):
                    if g.there:
                        wait(eng, S["res_v"], g.t - DEEP + 1)
                        eng.dma_start(own_c[:, g.q, :, :], node_rows(tab_c, g.t)).then_inc(S[f"cl{g.q}"], 16)
                        eng.dma_start(x1c[:, g.q, :, :], node_rows(x1_d, g.t)).then_inc(S[f"cl{g.q}"], 16)
                o = s.at(-3)
                if o.there:
                    eng.wait_ge(S["res_v"], o.t + 1)
                    if o.last:
                        eng.dma_start(out[N - TAIL:N, :], res[0:TAIL, o.b, 0, :]).then_inc(S[f"out{o.b}"], 16)
                    else:
                        eng.dma_start(node_rows(out, o.t), res[:, o.b, :, :]).then_inc(S[f"out{o.b}"], 16)
            steps(eng, 3, phase_c)
            for b in range(2):
                eng.wait_ge(S[f"out{b}"], 16 * NG // 2)

        def gpsimd_program(eng):
            g = S["const_g"]
            eng.memset(ident[:, :], 0.0).then_inc(g, 1)
            eng.iota(iota_i[:, :], pattern=[[1, RUN]], base=0, channel_multiplier=0).then_inc(g, 1)
            eng.iota(part_i[:, :], pattern=[[P, 2]], base=0, channel_multiplier=1).then_inc(g, 1)
            eng.memset(xin[:, :, :, :], 0.0).then_inc(g, 1)
            eng.wait_ge(g, 1)
            eng.affine_select(out=ident[:, :], in_=ident[:, :], compare_op=ALU.not_equal, fill=1.0,
                              base=0, pattern=[[-1, P]], channel_multiplier=1).then_inc(g, 1)
            eng.memset(rows[:, :, :, :], 0.0).then_inc(S["zrow"], 1)
            eng.memset(low[:, :], 0.0).then_inc(S["low_g"], 1)
            eng.memset(g_row[:, :], 0.0).then_inc(S["low_g"], 1)
            eng.memset(g_dst[:, :], 0.0).then_inc(S["low_g"], 1)
            eng.memset(g_sum[:, :], 0.0).then_inc(S["low_g"], 1)
            eng.memset(g_new[:, :], 0.0).then_inc(S["low_g"], 1)
            eng.memset(g_node[:, :], 0.0).then_inc(S["low_g"], 1)
            eng.memset(g_x[:, :], 0.0).then_inc(S["low_g"], 1)
            eng.memset(g_init[:, :, :], 0.0).then_inc(S["low_g"], 1)
            eng.wait_ge(S["low_g"], 8)
            eng.affine_select(out=low[:, :], in_=low[:, :], compare_op=ALU.is_ge, fill=1.0,
                              base=0, pattern=[[1, P]], channel_multiplier=-1).then_inc(S["low_g"], 1)
            eng.memset(g_init[:, 1, D + 1:D + 2], -BIG).then_inc(S["low_g"], 1)
            eng.memset(g_node[:, D:D + 1], 1.0).then_inc(S["low_g"], 1)

            eng.wait_ge(S["prep_v"], 1)
            for q in range(2):
                eng.indirect_dma_start(out=row_d[:, q, :], out_offset=None,
                                       in_=dst.rearrange("(p a) -> p a", a=NAT),
                                       in_offset=bass.IndirectOffsetOnAxis(ap=row_i[:, q:q + 1], axis=0)
                                       ).then_inc(S["row_ld"], 16)
            eng.wait_ge(S["prep_v"], 2)
            eng.wait_ge(S["edge_st"], 64)
            view = [a.rearrange("(p a) -> p a", a=RUN + 1) for a in edges]
            for q in range(2):
                for a, to in zip(view, (run_s, run_d)):
                    eng.indirect_dma_start(out=to[:, q, :], out_offset=None, in_=a,
                                           in_offset=bass.IndirectOffsetOnAxis(ap=start_i[:, q:q + 1], axis=1)
                                           ).then_inc(S["run_ld"], 16)

            eng.wait_ge(S["flag_rdy"], 1)
            ok = eng.value_load(flag[0:1, 0:1], min_val=0, max_val=1)
            with eng.If(ok):
                fast_gpsimd(eng)
            with eng.Else():
                general_gpsimd(eng)

        def fast_gpsimd(eng):
            eng.wait_ge(S["zrow"], 2)
            for ph in range(1, LAYERS + 2):
                ka = (ph - 1) * NG
                for r in range(RING):
                    eng.wait_ge(S[f"st{r}"], 16 * (ph * NG // RING))
                table = tab[(ph - 1) % 2] if ph <= LAYERS else tab_c
                width = D if ph <= LAYERS else CW
                last = 2 * NPAD - 1 if ph <= LAYERS else NPAD - 1

                def gathers(s):
                    if not s.there:
                        return
                    eng.wait_ge(S["ibuf_cp"], ka + s.t + 1)
                    if ph <= LAYERS:
                        wait(eng, S["agg_done"], ka + s.t - DEEP + 1)
                    else:
                        wait(eng, S["pv_done"], s.t - DEEP + 1)
                    if s.i is not None:
                        eng.sem_inc(S["turn"], 1)
                    for w in range(NW):
                        eng.indirect_dma_start(out=rows[:, s.q, w, 0:width], out_offset=None, in_=table,
                                               in_offset=bass.IndirectOffsetOnAxis(ap=ibuf[:, s.q, w:w + 1], axis=0),
                                               bounds_check=last, oob_is_err=False
                                               ).then_inc(row_ld[s.q], 16)
                if ph == LAYERS + 1:
                    eng.wait_ge(S["agg_done"], LAYERS * NG)
                steps(eng, 0, gathers)

        def scalar_program(eng):
            for n in range(7):
                eng.wait_ge(S["wt_ps"], n + 1)
                to = wcat[:, n // 2, (n % 2) * D:(n % 2 + 1) * D] if n < 6 else w_t[:, :]
                eng.activation(to, bank[n][:, 0:P], ACT.Copy).then_inc(S["wt_cp"], 1)
            eng.activation(wg[:, 0:D], w_raw[:, 6, :], ACT.Copy).then_inc(S["wt_cp"], 1)
            eng.wait_ge(S["wt_ps"], 8)
            eng.activation(wg[:, D:D + 2], bank[0][:, 0:2], ACT.Copy).then_inc(S["wg_cp"], 1)

            for q in range(2):
                for k in range(4):
                    n = 4 * q + k
                    eng.wait_ge(S["prep_p"], n + 1)
                    view = bank[n % 4 + 2][:, 0:CH * HALF].rearrange("p (c t) -> p t c", c=CH)
                    to = place[:, q * HALF:(q + 1) * HALF, :] if k == 0 else \
                        vals[:, q * HALF:(q + 1) * HALF, :, k - 1]
                    eng.activation(to, view, ACT.Copy).then_inc(S["pl_cp"], 1)

            eng.wait_ge(S["flag_rdy"], 1)
            ok = eng.value_load(flag[0:1, 0:1], min_val=0, max_val=1)
            with eng.If(ok):
                fast_scalar(eng)
            with eng.Else():
                general_scalar(eng)

        def fast_scalar(eng):
            def norm_scale(g, k):
                eng.wait_ge(S["ln_v"], k + 1)
                eng.activation(std[:, g.b, :], mv[:, g.b, :, 1], ACT.Sqrt, bias=eps[:, 0:1]).then_inc(S["ln_a"], 1)

            def norm(g, k, kb, tile, at):
                eng.wait_ge(S["nmr_v"], k + 1)
                wait(eng, S["tr_done"], kb + g.t - 1)
                for j in range(2):
                    a = eng.activation(h[:, g.b, j * D:(j + 1) * D], tile[:, at, j, :], ACT.Relu,
                                       bias=nmr[:, g.b, j:j + 1], scale=rstd[:, g.b, j:j + 1])
                a.then_inc(S["h_a"], 1)

            def ht_copy(g, kb):
                eng.wait_ge(S["tr_done"], kb + g.t + 1)
                wait(eng, S["dense_done"], kb + g.t - 1)
                eng.activation(h_t[:, g.b, :], ps_t[g.b][:, 0:2 * P], ACT.Copy).then_inc(S["ht_cp"], 1)

            def g_copy(g, kb, width=D):
                eng.wait_ge(S["dense_done"], kb + g.t + 1)
                wait(eng, S[f"st{g.r}"], 16 * (kb // RING + g.uses(RING)))
                eng.activation(gu[:, g.r, :, 0:width], pair(ps_g[g.b], width, TILE), ACT.Copy).then_inc(S["g_cp"], 1)

            def phase0(s):
                if s.at(-1).there:
                    norm_scale(s.at(-1), s.t - 1)
                if s.at(-2).there:
                    norm(s.at(-2), s.t - 2, 0, xin, s.at(-2).r)
                if s.at(-3).there:
                    ht_copy(s.at(-3), 0)
                if s.at(-4).there:
                    g_copy(s.at(-4), 0)
                o = s.at(-2)
                if o.there:
                    eng.wait_ge(S["pl_ps"], o.t + 1)
                    eng.activation(placed[:, bass.ds(o.t, 1), :, :].rearrange("p t w v -> p (t w v)"),
                                   ps_place[o.b][:, 0:NW * 4], ACT.Copy).then_inc(S["prep_end"], 1)
            steps(eng, 4, phase0)

            def idx_copy(g, ph):
                wait(eng, row_ld[g.q], 16 * NW * ((ph - 1) * in_phase(g.q) + g.uses(DEEP)))
                frm = idx[:, bass.ds(g.t, 1), :].rearrange("p t w -> p (t w)")
                eng.activation(ibuf[:, g.q, :], frm, ACT.Copy,
                               scale=1.0 if ph <= LAYERS else 0.5).then_inc(S["ibuf_cp"], 1)

            eng.wait_ge(S["idx_g"], 1)
            for ph in range(1, LAYERS + 1):
                kb = ph * NG

                def phase(s):
                    if ph == LAYERS and s.at(-2).there:
                        norm(s.at(-2), NG + s.t - 2, kb, x1, s.b)
                    if ph == LAYERS and s.at(-3).there:
                        ht_copy(s.at(-3), kb)
                    o = s.at(-3 if ph < LAYERS else -5)
                    if o.there:
                        g_copy(o, kb, D if ph < LAYERS else D + 2)
                    for g in ahead(s, 4):
                        if g.there:
                            idx_copy(g, ph)
                    if ph < LAYERS and s.at(-1).there:
                        ht_copy(s.at(-1), kb)
                    if ph == LAYERS and s.at(-1).there:
                        norm_scale(s.at(-1), NG + s.t - 1)
                steps(eng, 5 if ph == LAYERS else 3, phase)

            def phase_c(s):
                for g in ahead(s, 4):
                    if g.there:
                        idx_copy(g, LAYERS + 1)
                if s.there:
                    eng.wait_ge(S[f"cl{s.q}"], 32 * (s.uses(DEEP) + 1))
                    wait(eng, S["br_done"], s.t - 1)
                    eng.activation(adm[:, s.b, 0, :], own_c[:, s.q, :, D + 1], ACT.Copy).then_inc(S["ad_a"], 1)
                o = s.at(-1)
                if o.there:
                    eng.wait_ge(S["nm_v"], o.t + 1)
                    eng.activation(pself[:, o.b, :], dself[:, o.b, :], ACT.Exp).then_inc(S["pf_a"], 1)
                    eng.wait_ge(S["pf_a"], o.t + 1)
                    wait(eng, S["pv_done"], o.t - 1)
                    for j in range(2):
                        a = eng.activation(own_p[:, o.b, j, :], own_c[:, o.q, j, 0:D + 3], ACT.Copy,
                                           scale=pself[:, o.b, j:j + 1])
                    a.then_inc(S["os_a"], 1)
                    eng.wait_ge(S["ed_v"], o.t + 1)
                    for w, at, n in ((0, 0, P), (1, P, TILE), (2, 3 * P, P)):
                        a = eng.activation(prob[:, o.b, at:at + n], cut[:, o.r, at:at + n], ACT.Exp,
                                           bias=ed[:, o.b, w:w + 1])
                    a.then_inc(S["pr_a"], 1)
                if s.there:
                    eng.wait_ge(S["mx_v"], s.t + 1)
                    eng.activation(node_of[:, s.b, :], ps_z[s.b][:, :], ACT.Identity, scale=1.0 / CUT,
                                   bias=ones[:, 0:1]).then_inc(S["mt_a"], 1)
            steps(eng, 1, phase_c)

        def tensor_program(eng):
            eng.wait_ge(S["const_g"], 5)
            eng.wait_ge(S["wt_ld"], 16 * 13)
            for n in range(7):
                eng.transpose(bank[n][:, 0:P], w_raw[:, n, :], ident[:, :]).then_inc(S["wt_ps"], 1)
            eng.wait_ge(S["wt_cp"], 7)
            eng.matmul(bank[0][:, 0:2], w_t[:, :], att[:, :], start=True, stop=True).then_inc(S["wt_ps"], 1)
            eng.wait_ge(S["prep_ld"], 1)
            eng.transpose(bank[7][:, 0:NAT_P], first[:, :], ident[0:NAT_P, 0:NAT_P]).then_inc(S["first_ps"], 1)
            eng.wait_ge(S["wt_cp"], 8)
            for q in range(2):
                for k in range(4):
                    n = 4 * q + k
                    eng.wait_ge(S["prep_v"], 3 + q)
                    if n >= 4:
                        eng.wait_ge(S["pl_cp"], n - 3)
                    for c in range(CH):
                        m = eng.transpose(bank[n % 4 + 2][:, c * HALF:(c + 1) * HALF],
                                          qty[:, k, c * P:(c + 1) * P], ident[0:HALF, 0:HALF])
                    m.then_inc(S["prep_p"], 1)
            eng.wait_ge(S["flag_v"], 1)
            eng.matmul(bank[1][0:1, 0:8], ones[:, 0:1], stat[:, :], start=True, stop=True).then_inc(S["flag_ps"], 1)

            eng.wait_ge(S["flag_rdy"], 1)
            ok = eng.value_load(flag[0:1, 0:1], min_val=0, max_val=1)
            with eng.If(ok):
                fast_tensor(eng)
            with eng.Else():
                general_tensor(eng)

        def fast_tensor(eng):
            eng.wait_ge(S["pl_cp"], 8)

            def placing(s):
                eng.wait_ge(S["cm_done"], s.t + 1)
                wait(eng, S["prep_end"], s.t - 1)
                for w in range(NW):
                    cs = [c for c in range(CH) if w - BAND[c] in (0, 1)]
                    for c in cs:
                        a = (w - BAND[c]) * P
                        m = eng.matmul(ps_place[s.b][:, 4 * w:4 * w + 3], cmask[:, s.b, c, a:a + P],
                                       vals[:, bass.ds(s.t, 1), c, 0:3].rearrange("p t v -> p (t v)"),
                                       start=(c == cs[0]), stop=(c == cs[-1]))
                m.then_inc(S["pl_ps"], 1)

            def turn_h(g, kb, ready, n):
                eng.wait_ge(ready, n)
                wait(eng, S["ht_cp"], kb + g.t - 1)
                for j in range(2):
                    m = eng.transpose(ps_t[g.b][:, j * P:(j + 1) * P], h[:, g.b, j * D:(j + 1) * D], ident[:, :])
                m.then_inc(S["tr_done"], 1)

            def dense(g, kb, w_g, w_u, width):
                eng.wait_ge(S["ht_cp"], kb + g.t + 1)
                wait(eng, S["g_cp"], kb + g.t - 1)
                if w_u is not None:
                    wait(eng, S["u_cp"], kb + g.t - 1)
                for j in range(2):
                    m = eng.matmul(ps_g[g.b][:, j * TILE:j * TILE + width], h_t[:, g.b, j * P:(j + 1) * P], w_g,
                                   start=True, stop=True)
                    if w_u is not None:
                        m = eng.matmul(ps_u[g.b][:, j * TILE:j * TILE + D], h_t[:, g.b, j * P:(j + 1) * P], w_u,
                                       start=True, stop=True)
                m.then_inc(S["dense_done"], 1)

            def phase0(s):
                if s.at(-2).there:
                    turn_h(s.at(-2), 0, S["h_a"], s.t - 1)
                if s.at(-1).there:
                    placing(s.at(-1))
                if s.at(-3).there:
                    dense(s.at(-3), 0, wcat[:, 0, 0:D], wcat[:, 0, D:2 * D], D)
            steps(eng, 3, phase0)

            for ph in range(1, LAYERS + 1):
                kb = ph * NG
                ka = (ph - 1) * NG

                def phase(s):
                    if s.there:
                        eng.wait_ge(S["mask_done"], ka + s.t + 1)
                        wait(eng, S["z_v"], ka + s.t - 1)
                        rows_there(eng, s, ph)
                        for w, j, m0 in ((0, 0, 0), (1, 0, 1), (1, 1, 2), (2, 1, 3)):
                            eng.matmul(ps_agg[s.b][:, j * TILE:j * TILE + D + 1],
                                       mask[:, s.b, m0 * P:(m0 + 1) * P], rows[:, s.q, w, 0:D + 1],
                                       start=(m0 % 2 == 0), stop=False)
                            if m0 == 1:
                                eng.wait_ge(S[f"own_ld{s.r}"], 16 * (ka // RING + s.uses(RING) + 1))
                            if m0 % 2:
                                m = eng.matmul(ps_agg[s.b][:, j * TILE:j * TILE + D], ident[:, :],
                                               own[:, s.r, j, 0:D], start=False, stop=True)
                        m.then_inc(S["agg_done"], 1)
                    if ph < LAYERS:
                        if s.at(-1).there:
                            turn_h(s.at(-1), kb, S["h_v"], ka + s.t)
                        if s.at(-2).there:
                            dense(s.at(-2), kb, wcat[:, ph, 0:D], wcat[:, ph, D:2 * D], D)
                    else:
                        if s.at(-3).there:
                            turn_h(s.at(-3), kb, S["h_a"], NG + s.t - 2)
                        if s.at(-4).there:
                            dense(s.at(-4), kb, wg[:, :], None, D + 2)
                steps(eng, 5 if ph == LAYERS else 3, phase)

            eng.wait_ge(S["g_cp"], (LAYERS + 1) * NG)
            eng.wait_ge(S["z_v"], LAYERS * NG)
            eng.wait_ge(S["ident_bv"], 2)

            def phase_c(s):
                if s.there:
                    eng.wait_ge(S["cut_v"], s.t + 1)
                    wait(eng, S["mt_a"], s.t - 1)
                    rows_there(eng, s, LAYERS + 1)
                    for w, j, m0 in ((0, 0, 0), (1, 0, 1), (1, 1, 2), (2, 1, 3)):
                        to = ps_z[s.b][:, m0 * P:(m0 + 1) * P]
                        eng.matmul(to, rows[:, s.q, w, D:D + 1].to_broadcast([P, P]), ident[:, :],
                                   start=True, stop=False)
                        m = eng.matmul(to, cut[:, s.r, m0 * P:(m0 + 1) * P], ident_b[:, :], start=False, stop=True)
                    m.then_inc(S["zm_done"], 1)
                o = s.at(-1)
                if o.there:
                    eng.wait_ge(S["mt_a"], o.t + 1)
                    eng.wait_ge(S["ad_a"], o.t + 1)
                    eng.wait_ge(S["nm_v"], o.t + 1)
                    wait(eng, S["ed_v"], o.t - 1)
                    for w, j, m0 in ((0, 0, 0), (1, 0, 1), (1, 1, 2), (2, 1, 3)):
                        m = eng.matmul(ps_e[o.b][:, 2 * w:2 * w + 2], node_of[:, o.b, m0 * P:(m0 + 1) * P],
                                       adm[:, o.b, 0:2, j], start=(m0 != 2), stop=(m0 != 1))
                    m.then_inc(S["br_done"], 1)
                o = s.at(-2)
                if o.there:
                    eng.wait_ge(S["pr_a"], o.t + 1)
                    wait(eng, S["res_v"], o.t - 1)
                    eng.wait_ge(S["os_a"], o.t + 1)
                    for w, j, m0 in ((0, 0, 0), (1, 0, 1), (1, 1, 2), (2, 1, 3)):
                        to = ps_o[o.b][:, j * TILE:j * TILE + D + 3]
                        eng.matmul(to, prob[:, o.b, m0 * P:(m0 + 1) * P], rows[:, o.q, w, 0:D + 3],
                                   start=(m0 % 2 == 0), stop=False)
                        if m0 % 2:
                            m = eng.matmul(to, ident_2[:, :], own_p[:, o.b, j, :], start=False, stop=True)
                    m.then_inc(S["pv_done"], 1)
            steps(eng, 2, phase_c)

        def vector_program(eng):
            eng.memset(pad[:, :], BEYOND)
            eng.memset(d_nxt[:, :], N).then_inc(S["const_v"], 1)
            eng.memset(ones[:, :], 1.0).then_inc(S["const_v"], 1)
            eng.memset(eps[:, :], 1e-5).then_inc(S["const_v"], 1)
            eng.memset(stat[:, :], 0.0).then_inc(S["const_v"], 1)
            eng.wait_ge(S["const_g"], 5)
            seq = [0]

            def op(ins):
                seq[0] += 1
                ins.then_inc(S["prep_seq"], 1)
                eng.wait_ge(S["prep_seq"], seq[0])
            op(eng.tensor_copy(iota[:, :], iota_i[:, :]))
            op(eng.tensor_copy(part[:, :], part_i[:, :]))
            op(eng.tensor_scalar(iota_c[:, :], iota[:, 0:NW * P], -128.0, None, ALU.add))
            op(eng.tensor_scalar(iota_b[:, :], iota[:, 0:TILE], 0.0, None, ALU.add))
            eng.tensor_copy(ident_b[:, :], ident[:, :]).then_inc(S["ident_bv"], 1)
            eng.tensor_scalar(ident_2[:, :], ident[:, :], 2.0, None, ALU.mult).then_inc(S["ident_bv"], 1)
            op(eng.tensor_scalar(thr[:, 0:1], part[:, 0:1], float(TILE), None, ALU.mult))
            op(eng.tensor_scalar(thr[:, 1:2], part[:, 0:1], float(HALF), float(TILE), ALU.add, ALU.mult))
            eng.wait_ge(S["zrow"], 1)
            eng.memset(rows[:, :, :, D:D + 1], 1.0).then_inc(S["zrow"], 1)

            eng.wait_ge(S["nat_ld"], 32)
            op(eng.tensor_scalar(first[:, :], ones[0:NAT_P, :], d_nat[:, 0:1], None, ALU.mult))
            eng.sem_inc(S["prep_ld"], 1)
            eng.wait_ge(S["nxt_ld"], 32)
            op(eng.tensor_tensor(cmp_n[:, :], d_nat[:, :], d_nxt[:, :], ALU.is_gt))
            op(eng.tensor_reduce(stat[0:NAT_P, 0:1], cmp_n[:, :], AX.X, ALU.add))
            op(eng.tensor_tensor(cmp_n[:, :], d_nat[:, :], d_nxt[:, :], ALU.not_equal))
            op(eng.tensor_reduce(stat[0:NAT_P, 1:2], cmp_n[:, :], AX.X, ALU.add))
            op(eng.tensor_tensor(cmp_m[:, :], s_nat[:, :], d_nat[:, :], ALU.not_equal))
            op(eng.tensor_tensor(cmp_m[:, :], cmp_m[:, :], cmp_n[:, :], ALU.mult))
            op(eng.tensor_reduce(stat[0:NAT_P, 2:3], cmp_m[:, :], AX.X, ALU.add))

            eng.wait_ge(S["first_ps"], 1)
            for q in range(2):
                op(eng.tensor_scalar(cmp_n[0:HALF, 0:NAT_P], bank[7][0:HALF, 0:NAT_P], thr[0:HALF, q:q + 1], None,
                                     ALU.is_lt))
                op(eng.tensor_reduce(row_c[:, q:q + 1], cmp_n[0:HALF, 0:NAT_P], AX.X, ALU.add))
            op(eng.tensor_scalar(row_c[:, :], row_c[:, :], -1.0, 0.0, ALU.add, ALU.max))
            op(eng.tensor_copy(row_i[:, :], row_c[:, :]))
            eng.sem_inc(S["prep_v"], 1)
            eng.wait_ge(S["row_ld"], 32)
            for q in range(2):
                op(eng.tensor_scalar(cmp_n[0:HALF, :], row_d[:, q, :], thr[0:HALF, q:q + 1], None, ALU.is_lt))
                op(eng.tensor_reduce(in_row[:, q:q + 1], cmp_n[0:HALF, :], AX.X, ALU.add))
            op(eng.scalar_tensor_tensor(e_first[:, :], row_c[:, :], float(NAT), in_row[:, :], ALU.mult, ALU.add))
            op(eng.tensor_copy(start_i[:, :], e_first[:, :]))
            eng.sem_inc(S["prep_v"], 1)
            eng.wait_ge(S["run_ld"], 64)
            for q in range(2):
                if q == 1:
                    eng.wait_ge(S["prep_p"], 4)
                drel = qty[:, 3, :]
                op(eng.tensor_tensor(w_valid[:, :], run_d[:, q, 0:RUN], run_d[:, q, 1:RUN + 1], ALU.is_equal))
                op(eng.tensor_scalar(drel, run_d[:, q, 0:RUN], thr[0:HALF, q:q + 1], None, ALU.subtract))
                op(eng.scalar_tensor_tensor(w_valid[:, :], drel, 0.0, w_valid[:, :], ALU.is_ge, ALU.mult))
                op(eng.scalar_tensor_tensor(w_valid[:, :], drel, float(TILE), w_valid[:, :], ALU.is_lt, ALU.mult))
                op(eng.tensor_reduce(stat[0:HALF, 3 + q:4 + q], w_valid[:, :], AX.X, ALU.add))
                op(eng.scalar_tensor_tensor(w_a[:, :], iota[0:HALF, :], float(OFF), drel, ALU.add, ALU.subtract))
                op(eng.tensor_scalar(w_b[:, :], drel, float(P), float(P), ALU.is_ge, ALU.mult))
                op(eng.tensor_tensor(w_b[:, :], w_a[:, :], w_b[:, :], ALU.subtract))
                op(eng.scalar_tensor_tensor(qty[:, 1, :], w_b[:, :], 0.0, w_valid[:, :], ALU.is_lt, ALU.mult))
                op(eng.scalar_tensor_tensor(qty[:, 2, :], w_b[:, :], float(TILE), w_valid[:, :], ALU.is_ge, ALU.mult))
                op(eng.tensor_tensor(qty[:, 1, :], qty[:, 1, :], qty[:, 2, :], ALU.add))
                op(eng.tensor_reduce(stat[0:HALF, 5 + q:6 + q], qty[:, 1, :], AX.X, ALU.add))
                for c in range(CH):
                    cc = slice(c * P, (c + 1) * P)
                    op(eng.tensor_scalar(w_b[:, cc], w_a[:, cc], float(-BAND[c] * P), None, ALU.add))
                op(eng.scalar_tensor_tensor(qty[:, 1, :], w_b[:, :], 0.0, w_valid[:, :], ALU.is_lt, ALU.mult))
                op(eng.scalar_tensor_tensor(qty[:, 2, :], w_b[:, :], float(TILE), w_valid[:, :], ALU.is_ge, ALU.mult))
                op(eng.tensor_tensor(qty[:, 1, :], qty[:, 1, :], qty[:, 2, :], ALU.add))
                op(eng.tensor_reduce(stat[0:HALF, 7:8] if q else extra[:, :], qty[:, 1, :], AX.X, ALU.add))
                if q:
                    op(eng.tensor_tensor(stat[0:HALF, 7:8], stat[0:HALF, 7:8], extra[:, :], ALU.add))
                op(eng.scalar_tensor_tensor(w_a[:, :], w_a[:, :], -128.0 - NOWHERE, w_valid[:, :], ALU.add, ALU.mult))
                op(eng.tensor_scalar(qty[:, 0, :], w_a[:, :], NOWHERE, None, ALU.add))
                op(eng.tensor_scalar(drel, drel, 1.0, None, ALU.add))
                op(eng.tensor_scalar(w_int[:, 0, :], run_s[:, q, 0:RUN], 8, None, ALU.logical_shift_right))
                op(eng.tensor_scalar(w_int[:, 1, :], run_s[:, q, 0:RUN], 255, None, ALU.bitwise_and))
                op(eng.tensor_copy(qty[:, 1:3, :], w_int[:, :, :]))
                eng.sem_inc(S["prep_v"], 1)
            eng.sem_inc(S["flag_v"], 1)

            eng.wait_ge(S["flag_ps"], 1)
            op(eng.tensor_copy(stat_sb[:, :], bank[1][0:1, 0:8]))
            op(eng.tensor_tensor(flag_f[:, 0:1], stat_sb[:, 0:1], stat_sb[:, 2:3], ALU.add))
            op(eng.tensor_tensor(flag_f[:, 1:2], stat_sb[:, 5:6], stat_sb[:, 6:7], ALU.add))
            op(eng.tensor_tensor(flag_f[:, 0:1], flag_f[:, 0:1], flag_f[:, 1:2], ALU.add))
            op(eng.tensor_tensor(flag_f[:, 0:1], flag_f[:, 0:1], stat_sb[:, 7:8], ALU.add))
            op(eng.tensor_scalar(flag_f[:, 0:1], flag_f[:, 0:1], 0.0, None, ALU.is_equal))
            op(eng.tensor_scalar(flag_f[:, 1:2], stat_sb[:, 1:2], float(N), None, ALU.is_equal))
            op(eng.tensor_tensor(flag_f[:, 2:3], stat_sb[:, 3:4], stat_sb[:, 4:5], ALU.add))
            op(eng.tensor_scalar(flag_f[:, 2:3], flag_f[:, 2:3], float(E - N), None, ALU.is_equal))
            op(eng.tensor_tensor(flag_f[:, 0:1], flag_f[:, 0:1], flag_f[:, 1:2], ALU.mult))
            op(eng.tensor_tensor(flag[:, :], flag_f[:, 0:1], flag_f[:, 2:3], ALU.mult))
            eng.sem_inc(S["flag_rdy"], 1)
            ok = eng.value_load(flag[0:1, 0:1], min_val=0, max_val=1)
            eng.wait_ge(S["wt_ld"], 16 * 13)
            with eng.If(ok):
                fast_vector(eng, op)
            with eng.Else():
                general_vector(eng)

        def fast_vector(eng, op):
            eng.wait_ge(S["pl_cp"], 8)

            def place_mask(s):
                wait(eng, S["pl_ps"], s.t - 1)
                for c in range(CH):
                    m = eng.tensor_scalar(cmask[:, s.b, c, :], iota_c[:, BAND[c] * P:BAND[c] * P + TILE],
                                          place[:, bass.ds(s.t, 1), c:c + 1].rearrange("p t c -> p (t c)"),
                                          None, ALU.is_equal)
                m.then_inc(S["cm_done"], 1)

            def stats(g, k, tile, at):
                wait(eng, S["ln_v"], k)
                for j in range(2):
                    m = eng.bn_stats(bst[:, j, :], tile[:, at, j, :])
                m.then_inc(S["bn_v"], 1)

            def stats_end(g, k):
                eng.wait_ge(S["bn_v"], k + 1)
                if g.i is not None:
                    eng.sem_inc(S["turn_v"], 1)
                for j in range(2):
                    m = eng.bn_aggr(mv[:, g.b, j, :], bst[:, j, :])
                m.then_inc(S["ln_v"], 1)

            def scale(g, k):
                eng.wait_ge(S["ln_a"], k + 1)
                wait(eng, S["h_a"], k - 1)
                eng.reciprocal(rstd[:, g.b, :], std[:, g.b, :]).then_inc(S["rs_v"], 1)

            def shift(g, k):
                eng.wait_ge(S["rs_v"], k + 1)
                eng.scalar_tensor_tensor(nmr[:, g.b, :], mv[:, g.b, :, 0], -1.0, rstd[:, g.b, :], ALU.mult,
                                         ALU.mult).then_inc(S["nmr_v"], 1)

            def u_copy(g, kb, layer):
                eng.wait_ge(S["dense_done"], kb + g.t + 1)
                wait(eng, S[f"st{g.r}"], 16 * (kb // RING + g.uses(RING)))
                eng.tensor_tensor(gu[:, g.r, :, D:2 * D], pair(ps_u[g.b], D, TILE),
                                  b_bc[:, layer, :].unsqueeze(1).to_broadcast([P, 2, D]), ALU.add
                                  ).then_inc(S["u_cp"], 1)

            def phase0(s):
                if s.there:
                    eng.wait_ge(S[f"x_ld{s.r}"], 16 * (s.uses(RING) + 1))
                    stats(s, s.t, xin, s.r)
                if s.at(-1).there:
                    scale(s.at(-1), s.t - 1)
                if s.at(-4).there:
                    u_copy(s.at(-4), 0, 0)
                if s.at(-1).there:
                    shift(s.at(-1), s.t - 1)
                if s.there:
                    place_mask(s)
                    stats_end(s, s.t)
            steps(eng, 4, phase0)

            eng.wait_ge(S["prep_end"], NG)
            pv = placed[:, :, :, :].rearrange("p t w v -> p (t w) v")
            idx_f = idx[:, :, :].rearrange("p t w -> p (t w)")
            dc_f = dcol[:, :, :].rearrange("p t w -> p (t w)")
            op(eng.tensor_scalar(dc_f, pv[:, :, 2], -1.0, None, ALU.add))
            op(eng.tensor_scalar(empty[:, :], dc_f, 0.0, FAR, ALU.is_lt, ALU.mult))
            op(eng.scalar_tensor_tensor(empty[:, :], pv[:, :, 1], 2.0, empty[:, :], ALU.mult, ALU.add))
            op(eng.scalar_tensor_tensor(idx_f, pv[:, :, 0], 512.0, empty[:, :], ALU.mult, ALU.add))
            eng.sem_inc(S["idx_g"], 1)

            def masks(g, to, io, done, w, value):
                a, b, at = ((0, P, 0), (0, TILE, P), (P, TILE, 3 * P))[w]
                node = dcol[:, bass.ds(g.t, 1), w:w + 1].rearrange("p t w -> p (t w)")
                if value is None:
                    m = eng.tensor_scalar(to[:, at:at + b - a], io[:, a:b], node, None, ALU.is_equal)
                else:
                    m = eng.tensor_scalar(to[:, at:at + b - a], io[:, a:b], node, value, ALU.not_equal, ALU.mult)
                if w == NW - 1:
                    m.then_inc(S[done], 1)

            for ph in range(1, LAYERS + 1):
                ka = (ph - 1) * NG
                kb = ph * NG
                if ph == LAYERS:
                    for r in range(RING):
                        eng.wait_ge(S[f"st{r}"], 16 * (ph * NG // RING))
                    eng.memset(gu[:, :, :, D + 2:CW], 1.0).then_inc(S["one_v"], 1)

                def phase(s):
                    def mask_part(w):
                        g = s.at(1)
                        if g.there:
                            if w == 0:
                                wait(eng, S["agg_done"], ka + g.t - 1)
                            masks(g, mask[:, g.b, :], iota, "mask_done", w, None)
                    if s.i is None and s.t == 0:
                        for w in range(NW):
                            masks(s, mask[:, s.b, :], iota, "mask_done", w, None)
                    if ph < LAYERS and s.at(-3).there:
                        u_copy(s.at(-3), kb, ph)
                    k = ka + s.t
                    if s.there:
                        eng.wait_ge(S["agg_done"], k + 1)
                        acc_ps = pair(ps_agg[s.b], D + 1, TILE)
                        if ph == 1:
                            eng.tensor_scalar(cnt[:, :], acc_ps[:, :, D], 1.0, None, ALU.add).then_inc(S["cnt_v"], 1)
                    if s.there:
                        mask_part(0)
                        inv_t = inv[:, bass.ds(s.t, 1), :].rearrange("p t j -> p (t j)")
                        if ph == 1:
                            eng.wait_ge(S["cnt_v"], k + 1)
                            eng.reciprocal(inv_t, cnt[:, :]).then_inc(S["inv_v"], 1)
                        mask_part(1)
                        mask_part(2)
                        if ph == 1:
                            eng.wait_ge(S["inv_v"], k + 1)
                        wait(eng, S["h_v"], k)
                        for j in range(2):
                            m = eng.scalar_tensor_tensor(zed[:, j, :], acc_ps[:, j, 0:D], inv_t[:, j:j + 1],
                                                         own[:, s.r, j, D:2 * D], ALU.mult, ALU.add)
                        m.then_inc(S["z_v"], 1)
                    if ph == LAYERS and s.at(-1).there:
                        eng.wait_ge(S["x1_v"], s.t)
                        stats(s.at(-1), NG + s.t - 1, x1, s.at(-1).b)
                    if s.there:
                        if ph < LAYERS:
                            to = h[:, s.b, :].rearrange("p (j d) -> p j d", j=2)
                            eng.wait_ge(S["tr_done"], kb + s.t - 1)
                        else:
                            to = act[:, :, :]
                        eng.wait_ge(S["z_v"], k + 1)
                        eng.scalar_tensor_tensor(to, zed[:, :, :], 0.01, zed[:, :, :], ALU.mult, ALU.max
                                                 ).then_inc(S["h_v"], 1)
                    if ph == LAYERS and s.at(-1).there:
                        stats_end(s.at(-1), NG + s.t - 1)
                    if ph == LAYERS:
                        if s.there:
                            eng.wait_ge(S["h_v"], k + 1)
                            eng.wait_ge(S[f"x_ld{s.r}"], 16 * (NG // RING + s.uses(RING) + 1))
                            wait(eng, S["h_a"], NG + s.t - 1)
                            eng.tensor_tensor(x1[:, s.b, :, :], act[:, :, :], xin[:, s.r, :, :], ALU.add
                                              ).then_inc(S["x1_v"], 1)
                        o = s.at(-1)
                        if o.there:
                            scale(o, NG + o.t)
                            wait(eng, S[f"stx{o.b}"], 16 * o.uses(2))
                            eng.tensor_tensor(x1b[:, o.b, :, :], x1[:, o.b, :, :],
                                              b_bc[:, LAYERS, :].unsqueeze(1).to_broadcast([P, 2, D]), ALU.add
                                              ).then_inc(S["x1b_v"], 1)
                            shift(o, NG + o.t)
                steps(eng, 4 if ph == LAYERS else 3, phase)

            def phase_c(s):
                o, f = s.at(-1), s.at(-3)
                k = s.t
                oc = own_c[:, s.q, :, :]

                def cut_part(g, w):
                    if w == 0:
                        wait(eng, S["pr_a"], g.t - RING + 1)
                    masks(g, cut[:, g.r, :], iota_b, "cut_v", w, -CUT)
                if s.i is None and s.t == 0:
                    for g in (s, s.at(1)):
                        for w in range(NW):
                            cut_part(g, w)
                if s.there:
                    eng.wait_ge(S[f"cl{s.q}"], 32 * (s.uses(DEEP) + 1))
                    eng.tensor_tensor(zs[:, 1, :], oc[:, :, D], oc[:, :, D + 1], ALU.add).then_inc(S["cs_v"], 1)
                    eng.wait_ge(S["zm_done"], k + 1)
                    eng.tensor_reduce(mx[:, :], ps_z[s.b][:, :].rearrange("p (j e) -> p j e", j=2), AX.X, ALU.max
                                      ).then_inc(S["mx_v"], 1)
                if o.there:
                    pse = ps_e[o.b][:, 0:2 * NW].rearrange("p (w v) -> p w v", w=NW)
                    eng.wait_ge(S["br_done"], o.t + 1)
                    eng.tensor_tensor(ez[:, :], rows[:, o.q, :, D], pse[:, :, 0], ALU.add).then_inc(S["es_v"], 1)
                if s.there:
                    eng.wait_ge(S["mx_v"], k + 1)
                    eng.tensor_tensor(top[:, :], mx[:, :], oc[:, :, D], ALU.max).then_inc(S["cs_v"], 1)
                if o.there:
                    eng.wait_ge(S["es_v"], 2 * o.t + 1)
                    eng.scalar_tensor_tensor(el[:, :], ez[:, :], 0.2, ez[:, :], ALU.mult, ALU.max
                                             ).then_inc(S["es_v"], 1)
                if s.there:
                    eng.wait_ge(S["cs_v"], 3 * k + 2)
                    eng.tensor_tensor(zs[:, 0, :], top[:, :], oc[:, :, D + 1], ALU.add).then_inc(S["cs_v"], 1)
                if o.there:
                    eng.wait_ge(S["es_v"], 2 * o.t + 2)
                    wait(eng, S["pr_a"], o.t - 1)
                    eng.tensor_tensor(ed[:, o.b, :], el[:, :], pse[:, :, 1], ALU.subtract).then_inc(S["ed_v"], 1)
                if s.there:
                    eng.wait_ge(S["cs_v"], 3 * k + 3)
                    wait(eng, S["br_done"], k - 1)
                    eng.scalar_tensor_tensor(adm[:, s.b, 1:3, :], zs[:, :, :], 0.2, zs[:, :, :], ALU.mult, ALU.max
                                             ).then_inc(S["ls_v"], 1)
                if s.at(2).there:
                    cut_part(s.at(2), 0)
                if s.there:
                    eng.wait_ge(S["ls_v"], k + 1)
                    wait(eng, S["pf_a"], k - 1)
                    eng.tensor_tensor(dself[:, s.b, :], adm[:, s.b, 2, :], adm[:, s.b, 1, :], ALU.subtract
                                      ).then_inc(S["nm_v"], 1)
                if f.there:
                    eng.wait_ge(S["pv_done"], f.t + 1)
                    eng.tensor_scalar(dsum[:, :], pair(ps_o[f.b], D + 3, TILE)[:, :, D + 2], 1e-16, None, ALU.add
                                      ).then_inc(S["cd_v"], 1)
                if s.at(2).there:
                    cut_part(s.at(2), 1)
                if f.there:
                    eng.wait_ge(S["cd_v"], 2 * f.t + 1)
                    eng.reciprocal(rden[:, :], dsum[:, :]).then_inc(S["cd_v"], 1)
                if s.at(2).there:
                    cut_part(s.at(2), 2)
                if f.there:
                    eng.wait_ge(S["cd_v"], 2 * f.t + 2)
                    wait(eng, S[f"out{f.b}"], 16 * f.uses(2))
                    for j in range(2):
                        m = eng.scalar_tensor_tensor(res[:, f.b, j, :], ps_o[f.b][:, j * TILE:j * TILE + D],
                                                     rden[:, j:j + 1], x1c[:, f.q, j, :], ALU.mult, ALU.add)
                    m.then_inc(S["res_v"], 1)
            steps(eng, 3, phase_c)

        NODE_V, NODE_M, NODE_A = (4, 5, 5, 12, 12), (0, 2, 2, 4, 0), (2, 1, 1, 4, 1)

        def tile_of(a, t, w=None):
            rows_ = a[bass.ds(t * P, P), :] if not isinstance(t, int) else a[t * P:(t + 1) * P, :]
            return rows_ if w is None else rows_[:, 0:w]

        def node_loop(eng, body):
            with eng.Fori(0, NT - 1) as t:
                body(t, P)
            body(NT - 1, TAIL_T)

        def general_sync(eng):
            v_base = 0
            eng.wait_ge(S["low_g"], 11)
            for ph in range(LAYERS + 2):
                ld, st = Count(S[f"gn_ld{ph}"]), Count(S[f"gn_st{ph}"])
                if ph:
                    eng.wait_ge(S[f"ge_st{ph - 1}"], 16 * NE)
                loads = {0: 1, 3: 3, 4: 3}.get(ph, 2)
                stores = {0: 2, 3: 3, 4: 1}.get(ph, 2)

                def body(t, n):
                    ld.begin(16 * loads, t)
                    st.begin(16 * stores, t)
                    if ph in (0, 3):
                        ld.inc(eng.dma_start(g_x[0:n, :], x[bass.ds(t * P, n), :]), 16)
                    if ph:
                        ld.inc(eng.dma_start(g_sum[:, :], tile_of(gen_s, t)), 16)
                        ld.inc(eng.dma_start(g_row[:, :], tile_of(gen_h if ph <= 3 else tab_c, t)), 16)
                    if ph == 4:
                        ld.inc(eng.dma_start(g_x1b[:, :], tile_of(x1_d, t)), 16)
                    if ph == 0:
                        eng.wait_ge(S["gn_a"], 2 * t + 2)
                    else:
                        eng.wait_ge(S["gn_v"], t * NODE_V[ph] + (v_base + NODE_V[ph]))
                    if ph <= 2:
                        st.inc(eng.dma_start(tile_of(gen_h, t), g_node[:, :]), 16)
                    if ph == 3:
                        st.inc(eng.dma_start(tile_of(tab_c, t), g_node[:, :]), 16)
                        st.inc(eng.dma_start(tile_of(x1_d, t), g_x1b[:, :]), 16)
                    if ph <= 3:
                        st.inc(eng.dma_start(tile_of(gen_s, t), g_init[:, int(ph == 3), :]), 16)
                    else:
                        st.inc(eng.dma_start(out[bass.ds(t * P, n), :], g_out[0:n, :]), 16)
                    eng.wait_ge(S[f"gn_st{ph}"], st.now())
                    eng.sem_inc(S["turn_s"], 1)
                node_loop(eng, body)
                ld.end(NT)
                st.end(NT)
                v_base += NODE_V[ph] * NT

        def general_gpsimd(eng):
            stored = {0: 32, 1: 32, 2: 32, 3: 48}
            v_base = 0
            for ph in range(LAYERS + 1):
                ld, rw, st = Count(S[f"ge_ld{ph}"]), Count(S[f"ge_rows{ph}"]), Count(S[f"ge_st{ph}"])
                eng.wait_ge(S[f"gn_st{ph}"], stored[ph] * NT)
                table = gen_h if ph < LAYERS else tab_c[0:NT * P, :]
                k = 3 if ph == LAYERS else 2
                v_n = 7 + 1 if ph < LAYERS else 18
                with eng.Fori(0, NE) as i:
                    ld.begin(32, i)
                    rw.begin(16 * k, i)
                    st.begin(16, i)
                    for c in range(2):
                        ld.inc(eng.dma_start(se[:, c:c + 1],
                                             edges[c][bass.ds(i * P, P)].rearrange("(p a) -> p a", a=1)), 16)
                    eng.wait_ge(S[f"ge_ld{ph}"], ld.now())
                    eng.sem_inc(S["turn"], 1)
                    for to, frm, c in ((g_row, table, 0), (g_sum, gen_s, 1), (g_dst, table, 1))[:k]:
                        rw.inc(eng.indirect_dma_start(out=to[:, :], out_offset=None, in_=frm,
                                                      in_offset=bass.IndirectOffsetOnAxis(ap=se[:, c:c + 1], axis=0),
                                                      bounds_check=N - 1, oob_is_err=False), 16)
                    eng.wait_ge(S["ge_v"], i * v_n + (v_base + v_n))
                    eng.sem_inc(S["turn"], 1)
                    st.inc(eng.indirect_dma_start(out=gen_s,
                                                   out_offset=bass.IndirectOffsetOnAxis(ap=w_idx[:, :], axis=0),
                                                  in_=g_new[:, :], in_offset=None,
                                                  bounds_check=N - 1, oob_is_err=False), 16)
                    eng.wait_ge(S[f"ge_st{ph}"], st.now())
                    eng.sem_inc(S["turn"], 1)
                for c in (ld, rw, st):
                    c.end(NE)
                v_base += v_n * NE

        def general_scalar(eng):
            v_base = m_base = 0
            for ph in range(LAYERS + 2):
                vn = NODE_V[ph]
                mn = NODE_M[ph]
                if ph == LAYERS + 1:
                    with eng.Fori(0, NE) as i:
                        eng.wait_ge(S["ge_v"], i * 18 + (8 * NE * LAYERS + 16))
                        eng.activation(g1[:, 6:7], g1[:, 5:6], ACT.Exp).then_inc(S["ge_a"], 1)
                        eng.activation(same[:, :], tmp[:, :], ACT.Exp, bias=g1[:, 4:5], accum_out=g1[:, 7:8]
                                       ).then_inc(S["ge_a"], 1)
                        eng.wait_ge(S["ge_m"], i * 4 + (2 * NE * LAYERS + 3))
                        eng.activation(wide[:, :], bank[2][:, 0:P], ACT.Copy).then_inc(S["ge_a"], 1)

                def body(t, n):
                    def a(ins):
                        ins.then_inc(S["gn_a"], 1)

                    def v_at(n):
                        eng.wait_ge(S["gn_v"], t * vn + (v_base + n))

                    def m_at(n):
                        eng.wait_ge(S["gn_m"], t * mn + (m_base + n))
                    if ph == 0:
                        v_at(2)
                        a(eng.activation(g1[:, 0:1], g_mv[:, 1:2], ACT.Sqrt, bias=eps[:, 0:1]))
                        v_at(4)
                        a(eng.activation(g_node[:, 0:D], g_x[:, :], ACT.Relu, bias=g1[:, 2:3], scale=g1[:, 1:2]))
                    elif ph <= LAYERS:
                        m_at(1)
                        a(eng.activation(g_t[:, :], bank[0][:, 0:2 * P], ACT.Copy))
                        if ph == LAYERS:
                            v_at(9)
                            a(eng.activation(g1[:, 0:1], g_mv[:, 1:2], ACT.Sqrt, bias=eps[:, 0:1]))
                            v_at(11)
                            a(eng.activation(g_h[:, :], g_x1[:, :], ACT.Relu, bias=g1[:, 2:3], scale=g1[:, 1:2]))
                            m_at(3)
                            a(eng.activation(g_t[:, 0:P], bank[0][:, 0:P], ACT.Copy))
                    else:
                        v_at(5)
                        a(eng.activation(g1[:, 4:6], g1[:, 2:4], ACT.Exp))
                node_loop(eng, body)
                v_base += vn * NT
                m_base += mn * NT

        def general_tensor(eng):
            v_base = a_base = 0
            for ph in range(LAYERS + 2):
                vn = NODE_V[ph]
                an = NODE_A[ph]
                if 1 <= ph <= LAYERS:
                    kb = NE * (ph - 1)
                    with eng.Fori(0, NE) as i:
                        eng.wait_ge(S["ge_v"], i * 8 + (8 * kb + 2))
                        eng.transpose(bank[0][:, 0:P], wide[:, :], ident[:, :]).then_inc(S["ge_m"], 1)
                        eng.wait_ge(S["ge_v"], i * 8 + (8 * kb + 3))
                        eng.wait_ge(S[f"ge_rows{ph - 1}"], i * 32 + 32)
                        eng.matmul(bank[1][:, 0:D + 1], same[:, :], g_row[:, 0:D + 1], start=True, stop=True
                                   ).then_inc(S["ge_m"], 1)
                if ph == LAYERS + 1:
                    vb = 8 * NE * LAYERS
                    with eng.Fori(0, NE) as i:
                        eng.wait_ge(S["ge_v"], i * 18 + (vb + 2))
                        eng.transpose(bank[0][:, 0:P], wide[:, :], ident[:, :]).then_inc(S["ge_m"], 1)
                        eng.wait_ge(S["ge_v"], i * 18 + (vb + 10))
                        eng.transpose(bank[1][:, 0:P], tmp[:, :], ident[:, :]).then_inc(S["ge_m"], 1)
                        eng.wait_ge(S["ge_a"], i * 3 + 2)
                        eng.transpose(bank[2][:, 0:P], same[:, :], ident[:, :]).then_inc(S["ge_m"], 1)
                        eng.wait_ge(S["ge_a"], i * 3 + 3)
                        eng.matmul(bank[3][:, 0:D], wide[:, :], g_row[:, 0:D], start=True, stop=True
                                   ).then_inc(S["ge_m"], 1)

                def body(t, n):
                    if ph in (1, 2, 3):
                        eng.wait_ge(S["gn_v"], t * vn + (v_base + 3))
                        eng.transpose(bank[0][:, 0:P], g_h[:, :], ident[:, :])
                        eng.transpose(bank[0][:, P:2 * P], g_row[:, 0:D], ident[:, :]).then_inc(S["gn_m"], 1)
                        eng.wait_ge(S["gn_a"], t * an + (a_base + 1))
                        eng.matmul(bank[1][:, 0:D], g_t[:, 0:P], wcat[:, ph - 1, 0:D], start=True, stop=False)
                        eng.matmul(bank[1][:, 0:D], g_t[:, P:2 * P], wcat[:, ph - 1, D:2 * D], start=False, stop=True
                                   ).then_inc(S["gn_m"], 1)
                    if ph == 3:
                        eng.wait_ge(S["gn_a"], t * an + (a_base + 3))
                        eng.transpose(bank[0][:, 0:P], g_h[:, :], ident[:, :]).then_inc(S["gn_m"], 1)
                        eng.wait_ge(S["gn_a"], t * an + (a_base + 4))
                        eng.matmul(bank[2][:, 0:D + 2], g_t[:, 0:P], wg[:, :], start=True, stop=True
                                   ).then_inc(S["gn_m"], 1)
                if ph in (1, 2, 3):
                    node_loop(eng, body)
                v_base += vn * NT
                a_base += an * NT

        def general_vector(eng):
            ev, nv = Count(S["ge_v"]), Count(S["gn_v"])
            m_base = a_base = 0
            eng.wait_ge(S["low_g"], 11)

            def edge_ids(o, i, kb):
                eng.wait_ge(S[f"ge_ld{kb // NE}"], i * 32 + 32)
                o(eng.tensor_copy(df[:, :], se[:, 1:2]))
                o(eng.tensor_scalar(wide[:, :], ones[:, :], df[:, 0:1], None, ALU.mult))

            def first_of(o):
                o(eng.tensor_tensor(tmp[:, :], same[:, :], low[:, :], ALU.mult))
                o(eng.tensor_reduce(g1[:, 0:1], tmp[:, :], AX.X, ALU.max))
                o(eng.tensor_scalar(g1[:, 1:2], g1[:, 0:1], FAR, None, ALU.mult))
                o(eng.tensor_tensor(w_idx[:, :], g1[:, 1:2], df[:, :], ALU.add))

            def sums(ph):
                kb = NE * (ph - 1)
                with eng.Fori(0, NE) as i:
                    ev.begin(8, i)

                    def o(ins):
                        ev.inc(ins)
                        eng.wait_ge(S["ge_v"], ev.now())
                    edge_ids(o, i, kb)
                    eng.wait_ge(S["ge_m"], i * 2 + (2 * kb + 1))
                    o(eng.tensor_scalar(same[:, :], bank[0][:, 0:P], df[:, 0:1], None, ALU.is_equal))
                    first_of(o)
                    eng.wait_ge(S["ge_m"], i * 2 + (2 * kb + 2))
                    eng.wait_ge(S[f"ge_rows{ph - 1}"], i * 32 + 32)
                    o(eng.tensor_tensor(g_new[:, 0:D + 1], g_sum[:, 0:D + 1], bank[1][:, 0:D + 1], ALU.add))
                ev.end(NE)

            def attention_sums():
                kb = NE * LAYERS
                with eng.Fori(0, NE) as i:
                    ev.begin(18, i)

                    def o(ins):
                        ev.inc(ins)
                        eng.wait_ge(S["ge_v"], ev.now())
                    edge_ids(o, i, kb)
                    eng.wait_ge(S["ge_m"], i * 4 + (2 * kb + 1))
                    o(eng.tensor_scalar(same[:, :], bank[0][:, 0:P], df[:, 0:1], None, ALU.is_equal))
                    first_of(o)
                    eng.wait_ge(S[f"ge_rows{LAYERS}"], i * 48 + 48)
                    o(eng.tensor_tensor(g1[:, 0:1], g_row[:, D:D + 1], g_dst[:, D + 1:D + 2], ALU.add))
                    o(eng.scalar_tensor_tensor(g1[:, 1:2], g1[:, 0:1], 0.2, g1[:, 0:1], ALU.mult, ALU.max))
                    o(eng.tensor_scalar(tmp[:, :], ones[:, :], g1[:, 1:2], None, ALU.mult))
                    eng.wait_ge(S["ge_m"], i * 4 + (2 * kb + 2))
                    o(eng.tensor_scalar(wide[:, :], same[:, :], -1.0, BIG, ALU.add, ALU.mult))
                    o(eng.tensor_tensor(tmp[:, :], bank[1][:, 0:P], wide[:, :], ALU.add))
                    o(eng.tensor_reduce(g1[:, 2:3], tmp[:, :], AX.X, ALU.max))
                    o(eng.tensor_tensor(g_new[:, D + 1:D + 2], g1[:, 2:3], g_sum[:, D + 1:D + 2], ALU.max))
                    o(eng.tensor_scalar(g1[:, 4:5], g_new[:, D + 1:D + 2], -1.0, None, ALU.mult))
                    o(eng.tensor_tensor(g1[:, 5:6], g_sum[:, D + 1:D + 2], g_new[:, D + 1:D + 2], ALU.subtract))
                    eng.wait_ge(S["ge_a"], i * 3 + 2)
                    o(eng.scalar_tensor_tensor(g_new[:, D:D + 1], g_sum[:, D:D + 1], g1[:, 6:7], g1[:, 7:8],
                                               ALU.mult, ALU.add))
                    eng.wait_ge(S["ge_m"], i * 4 + (2 * kb + 4))
                    o(eng.scalar_tensor_tensor(g_new[:, 0:D], g_sum[:, 0:D], g1[:, 6:7], bank[3][:, 0:D],
                                               ALU.mult, ALU.add))
                ev.end(NE)

            for ph in range(LAYERS + 2):
                if 1 <= ph <= LAYERS:
                    sums(ph)
                if ph == LAYERS + 1:
                    attention_sums()
                vn = NODE_V[ph]
                mn = NODE_M[ph]
                an = NODE_A[ph]
                ln = 16 * {0: 1, 3: 3, 4: 3}.get(ph, 2)

                def body(t, n):
                    nv.begin(vn, t)

                    def o(ins):
                        nv.inc(ins)
                        eng.wait_ge(S["gn_v"], nv.now())

                    def stats_of(tile):
                        o(eng.bn_stats(g_st[:, :], tile))
                        if n == P:
                            eng.sem_inc(S["turn_v"], 1)
                        o(eng.bn_aggr(g_mv[:, :], g_st[:, :]))

                    def scale_of(a_at):
                        eng.wait_ge(S["gn_a"], t * an + (a_base + a_at))
                        o(eng.reciprocal(g1[:, 1:2], g1[:, 0:1]))
                        o(eng.scalar_tensor_tensor(g1[:, 2:3], g_mv[:, 0:1], -1.0, g1[:, 1:2], ALU.mult, ALU.mult))
                    eng.wait_ge(S[f"gn_ld{ph}"], t * ln + ln)
                    if ph == 0:
                        stats_of(g_x[:, :])
                        scale_of(1)
                    elif ph <= LAYERS:
                        o(eng.tensor_scalar(g1[:, 0:1], g_sum[:, D:D + 1], 1.0, None, ALU.max))
                        o(eng.reciprocal(g1[:, 1:2], g1[:, 0:1]))
                        o(eng.tensor_scalar(g_h[:, :], g_sum[:, 0:D], g1[:, 1:2], None, ALU.mult))
                        eng.wait_ge(S["gn_m"], t * mn + (m_base + 2))
                        o(eng.tensor_tensor(tmp[:, :], bank[1][:, 0:D], b_bc[:, ph - 1, :], ALU.add))
                        to = g_node[:, 0:D] if ph < LAYERS else wide[:, :]
                        o(eng.scalar_tensor_tensor(to, tmp[:, :], 0.01, tmp[:, :], ALU.mult, ALU.max))
                        if ph == LAYERS:
                            o(eng.tensor_tensor(g_x1[:, :], wide[:, :], g_x[:, :], ALU.add))
                            o(eng.tensor_tensor(g_x1b[:, :], g_x1[:, :], b_bc[:, LAYERS, :], ALU.add))
                            stats_of(g_x1[:, :])
                            scale_of(2)
                            eng.wait_ge(S["gn_m"], t * mn + (m_base + 4))
                            o(eng.tensor_copy(g_node[:, 0:D + 2], bank[2][:, 0:D + 2]))
                    else:
                        o(eng.tensor_tensor(g1[:, 0:1], g_row[:, D:D + 1], g_row[:, D + 1:D + 2], ALU.add))
                        o(eng.scalar_tensor_tensor(g1[:, 1:2], g1[:, 0:1], 0.2, g1[:, 0:1], ALU.mult, ALU.max))
                        o(eng.tensor_tensor(g1[:, 0:1], g1[:, 1:2], g_sum[:, D + 1:D + 2], ALU.max))
                        o(eng.tensor_tensor(g1[:, 2:3], g_sum[:, D + 1:D + 2], g1[:, 0:1], ALU.subtract))
                        o(eng.tensor_tensor(g1[:, 3:4], g1[:, 1:2], g1[:, 0:1], ALU.subtract))
                        eng.wait_ge(S["gn_a"], t * an + (a_base + 1))
                        o(eng.tensor_scalar(g1[:, 6:7], g1[:, 5:6], 1e-16, None, ALU.add))
                        o(eng.scalar_tensor_tensor(g1[:, 7:8], g_sum[:, D:D + 1], g1[:, 4:5], g1[:, 6:7],
                                                   ALU.mult, ALU.add))
                        o(eng.reciprocal(g1[:, 0:1], g1[:, 7:8]))
                        o(eng.tensor_scalar(tmp[:, :], g_sum[:, 0:D], g1[:, 4:5], None, ALU.mult))
                        o(eng.scalar_tensor_tensor(wide[:, :], g_row[:, 0:D], g1[:, 5:6], tmp[:, :], ALU.mult, ALU.add))
                        o(eng.tensor_scalar(tmp[:, :], wide[:, :], g1[:, 0:1], None, ALU.mult))
                        o(eng.tensor_tensor(g_out[:, :], tmp[:, :], g_x1b[:, :], ALU.add))
                node_loop(eng, body)
                nv.end(NT)
                m_base += mn * NT
                a_base += an * NT

        block.sync(sync_program)
        block.gpsimd(gpsimd_program)
        block.scalar(scalar_program)
        block.tensor(tensor_program)
        block.vector(vector_program)

_INS = ['x', 'src', 'dst', 'L0_gnn_Wl1', 'L0_gnn_bl1', 'L0_gnn_Wr1', 'L0_gnn_Wlh', 'L0_gnn_blh', 'L0_gnn_Wrh',
        'L1_gnn_W', 'L1_gnn_att_src', 'L1_gnn_att_dst', 'L1_gnn_bias']


def kernel(**inputs):
    import numpy as _np
    import concourse.bacc as _bacc
    from concourse import mybir as _mybir
    from concourse.bass_utils import run_bass_kernel_spmd as _run

    nc = _bacc.Bacc("TRN2", target_bir_lowering=False, num_devices=1)
    arrays, args = {}, []
    for name in _INS:
        a = _np.ascontiguousarray(inputs[name])
        arrays[f"in_{name}"] = a
        args.append(nc.dram_tensor(f"in_{name}", a.shape, _mybir.dt.from_np(a.dtype), kind="ExternalInput").ap())
    args.append(nc.dram_tensor("out_0", (N, D), _mybir.dt.float32, kind="ExternalOutput").ap())
    build(nc, *args)
    return _run(nc, [arrays], core_ids=[0]).results[0]["out_0"]
```
